# Optimizing a Trainium2 kernel written in Bass

```python
import numpy as np
import jax
import jax.numpy as jnp

def _softmax(x, axis=-1):
    return jax.nn.softmax(x, axis=axis)

def _gelu(x):
    return jax.nn.gelu(x, approximate=True)

def _silu(x):
    return jax.nn.silu(x)

def _sigmoid(x):
    return jax.nn.sigmoid(x)

def _layernorm(x, axis=-1, eps=1e-05):
    m = jnp.mean(x, axis=axis, keepdims=True)
    v = jnp.var(x, axis=axis, keepdims=True)
    return (x - m) / jnp.sqrt(v + eps)

def _scatter_add(tgt, idx, src, axis=0):
    return tgt.at[idx].add(src)

def _segment_sum(src, seg, n):
    return jax.ops.segment_sum(src, seg, n)
kernel_name = 'mk_conv_attn_hybrid_d4_conv_nhwc1024_r4_fd8e2f'

def setup_inputs(seed: int=0):
    np.random.seed(seed)
    _w = jnp.asarray

    def _rec_inputs():
        import jax
        import jax.numpy as jnp
        _gk = jax.random.key(seed)
        x = -0.000125 + 0.9999 * jax.random.normal(jax.random.fold_in(_gk, 1), (8, 16, 16, 256), jnp.float32)
        return x
    x = _rec_inputs()

    def _L0_conv_setup():
        import jax, jax.numpy as jnp
        import numpy as np
        HEADS = 16

        def _self_attention(x, w_qkv, w_out, heads):
            b, t, d = x.shape
            dh = d // heads
            qkv = x @ w_qkv
            q, k, v = jnp.split(qkv, 3, axis=-1)
            split = lambda z: z.reshape(b, t, heads, dh).transpose(0, 2, 1, 3)
            q, k, v = (split(q), split(k), split(v))
            dots = jnp.einsum('bhie,bhje->bhij', q, k) * d ** (-0.5)
            out = jnp.einsum('bhij,bhje->bhie', dots, v)
            out = out.transpose(0, 2, 1, 3).reshape(b, t, d)
            return out @ w_out
        key = jax.random.key(seed)
        ks = jax.random.split(key, 5)
        B, H, W, D = (8, 16, 16, 256)
        s = D ** (-0.5)
        return {'x': jax.random.normal(ks[0], (B, H, W, D), jnp.float32), 'w_qkv0': jax.random.normal(ks[1], (D, 3 * D), jnp.float32) * s, 'w_out0': jax.random.normal(ks[2], (D, D), jnp.float32) * s, 'w_qkv1': jax.random.normal(ks[3], (D, 3 * D), jnp.float32) * s, 'w_out1': jax.random.normal(ks[4], (D, D), jnp.float32) * s}
    _L0_conv_all = _L0_conv_setup()
    _L0_conv_in = {k: v for k, v in _L0_conv_all.items() if k in ('w_qkv0', 'w_out0', 'w_qkv1', 'w_out1')}
    del _L0_conv_all

    def _L1_conv_setup():
        import jax, jax.numpy as jnp
        import numpy as np
        NUM_HEADS = 16
        key = jax.random.key(seed)
        ks = jax.random.split(key, 7)
        B, H, W, C = (4, 56, 28, 256)
        hd = C // NUM_HEADS
        return {'hidden_states': jax.random.normal(ks[0], (B, H, W, C), jnp.float32), 'qkv_w': jax.random.normal(ks[1], (C, 3 * C), jnp.float32) * 0.02, 'qkv_b': jax.random.normal(ks[2], (3 * C,), jnp.float32) * 0.02, 'proj_w': jax.random.normal(ks[3], (C, C), jnp.float32) * 0.02, 'proj_b': jax.random.normal(ks[4], (C,), jnp.float32) * 0.02, 'rel_pos_h': jax.random.normal(ks[5], (2 * H - 1, hd), jnp.float32) * 0.02, 'rel_pos_w': jax.random.normal(ks[6], (2 * W - 1, hd), jnp.float32) * 0.02}
    _L1_conv_all = _L1_conv_setup()
    _L1_conv_in = {k: v for k, v in _L1_conv_all.items() if k in ('qkv_w', 'qkv_b', 'proj_w', 'proj_b', 'rel_pos_h', 'rel_pos_w')}
    del _L1_conv_all

    def _L2_attn_setup():
        import jax, jax.numpy as jnp
        import numpy as np
        LN_EPS = 1e-05
        NUM_HEAD = 16
        key = jax.random.key(seed)
        ks = jax.random.split(key, 10)
        B, S, E = (2, 512, 256)
        sc = 0.02
        return {'x': jax.random.normal(ks[0], (B, S, E), jnp.float32), 'wq': jax.random.normal(ks[1], (E, E), jnp.float32) * sc, 'bq': jax.random.normal(ks[2], (E,), jnp.float32) * sc, 'wk': jax.random.normal(ks[3], (E, E), jnp.float32) * sc, 'bk': jax.random.normal(ks[4], (E,), jnp.float32) * sc, 'wv': jax.random.normal(ks[5], (E, E), jnp.float32) * sc, 'bv': jax.random.normal(ks[6], (E,), jnp.float32) * sc, 'wo': jax.random.normal(ks[7], (E, E), jnp.float32) * sc, 'bo': jax.random.normal(ks[8], (E,), jnp.float32) * sc, 'gamma': jnp.ones((E,), jnp.float32), 'beta': jnp.zeros((E,), jnp.float32)}
    _L2_attn_all = _L2_attn_setup()
    _L2_attn_in = {k: v for k, v in _L2_attn_all.items() if k in ('wq', 'bq', 'wk', 'bk', 'wv', 'bv', 'wo', 'bo', 'gamma', 'beta')}
    del _L2_attn_all

    def _L2_ffn_setup():
        import jax, jax.numpy as jnp
        import numpy as np
        B, T, D, E, H = (4, 512, 256, 8, 256)
        key = jax.random.key(seed)
        k1, k2, k3, k4, k5 = jax.random.split(key, 5)
        s = 1.0 / np.sqrt(D)
        return {'x': jax.random.normal(k1, (B, T, D), dtype=jnp.float32), 'Wg': jax.random.normal(k2, (E, D), dtype=jnp.float32) * s, 'gate_bank': jax.random.normal(k3, (E, D, H), dtype=jnp.float32) * s, 'up_bank': jax.random.normal(k4, (E, D, H), dtype=jnp.float32) * s, 'down_bank': jax.random.normal(k5, (E, H, D), dtype=jnp.float32) * (1.0 / np.sqrt(H))}
    _L2_ffn_all = _L2_ffn_setup()
    _L2_ffn_in = {k: v for k, v in _L2_ffn_all.items() if k in ('Wg', 'gate_bank', 'up_bank', 'down_bank')}
    del _L2_ffn_all

    def _L3_attn_setup():
        import jax, jax.numpy as jnp
        import numpy as np
        N_HEAD = 16
        key = jax.random.key(seed)
        k1, k2, k3, k4, k5 = jax.random.split(key, 5)
        B, S, D = (2, 512, 256)
        return {'hidden_states': jax.random.normal(k1, (B, S, D), jnp.float32), 'w_attn': jax.random.normal(k2, (D, 3 * D), jnp.float32) * 0.02, 'b_attn': jax.random.normal(k3, (3 * D,), jnp.float32) * 0.02, 'w_proj': jax.random.normal(k4, (D, D), jnp.float32) * 0.02, 'b_proj': jax.random.normal(k5, (D,), jnp.float32) * 0.02}
    _L3_attn_all = _L3_attn_setup()
    _L3_attn_in = {k: v for k, v in _L3_attn_all.items() if k in ('w_attn', 'b_attn', 'w_proj', 'b_proj')}
    del _L3_attn_all

    def _L3_ffn_setup():
        import jax, jax.numpy as jnp
        import numpy as np
        E, K = (8, 4)
        B, S, D = (4, 256, 256)
        H = D * 2 * 4 // 3

        def _swiglu(u, w1, w2, w3):
            h = jnp.einsum('...d,hd->...h', u, w1)
            v = jnp.einsum('...d,hd->...h', u, w2)
            return jnp.einsum('...h,dh->...d', jax.nn.sigmoid(h) * h * v, w3)
        key = jax.random.key(seed)
        ks = jax.random.split(key, 9)
        std = 0.02
        return {'x': jax.random.normal(ks[0], (B, S, D), jnp.float32), 'Wg': jax.random.normal(ks[1], (E, D), jnp.float32) * std, 'routing_bias': jnp.zeros((E,), jnp.float32), 'W1': jax.random.normal(ks[2], (E, H, D), jnp.float32) * std, 'W2': jax.random.normal(ks[3], (E, H, D), jnp.float32) * std, 'W3': jax.random.normal(ks[4], (E, D, H), jnp.float32) * std, 'Ws1': jax.random.normal(ks[5], (H, D), jnp.float32) * std, 'Ws2': jax.random.normal(ks[6], (H, D), jnp.float32) * std, 'Ws3': jax.random.normal(ks[7], (D, H), jnp.float32) * std}
    _L3_ffn_all = _L3_ffn_setup()
    _L3_ffn_in = {k: v for k, v in _L3_ffn_all.items() if k in ('Wg', 'routing_bias', 'W1', 'W2', 'W3', 'Ws1', 'Ws2', 'Ws3')}
    del _L3_ffn_all
    return {'x': x, 'L0_conv_w_qkv0': _L0_conv_in['w_qkv0'], 'L0_conv_w_out0': _L0_conv_in['w_out0'], 'L0_conv_w_qkv1': _L0_conv_in['w_qkv1'], 'L0_conv_w_out1': _L0_conv_in['w_out1'], 'L1_conv_qkv_w': _L1_conv_in['qkv_w'], 'L1_conv_qkv_b': _L1_conv_in['qkv_b'], 'L1_conv_proj_w': _L1_conv_in['proj_w'], 'L1_conv_proj_b': _L1_conv_in['proj_b'], 'L1_conv_rel_pos_h': _L1_conv_in['rel_pos_h'], 'L1_conv_rel_pos_w': _L1_conv_in['rel_pos_w'], 'L2_attn_wq': _L2_attn_in['wq'], 'L2_attn_bq': _L2_attn_in['bq'], 'L2_attn_wk': _L2_attn_in['wk'], 'L2_attn_bk': _L2_attn_in['bk'], 'L2_attn_wv': _L2_attn_in['wv'], 'L2_attn_bv': _L2_attn_in['bv'], 'L2_attn_wo': _L2_attn_in['wo'], 'L2_attn_bo': _L2_attn_in['bo'], 'L2_attn_gamma': _L2_attn_in['gamma'], 'L2_attn_beta': _L2_attn_in['beta'], 'L2_ffn_Wg': _L2_ffn_in['Wg'], 'L2_ffn_gate_bank': _L2_ffn_in['gate_bank'], 'L2_ffn_up_bank': _L2_ffn_in['up_bank'], 'L2_ffn_down_bank': _L2_ffn_in['down_bank'], 'L3_attn_w_attn': _L3_attn_in['w_attn'], 'L3_attn_b_attn': _L3_attn_in['b_attn'], 'L3_attn_w_proj': _L3_attn_in['w_proj'], 'L3_attn_b_proj': _L3_attn_in['b_proj'], 'L3_ffn_Wg': _L3_ffn_in['Wg'], 'L3_ffn_routing_bias': _L3_ffn_in['routing_bias'], 'L3_ffn_W1': _L3_ffn_in['W1'], 'L3_ffn_W2': _L3_ffn_in['W2'], 'L3_ffn_W3': _L3_ffn_in['W3'], 'L3_ffn_Ws1': _L3_ffn_in['Ws1'], 'L3_ffn_Ws2': _L3_ffn_in['Ws2'], 'L3_ffn_Ws3': _L3_ffn_in['Ws3']}

def reference(x, L0_conv_w_qkv0, L0_conv_w_out0, L0_conv_w_qkv1, L0_conv_w_out1, L1_conv_qkv_w, L1_conv_qkv_b, L1_conv_proj_w, L1_conv_proj_b, L1_conv_rel_pos_h, L1_conv_rel_pos_w, L2_attn_wq, L2_attn_bq, L2_attn_wk, L2_attn_bk, L2_attn_wv, L2_attn_bv, L2_attn_wo, L2_attn_bo, L2_attn_gamma, L2_attn_beta, L2_ffn_Wg, L2_ffn_gate_bank, L2_ffn_up_bank, L2_ffn_down_bank, L3_attn_w_attn, L3_attn_b_attn, L3_attn_w_proj, L3_attn_b_proj, L3_ffn_Wg, L3_ffn_routing_bias, L3_ffn_W1, L3_ffn_W2, L3_ffn_W3, L3_ffn_Ws1, L3_ffn_Ws2, L3_ffn_Ws3):
    import jax
    import jax.numpy as jnp

    def _L0_conv_ref(x, w_qkv0, w_out0, w_qkv1, w_out1):
        import jax, jax.numpy as jnp
        import numpy as np
        HEADS = 16

        def _self_attention(x, w_qkv, w_out, heads):
            b, t, d = x.shape
            dh = d // heads
            qkv = x @ w_qkv
            q, k, v = jnp.split(qkv, 3, axis=-1)
            split = lambda z: z.reshape(b, t, heads, dh).transpose(0, 2, 1, 3)
            q, k, v = (split(q), split(k), split(v))
            dots = jnp.einsum('bhie,bhje->bhij', q, k) * d ** (-0.5)
            out = jnp.einsum('bhij,bhje->bhie', dots, v)
            out = out.transpose(0, 2, 1, 3).reshape(b, t, d)
            return out @ w_out
        b, hh, ww, d = x.shape
        xh = x.transpose(0, 2, 1, 3).reshape(b * ww, hh, d)
        oh = _self_attention(xh, w_qkv0, w_out0, HEADS)
        oh = oh.reshape(b, ww, hh, d).transpose(0, 2, 1, 3)
        xw = x.reshape(b * hh, ww, d)
        ow = _self_attention(xw, w_qkv1, w_out1, HEADS)
        ow = ow.reshape(b, hh, ww, d)
        return oh + ow

    def _L1_conv_ref(hidden_states, qkv_w, qkv_b, proj_w, proj_b, rel_pos_h, rel_pos_w):
        import jax, jax.numpy as jnp
        import numpy as np
        NUM_HEADS = 16
        B, H, W, C = hidden_states.shape
        nH = NUM_HEADS
        hd = C // nH
        scale = hd ** (-0.5)
        qkv = hidden_states @ qkv_w + qkv_b
        qkv = qkv.reshape(B, H * W, 3, nH, hd).transpose(2, 0, 3, 1, 4)
        qkv = qkv.reshape(3, B * nH, H * W, hd)
        q, k, v = (qkv[0], qkv[1], qkv[2])
        attn = jnp.einsum('bqc,bkc->bqk', q * scale, k)
        coords_h = jnp.arange(H)[:, None] - jnp.arange(H)[None, :] + (H - 1)
        coords_w = jnp.arange(W)[:, None] - jnp.arange(W)[None, :] + (W - 1)
        Rh = rel_pos_h[coords_h]
        Rw = rel_pos_w[coords_w]
        rq = q.reshape(B * nH, H, W, hd)
        rel_h = jnp.einsum('bhwc,hkc->bhwk', rq, Rh)
        rel_w = jnp.einsum('bhwc,wkc->bhwk', rq, Rw)
        attn = attn.reshape(B * nH, H, W, H, W)
        attn = attn + rel_h[:, :, :, :, None] + rel_w[:, :, :, None, :]
        attn = attn.reshape(B * nH, H * W, H * W)
        attn = jax.nn.softmax(attn, axis=-1)
        out = attn @ v
        out = out.reshape(B, nH, H, W, hd).transpose(0, 2, 3, 1, 4).reshape(B, H, W, C)
        return out @ proj_w + proj_b

    def _L2_attn_ref(x, wq, bq, wk, bk, wv, bv, wo, bo, gamma, beta):
        import jax, jax.numpy as jnp
        import numpy as np
        LN_EPS = 1e-05
        NUM_HEAD = 16
        B, S, E = x.shape
        H = NUM_HEAD
        D = E // H
        Q = x @ wq + bq
        K = x @ wk + bk
        V = x @ wv + bv
        Q = Q.reshape(B * H, S, D)
        K = K.reshape(B * H, S, D)
        V = V.reshape(B * H, S, D)
        scores = jnp.einsum('bqd,bkd->bqk', Q, K) / jnp.sqrt(jnp.float32(D))
        attn = jax.nn.softmax(scores, axis=-1)
        ctx = jnp.einsum('bqk,bkd->bqd', attn, V)
        ctx = ctx.reshape(B, S, E)
        out = ctx @ wo + bo
        out = out + x
        mu = jnp.mean(out, axis=-1, keepdims=True)
        var = jnp.var(out, axis=-1, keepdims=True)
        out = (out - mu) * jax.lax.rsqrt(var + LN_EPS) * gamma + beta
        return out

    def _L2_ffn_ref(x, Wg, gate_bank, up_bank, down_bank):
        import jax, jax.numpy as jnp
        import numpy as np
        B, T, D, E, H = (4, 512, 256, 8, 256)
        logits = jnp.einsum('btd,ed->bte', x, Wg)
        selected = jnp.argmax(logits, axis=-1)
        a = jnp.einsum('btd,edh->bteh', x, gate_bank)
        u = jnp.einsum('btd,edh->bteh', x, up_bank)
        h = jax.nn.silu(a) * u
        y_all = jnp.einsum('bteh,ehd->bted', h, down_bank)
        idx = selected[:, :, None, None]
        y = jnp.take_along_axis(y_all, idx, axis=2)[:, :, 0, :]
        return y

    def _L3_attn_ref(hidden_states, w_attn, b_attn, w_proj, b_proj):
        import jax, jax.numpy as jnp
        import numpy as np
        N_HEAD = 16
        B, S, D = hidden_states.shape
        H = N_HEAD
        Dh = D // H
        qkv = hidden_states @ w_attn + b_attn
        q, k, v = jnp.split(qkv, 3, axis=-1)

        def split_heads(x):
            return x.reshape(B, S, H, Dh).transpose(0, 2, 1, 3)
        q, k, v = (split_heads(q), split_heads(k), split_heads(v))
        scores = jnp.einsum('bhqd,bhkd->bhqk', q, k) / jnp.sqrt(jnp.float32(Dh))
        attn = jax.nn.softmax(scores, axis=-1)
        out = jnp.einsum('bhqk,bhkd->bhqd', attn, v)
        out = out.transpose(0, 2, 1, 3).reshape(B, S, D)
        return out @ w_proj + b_proj

    def _L3_ffn_ref(x, Wg, routing_bias, W1, W2, W3, Ws1, Ws2, Ws3):
        import jax, jax.numpy as jnp
        import numpy as np
        E, K = (8, 4)
        B, S, D = (4, 256, 256)
        H = D * 2 * 4 // 3

        def _swiglu(u, w1, w2, w3):
            h = jnp.einsum('...d,hd->...h', u, w1)
            v = jnp.einsum('...d,hd->...h', u, w2)
            return jnp.einsum('...h,dh->...d', jax.nn.sigmoid(h) * h * v, w3)
        gate = jnp.einsum('bsd,ed->bse', x, Wg) + routing_bias
        _, top_idx = jax.lax.top_k(gate, K)
        mask = jax.nn.one_hot(top_idx, E, dtype=gate.dtype).sum(-2)
        masked_gate = jnp.where(mask > 0, gate, -jnp.inf)
        probs = jax.nn.softmax(masked_gate, axis=-1)
        weights = probs * mask
        out = _swiglu(x, Ws1, Ws2, Ws3)
        h1 = jnp.einsum('bsd,ehd->ebsh', x, W1)
        h2 = jnp.einsum('bsd,ehd->ebsh', x, W2)
        eo = jnp.einsum('ebsh,edh->ebsd', jax.nn.sigmoid(h1) * h1 * h2, W3)
        out = out + jnp.einsum('ebsd,bse->bsd', eo, weights)
        return out

    def _gn(v, G=32, eps=1e-05):
        B_, H_, W_, C_ = v.shape
        g = v.reshape(B_, H_, W_, G, C_ // G)
        m = jnp.mean(g, axis=(1, 2, 4), keepdims=True)
        s = jnp.var(g, axis=(1, 2, 4), keepdims=True)
        return ((g - m) / jnp.sqrt(s + eps)).reshape(v.shape)

    def _ln_c(v, eps=1e-06):
        m = jnp.mean(v, axis=-1, keepdims=True)
        s = jnp.var(v, axis=-1, keepdims=True)
        return (v - m) / jnp.sqrt(s + eps)

    def _ln_t(v, eps=1e-05):
        m = jnp.mean(v, axis=-1, keepdims=True)
        s = jnp.var(v, axis=-1, keepdims=True)
        return (v - m) / jnp.sqrt(s + eps)

    def _to_tokens(v):
        B_, H_, W_, C_ = v.shape
        return v.reshape(B_, H_ * W_, C_)

    def _from_tokens(t, like):
        return t.reshape(like.shape)
    x = x + _L0_conv_ref(_gn(x), L0_conv_w_qkv0, L0_conv_w_out0, L0_conv_w_qkv1, L0_conv_w_out1)
    x = x + _L1_conv_ref(_gn(x), L1_conv_qkv_w, L1_conv_qkv_b, L1_conv_proj_w, L1_conv_proj_b, L1_conv_rel_pos_h, L1_conv_rel_pos_w)
    t = _to_tokens(x)
    t = t + _L2_attn_ref(_ln_t(t), L2_attn_wq, L2_attn_bq, L2_attn_wk, L2_attn_bk, L2_attn_wv, L2_attn_bv, L2_attn_wo, L2_attn_bo, L2_attn_gamma, L2_attn_beta)
    t = t + _L2_ffn_ref(_ln_t(t), L2_ffn_Wg, L2_ffn_gate_bank, L2_ffn_up_bank, L2_ffn_down_bank)
    t = t + _L3_attn_ref(_ln_t(t), L3_attn_w_attn, L3_attn_b_attn, L3_attn_w_proj, L3_attn_b_proj)
    t = t + _L3_ffn_ref(_ln_t(t), L3_ffn_Wg, L3_ffn_routing_bias, L3_ffn_W1, L3_ffn_W2, L3_ffn_W3, L3_ffn_Ws1, L3_ffn_Ws2, L3_ffn_Ws3)
    x = _from_tokens(t, x)
    return x

_drawn_inputs = setup_inputs


def setup_inputs(seed=0):
    import zlib

    import numpy as np

    out = dict(_drawn_inputs(seed))
    spreads = {'L2_attn_gamma': (1.0, 0.2), 'L2_attn_beta': (0.0, 0.1), 'L3_ffn_routing_bias': (0.0, 0.8)}
    factors = {'L1_conv_qkv_w': 4.413,
     'L1_conv_qkv_b': 3.53,
     'L1_conv_proj_w': 3.549,
     'L1_conv_rel_pos_h': 8.0,
     'L1_conv_rel_pos_w': 8.0,
     'L2_attn_wq': 8.0,
     'L2_attn_bq': 8.0,
     'L2_attn_wk': 8.0,
     'L2_attn_bk': 8.0,
     'L2_attn_wv': 5.721,
     'L2_attn_bv': 8.0,
     'L2_attn_wo': 6.601,
     'L2_attn_bo': 2.89,
     'L3_attn_w_attn': 8.0,
     'L3_attn_b_attn': 8.0,
     'L3_attn_w_proj': 8.0,
     'L3_attn_b_proj': 8.0,
     'L3_ffn_Wg': 8.0,
     'L3_ffn_W1': 8.0,
     'L3_ffn_W2': 8.0,
     'L3_ffn_W3': 8.0,
     'L3_ffn_Ws1': 5.937,
     'L3_ffn_Ws2': 5.856,
     'L3_ffn_Ws3': 5.848}
    for name, (base, spread) in spreads.items():
        noise = np.random.default_rng([zlib.crc32(name.encode()), seed]).standard_normal(out[name].shape)
        drawn = base * np.exp(spread * noise) if base else spread * noise
        out[name] = jnp.asarray(drawn.astype(out[name].dtype))
    for name, factor in factors.items():
        out[name] = (out[name] * factor).astype(out[name].dtype)
    return out
```

```python
from contextlib import ExitStack

import concourse.bass as bass
import numpy as np
from concourse import mybir

F32, R32, BF16 = mybir.dt.float32, mybir.dt.float32r, mybir.dt.bfloat16
ALU = mybir.AluOpType
ACT = mybir.ActivationFunctionType
AX = mybir.AxisListType

P = 128
IMAGES, SIDE, D = 8, 16, 256
SEQ = SIDE * SIDE
TOKENS = IMAGES * SEQ
TILES = TOKENS // P
KD = D // P
HEADS, DH = 16, 16
BLOCK = 512
BLOCKS = TOKENS // BLOCK
GROUP = 8
PAIRS = [(0, 0), (1, 0), (2, 0), (0, 1), (1, 1), (0, 2)]
STACK = len(PAIRS) * DH
SHIFT = 2


class Phase:

    def __init__(self, nc, name):
        self.nc, self.name, self.ctx, self.sems = nc, name, ExitStack(), []

    def sem(self, name):
        s = self.ctx.enter_context(self.nc.semaphore(f"{self.name}_{name}"))
        self.sems.append(s)
        return s

    def sbuf(self, name, shape, dt=F32):
        return self.ctx.enter_context(self.nc.sbuf_tensor(f"{self.name}_{name}", shape, dt))

    def __enter__(self):
        return self

    def __exit__(self, *e):
        if e[0] is None:
            with self.nc.Block() as block:
                @block.sync
                def _(sp):
                    for s in self.sems:
                        sp.sem_clear(s)
        self.ctx.close()


class Chain:

    def __init__(self, eng, sem):
        self.eng, self.sem, self.n = eng, sem, 0

    def __call__(self, ins):
        self.n += 1
        ins.then_inc(self.sem, 1)
        self.eng.wait_ge(self.sem, self.n)


def split_matmuls(eng, out, lhs, rhs, n_k):
    terms = [(k, a, b) for k in range(n_k) for a, b in ((0, 0), (0, 1), (1, 0))]
    for i, (k, a, b) in enumerate(terms):
        last = eng.matmul(out, lhs(a, k), rhs(b, k), start=i == 0, stop=i == len(terms) - 1)
    return last


def inverse_root(dve, link, root, ve, r, t):
    link(dve.reciprocal(r, root))
    link(dve.tensor_tensor(t, r, r, ALU.mult))
    link(dve.tensor_tensor(t, t, ve, ALU.mult))
    link(dve.tensor_scalar(t, t, -0.5, 1.5, ALU.mult, ALU.add))
    link(dve.tensor_tensor(r, r, t, ALU.mult))


def normalise(nc, G, name, norm, eps=1e-5):
    X, U, RT, ident, ps = G["X"], G["U"], G["RT"], G["ident"], G["psum"]
    gn = norm == "group"
    with Phase(nc, name) as ph:
        ST = ph.sbuf("stats", [P, TILES, 6])
        MV = ph.sbuf("mean_var", [P, TILES, 2])
        SG = ph.sbuf("group_in", [P, 2, TILES])
        ME = ph.sbuf("group_mean", [P, 2, TILES])
        VE = ph.sbuf("var_eps", [P, TILES])
        SD = ph.sbuf("std", [P, TILES])
        RS = ph.sbuf("rstd", [P, TILES])
        TM = ph.sbuf("tmp", [P, TILES])
        transposed, evacuated, stats = ph.sem("transposed"), ph.sem("evacuated"), ph.sem("stats")
        group_in, group_out, var_ready, std_ready = (ph.sem("group_in"), ph.sem("group_out"),
                                                     ph.sem("var_ready"), ph.sem("std_ready"))
        chain, normed = ph.sem("chain"), ph.sem("normed")
        src = X if gn else U
        mean = (lambda t: ME[:, 0, t:t + 1]) if gn else (lambda t: MV[:, t, 0:1])

        def pair(b):
            return ps[:, b % 4, :].rearrange("p (k t) -> p k t", k=KD)

        with nc.Block() as block:
            @block.tensor
            def _(pe):
                for b in range(IMAGES):
                    if not gn:
                        pe.wait_ge(normed, 2 * b + 2)
                    if b >= 4:
                        pe.wait_ge(evacuated, b - 3)
                    for j in range(2):
                        for k in range(KD):
                            last = pe.transpose(pair(b)[:, k, j * P:(j + 1) * P],
                                                src[:, 2 * b + j, k * P:(k + 1) * P], ident[:])
                    last.then_inc(transposed, 1)
                if gn:
                    pe.wait_ge(group_in, 1)
                    pe.matmul(ps[:, 4, 0:2 * TILES], G["group_avg"][:],
                              SG[:].rearrange("p a t -> p (a t)"), start=True, stop=True).then_inc(group_out, 1)

            @block.scalar
            def _(act):
                def evacuate():
                    for b in range(IMAGES):
                        act.wait_ge(transposed, b + 1)
                        act.activation(RT[:, :, b * SEQ:(b + 1) * SEQ], pair(b), ACT.Copy).then_inc(evacuated, 1)
                if gn:
                    evacuate()
                act.wait_ge(var_ready, 1)
                act.activation(SD[:], VE[:], ACT.Sqrt).then_inc(std_ready, 1)
                if not gn:
                    evacuate()

            @block.vector
            def _(dve):
                link = Chain(dve, chain)
                for t in range(TILES):
                    if gn:
                        b, k = t // KD, t % KD
                        dve.wait_ge(evacuated, b + 1)
                        dve.bn_stats(ST[:, t, :], RT[:, k, b * SEQ:(b + 1) * SEQ]).then_inc(stats, 1)
                    else:
                        dve.bn_stats(ST[:, t, :], X[:, t, :]).then_inc(stats, 1)
                for t in range(TILES):
                    dve.wait_ge(stats, t + 1)
                    dve.bn_aggr(MV[:, t, :], ST[:, t, :]).then_inc(stats, 1)
                dve.wait_ge(stats, 2 * TILES)
                if gn:
                    link(dve.tensor_copy(SG[:, 0, :], MV[:, :, 0]))
                    link(dve.tensor_tensor(TM[:], SG[:, 0, :], SG[:, 0, :], ALU.mult))
                    dve.tensor_tensor(SG[:, 1, :], TM[:], MV[:, :, 1], ALU.add).then_inc(group_in, 1)
                    dve.wait_ge(group_out, 1)
                    link(dve.tensor_copy(ME[:].rearrange("p a t -> p (a t)"), ps[:, 4, 0:2 * TILES]))
                    link(dve.tensor_tensor(TM[:], ME[:, 0, :], ME[:, 0, :], ALU.mult))
                    link(dve.tensor_tensor(VE[:], ME[:, 1, :], TM[:], ALU.subtract))
                    dve.tensor_scalar_add(VE[:], VE[:], eps).then_inc(var_ready, 1)
                else:
                    dve.tensor_scalar_add(VE[:], MV[:, :, 1], eps).then_inc(var_ready, 1)
                dve.wait_ge(std_ready, 1)
                inverse_root(dve, link, SD[:], VE[:], RS[:], TM[:])
                for t in range(TILES):
                    if gn:
                        b, k = t // KD, t % KD
                        dst = RT[:, k, b * SEQ:(b + 1) * SEQ]
                        dve.tensor_scalar(dst, dst, mean(t), RS[:, t:t + 1], ALU.subtract, ALU.mult)\
                           .then_inc(normed, 1)
                    else:
                        dve.tensor_scalar(U[:, t, :], X[:, t, :], mean(t), RS[:, t:t + 1],
                                          ALU.subtract, ALU.mult).then_inc(normed, 1)


def project(nc, G, name, wqkv, bias, by_columns, vt, scr_q, scr_k, scr_v=None):
    RT, QF, KF, ps = G["RT"], G["QF"], G["KF"], G["psum"]
    with Phase(nc, name) as ph:
        WR = ph.sbuf("w_raw", [P, KD, 3 * D])
        WS = ph.sbuf("w_split", [P, 2, KD, 3 * D], R32)
        XS = ph.sbuf("x_split", [P, 2, 2, KD, BLOCK], R32)
        PT = ph.sbuf("parts", [P, 4, 3, BLOCK], BF16)
        R1 = ph.sbuf("rest", [P, 4, BLOCK])
        BQK = ph.sbuf("bias_qk", [P, 4])
        BV = ph.sbuf("bias_v", [P, 2, D])
        loaded, w_hi, w_lo = ph.sem("loaded"), ph.sem("w_hi"), ph.sem("w_lo")
        x_hi, x_lo = ph.sem("x_hi"), ph.sem("x_lo")
        qk_done, f_ready, part1, rest1, part2, part3 = (
            ph.sem(s) for s in ("qk_done", "f_ready", "part1", "rest1", "part2", "part3"))
        v_done, v_ready = ph.sem("v_done"), ph.sem("v_ready")
        spilled = [ph.sem(f"spilled{u}") for u in range(4)]
        v_spilled = ph.sem("v_spilled")
        n_loads = len(wqkv) + (4 if bias else 0)

        def blocks(n):
            if not by_columns:
                return [(RT[:, :, n * BLOCK:(n + 1) * BLOCK], lambda a: XS[:, n % 2, a])]
            return [(RT[:, :, b * SEQ:(b + 1) * SEQ].rearrange("p k (y x) -> p k x y", x=SIDE),
                     lambda a, h=b % 2: XS[:, n % 2, a, :, h * SEQ:(h + 1) * SEQ].rearrange("p k (x y) -> p k x y", y=SIDE))
                    for b in (2 * n, 2 * n + 1)]

        def feat(u, n):
            return (QF, KF)[u // 2][:, u % 2, n * BLOCK:(n + 1) * BLOCK]

        with nc.Block() as block:
            @block.sync
            def _(sp):
                col = 0
                for w in wqkv:
                    n = w.shape[1]
                    sp.dma_start(WR[:, :, col:col + n], w.rearrange("(k p) n -> p k n", p=P)).then_inc(loaded, 16)
                    col += n
                if bias:
                    bq, bk, bv = bias
                    with nc.allow_non_contiguous_dma("512 biases, one to a partition"):
                        sp.dma_start(BQK[:, 0:2], bq.rearrange("(u p) -> p u", p=P)).then_inc(loaded, 16)
                        sp.dma_start(BQK[:, 2:4], bk.rearrange("(u p) -> p u", p=P)).then_inc(loaded, 16)
                    for i in range(2):
                        sp.dma_start(BV[:, i, :], bv.partition_broadcast(P)).then_inc(loaded, 16)
                for n in range(BLOCKS):
                    for u in range(4):
                        sp.wait_ge(part3, 4 * n + u + 1)
                        dst = (scr_q, scr_k)[u // 2][:, (u % 2) * P:(u % 2 + 1) * P, n * BLOCK:(n + 1) * BLOCK]
                        sp.dma_start(dst.rearrange("a p n -> p a n"), PT[:, u, :, :]).then_inc(spilled[u], 16)
                if scr_v is not None:
                    sp.wait_ge(v_ready, 2 * BLOCKS)
                    sp.dma_start(scr_v.rearrange("(t p) n -> p t n", p=P), vt[:]).then_inc(v_spilled, 16)
                    sp.wait_ge(v_spilled, 16)
                for u in range(4):
                    sp.wait_ge(spilled[u], 16 * BLOCKS)

            @block.tensor
            def _(pe):
                pe.wait_ge(w_hi, 1)
                pe.wait_ge(w_lo, 1)
                for n in range(BLOCKS):
                    s = n % 2
                    pe.wait_ge(x_hi, n + 1)
                    pe.wait_ge(x_lo, n + 1)
                    for u in range(4):
                        if n:
                            pe.wait_ge(f_ready, 4 * (n - 1) + u + 1)
                        split_matmuls(pe, ps[:, u, :], lambda a, k: WS[:, a, k, u * P:(u + 1) * P],
                                      lambda a, k: XS[:, s, a, k, :], KD).then_inc(qk_done, 1)
                    for h in range(2):
                        if n:
                            pe.wait_ge(v_ready, 2 * (n - 1) + h + 1)
                        for j in range(2):
                            t0 = (2 * h + j) * P
                            last = split_matmuls(pe, ps[:, 4 + h, j * D:(j + 1) * D],
                                                 lambda a, k: XS[:, s, a, k, t0:t0 + P],
                                                 lambda a, k: WS[:, a, k, 2 * D:3 * D], KD)
                        last.then_inc(v_done, 1)

            def v_bank(h):
                return ps[:, 4 + h, :].rearrange("p (t n) -> p t n", t=2)

            @block.scalar
            def _(act):
                if bias:
                    act.wait_ge(loaded, 16 * n_loads)
                for n in range(BLOCKS):
                    for u in range(4):
                        act.wait_ge(qk_done, 4 * n + u + 1)
                        if bias:
                            act.activation(feat(u, n), ps[:, u, :], ACT.Identity, bias=BQK[:, u:u + 1]).then_inc(f_ready, 1)
                        else:
                            act.activation(feat(u, n), ps[:, u, :], ACT.Copy).then_inc(f_ready, 1)
                    if not bias:
                        for h in range(2):
                            act.wait_ge(v_done, 2 * n + h + 1)
                            act.activation(vt[:, 4 * n + 2 * h:4 * n + 2 * h + 2, :], v_bank(h), ACT.Copy).then_inc(v_ready, 1)

            @block.vector
            def _(dve):
                def split_block(n):
                    if n >= 2:
                        dve.wait_ge(v_done, 2 * (n - 1))
                    for src, split in blocks(n):
                        last = dve.tensor_copy(split(0), src)
                    last.then_inc(x_hi, 1)
                split_block(0)
                split_block(1)
                dve.wait_ge(loaded, 16 * n_loads)
                dve.tensor_copy(WS[:, 0], WR[:]).then_inc(w_hi, 1)
                dve.wait_ge(w_hi, 1)
                dve.tensor_tensor(WS[:, 1], WR[:], WS[:, 0], ALU.subtract).then_inc(w_lo, 1)
                for n in range(BLOCKS):
                    for u in range(4):
                        dve.wait_ge(f_ready, 4 * n + u + 1)
                        if n:
                            dve.wait_ge(spilled[u], 16 * n)
                        dve.tensor_copy(PT[:, u, 0, :], feat(u, n)).then_inc(part1, 1)
                    if n + 2 < BLOCKS:
                        split_block(n + 2)
                    for u in range(4):
                        dve.wait_ge(rest1, 4 * n + u + 1)
                        dve.tensor_copy(PT[:, u, 1, :], R1[:, u, :]).then_inc(part2, 1)
                        dve.wait_ge(part2, 4 * n + u + 1)
                        dve.tensor_tensor(PT[:, u, 2, :], R1[:, u, :], PT[:, u, 1, :], ALU.subtract).then_inc(part3, 1)
                    if bias:
                        for h in range(2):
                            dve.wait_ge(v_done, 2 * n + h + 1)
                            dve.tensor_tensor(vt[:, 4 * n + 2 * h:4 * n + 2 * h + 2, :], v_bank(h), BV[:],
                                              ALU.add).then_inc(v_ready, 1)

            @block.gpsimd
            def _(pool):
                def split_block(n):
                    pool.wait_ge(x_hi, n + 1)
                    for src, split in blocks(n):
                        last = pool.tensor_tensor(split(1), src, split(0), ALU.subtract)
                    last.then_inc(x_lo, 1)
                split_block(0)
                split_block(1)
                for n in range(BLOCKS):
                    for u in range(4):
                        pool.wait_ge(part1, 4 * n + u + 1)
                        if n:
                            pool.wait_ge(part3, 4 * (n - 1) + u + 1)
                        pool.tensor_tensor(R1[:, u, :], feat(u, n), PT[:, u, 0, :], ALU.subtract).then_inc(rest1, 1)
                    if n + 2 < BLOCKS:
                        split_block(n + 2)


def attend(nc, G, name, kind, vt, scr_q, scr_k, wo, bo=None, scr_v=None, scr_r=None, by_columns=False):
    X, U, ident, ps, masks = G["X"], G["U"], G["ident"], G["psum"], G["mask"]
    softmax, rel, rows = kind != "linear", kind == "rel", kind == "rows"
    K = STACK + SHIFT if softmax else STACK
    RING = 3
    PR = 8
    UNITS = 16
    with Phase(nc, name) as ph:
        QS = ph.sbuf("q_stack", [P, RING, HEADS, SEQ], BF16)
        KS = ph.sbuf("k_stack", [P, RING, HEADS, SEQ], BF16)
        RL = ph.sbuf("rel_stack", [P, RING, HEADS, SEQ], BF16) if rel else None
        VS = ph.sbuf("v_image", [P, 2, UNITS, 32])
        QK = ph.sbuf("staged", [STACK, 2, HEADS, SEQ], BF16) if rows else None
        VG = ph.sbuf("v_rows", [P, 2, 2, UNITS, DH]) if rows else None
        PB = ph.sbuf("probs", [P, PR, 2, SEQ])
        CR = ph.sbuf("context_raw", [P, 4, SEQ])
        CN = ph.sbuf("context", [P, 2, D])
        CT = ph.sbuf("context_t", [P, 2, KD, SEQ], R32)
        IV = ph.sbuf("inv_sum", [P, 2, HEADS])
        MX = ph.sbuf("maxima", [P, 2, 2, 8])
        MR = ph.sbuf("max_rows", [8, 2, 2, SEQ], BF16)
        WR = ph.sbuf("wo_raw", [P, KD, D])
        WS = ph.sbuf("wo_split", [P, 2, KD, D], R32)
        BO = ph.sbuf("bo", [P, D])
        names = ["w_loaded", "w_hi", "w_lo", "stacked", "v_loaded", "v_copied", "s_done", "s_used", "max_turned",
                 "neg_hi", "max_ready", "max_placed", "st_done", "probs", "pv_done", "cr_ready", "c_turned",
                 "inv_ready", "cn_ready", "cn_turned", "ct_hi", "ct_lo", "out_done", "x_ready", "setup", "biased", "permuted", "sp_steps"]
        S = {n: ph.sem(n) for n in names}
        n_stack = 2 * len(PAIRS) + (6 if rel else 0)
        per_half = 16 * 2

        def st_bank(u):
            return ps[:, 2 + u % 2, :].rearrange("p (t q) -> p t q", t=2)

        def s_bank(u):
            return ps[:, u % 2, :].rearrange("p (t k) -> p t k", t=2)

        def cols(stack, r, b, u, tile, width):
            return stack[0:r, b % RING, u, tile * P:tile * P + width]

        def index(b, n, k=0):
            return b * n + k

        with nc.Block() as block:
            @block.sync
            def _(sp):
                sp.dma_start(WR[:], wo.rearrange("(k p) n -> p k n", p=P)).then_inc(S["w_loaded"], 16)
                if bo is not None:
                    sp.dma_start(BO[:], bo.partition_broadcast(P)).then_inc(S["w_loaded"], 16)

                def hold(sem, value):
                    sp.wait_ge(sem, value)
                    sp.sem_inc(S["sp_steps"], 1)

                def load_v(b):
                    for h in range(HEADS):
                        src = scr_v[bass.ds(b * SEQ, SEQ), h * DH:(h + 1) * DH].rearrange("(g s) d -> s g d", s=DH)
                        sp.dma_start(VG[(h % 8) * DH:(h % 8 + 1) * DH, b % 2, h // 8, :, :], src).then_inc(S["v_loaded"], 16)

                def stack(b, first=False):
                    if rows and not first:
                        hold(S["permuted"], b)
                    for i, (a, c) in enumerate(PAIRS):
                        for j, (scr, part) in enumerate(((scr_q, a), (scr_k, c))):
                            src = scr[part, :, bass.ds(b * SEQ, SEQ)].rearrange("(h c) t -> c h t", c=DH)
                            r = slice(i * DH, (i + 1) * DH)
                            dst = QK[r, j, :, :] if rows else (QS, KS)[j][r, b % RING, :, :]
                            sp.dma_start(dst, src).then_inc(S["stacked"], 16)
                    if rel:
                        for i in range(6):
                            src = scr_r[i, :, bass.ds(b * SEQ, SEQ)].rearrange("(h c) t -> c h t", c=DH)
                            sp.dma_start(RL[i * DH:(i + 1) * DH, b % RING, :, :], src).then_inc(S["stacked"], 16)

                def place_max(b):
                    for half in range(2):
                        hold(S["max_ready"], index(b, 2, half + 1))
                        for part in range(2):
                            row = QS[STACK + part:STACK + part + 1, b % RING, half * 8:half * 8 + 8, :]
                            sp.dma_start(row, MR[:, half, part, :]).then_inc(S["max_placed"], 16)
                        hold(S["max_placed"], index(b, 2 * per_half, (half + 1) * per_half))
                for b in range(3):
                    stack(b, first=b == 0)
                    hold(S["stacked"], 16 * n_stack * (b + 1))
                    if rows and b < 2:
                        load_v(b)
                        hold(S["v_loaded"], 256 * (b + 1))
                    if softmax and b == 0:
                        place_max(0)

                def refill(i):
                    if softmax:
                        place_max(i + 1)
                    hold(S["st_done"], index(i, UNITS, UNITS))
                    stack(i + 3)
                    hold(S["stacked"], index(i + 3, 16 * n_stack, 16 * n_stack))
                    if rows:
                        hold(S["v_copied"], i + 1)
                        load_v(i + 2)
                        hold(S["v_loaded"], index(i + 2, 256, 256))
                with sp.Fori(0, IMAGES - 3) as i:
                    refill(i)
                for i in (IMAGES - 3, IMAGES - 2):
                    if softmax:
                        place_max(i + 1)
                    if rows and i + 2 < IMAGES:
                        hold(S["v_copied"], i + 1)
                        load_v(i + 2)
                        hold(S["v_loaded"], 256 * (i + 3))

            @block.tensor
            def _(pe):
                def stack_there(b):
                    if rows:
                        pe.wait_ge(S["permuted"], b + 1)
                    else:
                        pe.wait_ge(S["stacked"], index(b, 16 * n_stack, 16 * n_stack))

                def scores_for_max(b, u):
                    pe.wait_ge(S["s_used"], index(b, UNITS, u + 1))
                    for t in range(2):
                        last = pe.matmul(s_bank(u)[:, t, :], cols(QS, STACK, b, u, t, P),
                                         cols(KS, STACK, b, u, 0, SEQ), start=True, stop=not rel)
                        if rel:
                            last = pe.matmul(s_bank(u)[:, t, :], cols(RL, STACK, b, u, t, P),
                                             G["where"][0:STACK, :], start=False, stop=True)
                    last.then_inc(S["s_done"], 1)

                def turn_max(b, half):
                    pe.wait_ge(S["s_used"], index(b, UNITS, 8 * half + 8 + 2))
                    pe.wait_ge(S["max_ready"], index(b, 2, half))
                    for t in range(2):
                        last = pe.transpose(ps[0:8, 7, half * SEQ + t * P:half * SEQ + (t + 1) * P],
                                            MX[:, half, t, :], ident[:])
                    last.then_inc(S["max_turned"], 1)

                def scores(b, u):
                    pe.wait_ge(S["probs"], index(b, UNITS, u + 1))
                    if softmax and u % 8 == 0:
                        pe.wait_ge(S["max_placed"], index(b, 2 * per_half, (u // 8 + 1) * per_half))
                    for t in range(2):
                        if softmax:
                            last = pe.matmul(st_bank(u)[:, t, :], cols(KS, K, b, u, t, P), cols(QS, K, b, u, 0, SEQ),
                                             start=True, stop=not rel)
                            if rel:
                                last = pe.matmul(st_bank(u)[:, t, :], G["where"][0:STACK, t * P:(t + 1) * P],
                                                 cols(RL, STACK, b, u, 0, SEQ), start=False, stop=True)
                        else:
                            last = pe.matmul(st_bank(u)[:, t, 0:P], cols(KS, K, b, u, t, P), cols(QS, K, b, u, t, P),
                                             start=True, stop=True)
                    last.then_inc(S["st_done"], 1)
                def values(b, quad):
                    if quad % 2 == 0:
                        pe.wait_ge(S["cr_ready"], index(b, 2, quad // 2 + 1))
                    if quad == 0:
                        pe.wait_ge(S["v_copied"], b + 1)
                    pe.wait_ge(S["probs"], index(b, UNITS, 4 * quad + 4 + 2))
                    bank = ps[:, 4, :]
                    for us in ([[4 * quad + j for j in range(4)]] if not rows else [[4 * quad + j] for j in range(4)]):
                        for t in range(2):
                            for j in range(4):
                                if rows:
                                    u = us[0]
                                    pv = PB[:, u % PR, t, :].rearrange("p (a j s) -> p j a s", j=4, s=DH)[:, j]
                                    out = bank[32 * j:32 * j + 32, (u % 8) * 64:(u % 8) * 64 + 64]
                                    last = pe.matmul(out, VS[:, t, u, :], pv, start=t == 0, stop=t == 1)
                                elif softmax:
                                    u = us[j]
                                    out = bank[32 * j:32 * j + 32, (quad % 2) * SEQ:(quad % 2 + 1) * SEQ]
                                    last = pe.matmul(out, VS[:, t, u, :], PB[:, u % PR, t, :], start=t == 0, stop=t == 1)
                                else:
                                    u = us[j]
                                    out = bank[32 * j:32 * j + 32, (quad % 2) * SEQ + t * P:(quad % 2) * SEQ + (t + 1) * P]
                                    last = pe.matmul(out, VS[:, t, u, :], PB[:, u % PR, t, 0:P], start=True, stop=True)
                    last.then_inc(S["pv_done"], 1)

                def turn_context(b):
                    pe.wait_ge(S["cr_ready"], index(b, 2, 2 + 1))
                    for t in range(2):
                        if t == 0:
                            pe.wait_ge(S["ct_lo"], index(b, 1, 1))
                        else:
                            pe.wait_ge(S["x_ready"], index(b, 1, 1))
                        for a in range(4):
                            last = pe.transpose(ps[:, 5 + t, a * P:(a + 1) * P], CR[:, a, t * P:(t + 1) * P], ident[:])
                        last.then_inc(S["c_turned"], 1)

                def turn_normed(b):
                    pe.wait_ge(S["cn_ready"], index(b, 2, 2))
                    out = ps[:, 5, :].rearrange("p (k t) -> p k t", k=KD)
                    for t in range(2):
                        for k in range(KD):
                            last = pe.transpose(out[:, k, t * P:(t + 1) * P], CN[:, t, k * P:(k + 1) * P], ident[:])
                    last.then_inc(S["cn_turned"], 1)

                def project_out(b):
                    pe.wait_ge(S["ct_hi"], b + 1)
                    pe.wait_ge(S["ct_lo"], b + 1 + 1)
                    for t in range(2):
                        last = split_matmuls(pe, ps[:, 6, t * D:(t + 1) * D],
                                             lambda a, k: CT[:, a, k, t * P:(t + 1) * P],
                                             lambda a, k: WS[:, a, k, :], KD)
                    last.then_inc(S["out_done"], 1)

                def step(i, first=False, ahead=True):
                    for quad in range(4):
                        for u in range(4 * quad, 4 * quad + 4):
                            if softmax and ahead:
                                if u == 0:
                                    stack_there(i + 1)
                                scores_for_max(i + 1, u)
                            elif u == 0:
                                stack_there(i)
                            scores(i, u)
                        if softmax and ahead and quad == 3:
                            turn_max(i + 1, 1)
                        if softmax and ahead and quad == 1:
                            turn_max(i + 1, 0)
                        if quad:
                            values(i, quad - 1)
                        elif not first:
                            values(i - 1, 3)
                        if not first and quad:
                            (turn_context, turn_normed, project_out)[quad - 1](i - 1)

                pe.wait_ge(S["setup"], 5)
                pe.wait_ge(S["w_hi"], 1)
                pe.wait_ge(S["w_lo"], 1)
                stack_there(0)
                if softmax:
                    for u in range(UNITS):
                        scores_for_max(0, u)
                        if u % 8 == 7:
                            turn_max(0, u // 8)
                step(0, first=True)
                with pe.Fori(1, IMAGES - 1) as i:
                    step(i)
                last = IMAGES - 1
                step(last, ahead=False)
                values(last, 3)
                turn_context(last)
                turn_normed(last)
                project_out(last)

            @block.scalar
            def _(act):
                act.sem_inc(S["cr_ready"], 1)

                def copy_context(b, half):
                    act.wait_ge(S["pv_done"], index(b, 4, 2 * half + 2))
                    if half == 0:
                        act.wait_ge(S["c_turned"], index(b, 2, 1))
                    bank = ps[:, 4, :]
                    if rows:
                        src = bank.rearrange("p (g a s) -> p a g s", a=4, s=DH)
                        dst = CR[:, :, half * P:(half + 1) * P].rearrange("p a (g s) -> p a g s", s=DH)
                        act.activation(dst, src, ACT.Copy).then_inc(S["cr_ready"], 1)
                    elif by_columns:
                        for a in range(2):
                            src = bank[:, a * SEQ:(a + 1) * SEQ].rearrange("p (x y) -> p x y", y=SIDE)
                            dst = CR[:, 2 * half + a, :].rearrange("p (y x) -> p x y", x=SIDE)
                            last = act.activation(dst, src, ACT.Copy)
                        last.then_inc(S["cr_ready"], 1)
                    else:
                        act.activation(CR[:, 2 * half:2 * half + 2, :], bank.rearrange("p (a q) -> p a q", a=2),
                                       ACT.Copy).then_inc(S["cr_ready"], 1)

                def split_context(b):
                    act.wait_ge(S["cn_turned"], b + 1)
                    act.wait_ge(S["out_done"], b + 1)
                    act.activation(CT[:, 0], ps[:, 5, :].rearrange("p (k t) -> p k t", k=KD), ACT.Copy).then_inc(S["ct_hi"], 1)

                def step(i, first=False):
                    for u in range(UNITS):
                        if softmax:
                            act.wait_ge(S["st_done"], index(i, UNITS, u + 1))
                            if not (first and u < PR) and u % 4 == 0:
                                act.wait_ge(S["pv_done"], index(i, 4, u // 4 - 1))
                            act.activation(PB[:, u % PR], st_bank(u), ACT.Exp, scale=0.25).then_inc(S["probs"], 1)
                        if not first and u == 5:
                            copy_context(i - 1, 1)
                        if u == 13:
                            copy_context(i, 0)
                        if not first and u == 15:
                            split_context(i - 1)

                if softmax:
                    act.sem_inc(S["probs"], 2)
                step(0, first=True)
                with act.Fori(1, IMAGES) as i:
                    step(i)
                copy_context(IMAGES - 1, 1)
                split_context(IMAGES - 1)

            @block.vector
            def _(dve):
                dve.sem_inc(S["s_used"], 2)
                dve.sem_inc(S["ct_lo"], 1)
                dve.sem_inc(S["x_ready"], 1)
                dve.sem_inc(S["c_turned"], 1)
                dve.sem_inc(S["out_done"], 1)
                if not softmax:
                    dve.sem_inc(S["probs"], 2)
                for r in range(RING):
                    dve.memset(KS[STACK:STACK + SHIFT, r], 1.0).then_inc(S["setup"], 1)
                dve.memset(VS[:, :, :, DH:32], 0.0).then_inc(S["setup"], 1)
                dve.wait_ge(S["setup"], 4)
                dve.memset(VS[:, :, :, DH:DH + 1], 1.0).then_inc(S["setup"], 1)
                dve.wait_ge(S["w_loaded"], 16 * (1 + (bo is not None)))
                dve.tensor_copy(WS[:, 0], WR[:]).then_inc(S["w_hi"], 1)
                dve.wait_ge(S["w_hi"], 1)
                dve.tensor_tensor(WS[:, 1], WR[:], WS[:, 0], ALU.subtract).then_inc(S["w_lo"], 1)

                def maxima(b, u):
                    dve.wait_ge(S["s_done"], index(b, UNITS, u + 1))
                    dve.tensor_reduce(MX[:, u // 8, :, u % 8], s_bank(u), AX.X, ALU.max).then_inc(S["s_used"], 1)

                def split_max(b, half, first=False):
                    dve.wait_ge(S["max_turned"], index(b, 2, half + 1))
                    if not first:
                        dve.wait_ge(S["max_placed"], index(b, 2 * per_half, (half - 1) * per_half))
                    bank = ps[0:8, 7, half * SEQ:(half + 1) * SEQ]
                    dve.tensor_scalar(MR[:, half, 0, :], bank, -1.0, None, ALU.mult).then_inc(S["neg_hi"], 1)
                    dve.wait_ge(S["neg_hi"], index(b, 2, half + 1))
                    dve.scalar_tensor_tensor(MR[:, half, 1, :], bank, -1.0, MR[:, half, 0, :], ALU.mult,
                                             ALU.subtract).then_inc(S["max_ready"], 1)

                def mask(b, u):
                    dve.wait_ge(S["st_done"], index(b, UNITS, u + 1))
                    dve.tensor_tensor(PB[:, u % PR, :, 0:P], st_bank(u)[:, :, 0:P], masks[:], ALU.mult).then_inc(S["probs"], 1)

                def normalise_context(b, t):
                    dve.wait_ge(S["c_turned"], index(b, 2, t + 2))
                    src = ps[:, 5 + t, :].rearrange("p (h e) -> p h e", e=32)
                    dst = CN[:, t, :].rearrange("p (h e) -> p h e", e=DH)
                    if softmax:
                        dve.reciprocal(IV[:, t, :], src[:, :, DH]).then_inc(S["inv_ready"], 1)
                        dve.wait_ge(S["inv_ready"], index(b, 2, t + 1))
                        dve.tensor_tensor(dst, src[:, :, 0:DH], IV[:, t, :].unsqueeze(2).to_broadcast([P, HEADS, DH]),
                                          ALU.mult).then_inc(S["cn_ready"], 1)
                    else:
                        dve.tensor_copy(dst, src[:, :, 0:DH]).then_inc(S["cn_ready"], 1)

                def split_context(b):
                    dve.wait_ge(S["ct_hi"], b + 1)
                    dve.tensor_tensor(CT[:, 1], ps[:, 5, :].rearrange("p (k t) -> p k t", k=KD), CT[:, 0],
                                      ALU.subtract).then_inc(S["ct_lo"], 1)

                def add_out(b):
                    dve.wait_ge(S["out_done"], b + 2)
                    dst = (U if rows else X)[:, bass.ds(2 * b, 2), :]
                    dve.tensor_tensor(dst, ps[:, 6, :].rearrange("p (t n) -> p t n", t=2), dst,
                                      ALU.add).then_inc(S["x_ready"], 1)

                def step(i, first=False, ahead=True):
                    for u in range(UNITS):
                        if softmax and ahead:
                            maxima(i + 1, u)
                            if u == 9:
                                split_max(i + 1, 0)
                        if not softmax:
                            if not (first and u < PR) and u % 4 == 0:
                                dve.wait_ge(S["pv_done"], index(i, 4, u // 4 - 1))
                            mask(i, u)
                        if not first and u == 8:
                            normalise_context(i - 1, 0)
                            normalise_context(i - 1, 1)
                    if softmax and ahead:
                        split_max(i + 1, 1)
                    if not first:
                        split_context(i - 1)
                        add_out(i - 1)

                if bo is not None:
                    dve.wait_ge(S["biased"], 1)
                if softmax:
                    for u in range(UNITS):
                        maxima(0, u)
                        if u % 8 == 7:
                            split_max(0, u // 8, first=True)
                step(0, first=True)
                with dve.Fori(1, IMAGES - 1) as i:
                    step(i)
                step(IMAGES - 1, ahead=False)
                last = IMAGES - 1
                normalise_context(last, 0)
                normalise_context(last, 1)
                split_context(last)
                add_out(last)

            @block.gpsimd
            def _(pool):
                def copy_v(b):
                    dst = VS[:, :, :, 0:DH]
                    if rows:
                        pool.wait_ge(S["v_loaded"], index(b, 256, 256))
                        for t in range(2):
                            last = pool.tensor_copy(dst[:, t], VG[:, b % 2, t])
                    else:
                        last = pool.tensor_copy(dst, vt[:, bass.ds(2 * b, 2), :].rearrange("p t (h e) -> p t h e", e=DH))
                    last.then_inc(S["v_copied"], 1)
                def permute(b):
                    pool.wait_ge(S["stacked"], index(b, 16 * n_stack, 16 * n_stack))
                    for j, dst in enumerate((QS, KS)):
                        last = pool.tensor_copy(dst[0:STACK, b % RING].rearrange("p g (h s) -> p g h s", s=DH),
                                                QK[:, j].rearrange("p h (g s) -> p g h s", s=DH))
                    last.then_inc(S["permuted"], 1)
                if bo is not None:
                    pool.wait_ge(S["w_loaded"], 32)
                    for t in range(TILES):
                        dst = (U if rows else X)[:, t, :]
                        last = pool.tensor_tensor(dst, dst, BO[:], ALU.add)
                    last.then_inc(S["biased"], 1)
                pool.wait_ge(S["setup"], 5)
                if rows:
                    permute(0)
                copy_v(0)
                if rows:
                    permute(1)
                    permute(2)
                ahead = 2 if rows else 0
                with pool.Fori(1, IMAGES - ahead) as b:
                    pool.wait_ge(S["pv_done"], b * 4)
                    copy_v(b)
                    if rows:
                        permute(b + 2)
                for b in range(IMAGES - ahead, IMAGES):
                    pool.wait_ge(S["pv_done"], b * 4)
                    copy_v(b)


def relative(nc, G, name, rel_h, rel_w, scr_r):
    QF, ps = G["QF"], G["psum"]
    with Phase(nc, name) as ph:
        T = ph.sbuf("tables", [P, 2, SIDE, P])
        F = ph.sbuf("rel", [P, 2, TOKENS])
        R1 = ph.sbuf("rest", [P, TOKENS])
        PT = ph.sbuf("parts", [P, 3, TOKENS], BF16)
        zeroed, placed, done, ready = ph.sem("zeroed"), ph.sem("placed"), ph.sem("done"), ph.sem("ready")
        part1, rest1, part2, part3, spilled = (ph.sem(s) for s in ("part1", "rest1", "part2", "part3", "spilled"))
        UNITS = [(axis, t) for axis in range(2) for t in range(KD)]

        def queries(t, axis, q):
            x = QF[:, t, :].rearrange("p (b y x) -> p b y x", y=SIDE, x=SIDE)
            return x[:, :, q, :] if axis == 0 else x[:, :, :, q]

        def into(u, axis, g):
            x = F[:, u % 2, :].rearrange("p (b y x) -> p b y x", y=SIDE, x=SIDE)
            if axis == 0:
                return x[:, :, 4 * g:4 * g + 4, :].rearrange("p b q o -> p q b o")
            return x[:, :, :, 4 * g:4 * g + 4].rearrange("p b o q -> p q b o")

        with nc.Block() as block:
            @block.sync
            def _(sp):
                sp.wait_ge(zeroed, 1)
                for axis, table in enumerate((rel_h, rel_w)):
                    for j in range(8):
                        rows = slice(j * DH, (j + 1) * DH)
                        sp.dma_start(T[rows, axis, :, rows], table).then_inc(placed, 16)
                for u, (axis, t) in enumerate(UNITS):
                    sp.wait_ge(part3, u + 1)
                    dst = scr_r[3 * axis:3 * axis + 3, t * P:(t + 1) * P, :].rearrange("a p n -> p a n")
                    sp.dma_start(dst, PT[:]).then_inc(spilled, 16)
                    sp.wait_ge(spilled, 16 * (u + 1))

            @block.tensor
            def _(pe):
                pe.wait_ge(placed, 16 * 16)
                for u, (axis, t) in enumerate(UNITS):
                    for g in range(4):
                        bank = 4 * (u % 2) + g
                        if u >= 2:
                            pe.wait_ge(ready, 4 * (u - 2) + g + 1)
                        for q in range(4 * g, 4 * g + 4):
                            out = ps[:, bank, (q % 4) * P:(q % 4 + 1) * P]
                            last = pe.matmul(out, T[:, axis, q, :], queries(t, axis, q), start=True, stop=True)
                        last.then_inc(done, 1)

            @block.scalar
            def _(act):
                for u, (axis, t) in enumerate(UNITS):
                    if u >= 2:
                        act.wait_ge(rest1, u - 1)
                    for g in range(4):
                        act.wait_ge(done, 4 * u + g + 1)
                        src = ps[:, 4 * (u % 2) + g, :].rearrange("p (q b o) -> p q b o", b=IMAGES, o=SIDE)
                        for q in range(4):
                            last = act.activation(into(u, axis, g)[:, q], src[:, q], ACT.Copy, scale=4.0)
                        last.then_inc(ready, 1)

            @block.vector
            def _(dve):
                dve.memset(T[:].rearrange("p a q m -> p (a q m)"), 0.0).then_inc(zeroed, 1)
                for u in range(len(UNITS)):
                    dve.wait_ge(ready, 4 * u + 4)
                    if u:
                        dve.wait_ge(spilled, 16 * u)
                    dve.tensor_copy(PT[:, 0, :], F[:, u % 2, :]).then_inc(part1, 1)
                    dve.wait_ge(rest1, u + 1)
                    dve.tensor_copy(PT[:, 1, :], R1[:]).then_inc(part2, 1)
                    dve.wait_ge(part2, u + 1)
                    dve.tensor_tensor(PT[:, 2, :], R1[:], PT[:, 1, :], ALU.subtract).then_inc(part3, 1)

            @block.gpsimd
            def _(pool):
                for u in range(len(UNITS)):
                    pool.wait_ge(part1, u + 1)
                    if u:
                        pool.wait_ge(part3, u)
                    pool.tensor_tensor(R1[:], F[:, u % 2, :], PT[:, 0, :], ALU.subtract).then_inc(rest1, 1)


def route(nc, G, name, wg, bias, n_exp, top, first_col, softmax):
    RT, GW, ident, ps = G["RT"], G["GW"], G["ident"], G["psum"]
    with Phase(nc, name) as ph:
        WG = ph.sbuf("wg", [P, KD, n_exp])
        BG = ph.sbuf("bias", [P, n_exp])
        LT = ph.sbuf("logits_t", [n_exp, TOKENS])
        L = ph.sbuf("logits", [P, TILES, n_exp])
        CMP = ph.sbuf("compared", [P, TILES, n_exp, n_exp])
        EQ = ph.sbuf("equal", [P, TILES, n_exp, n_exp])
        RK = ph.sbuf("rank", [P, TILES, n_exp])
        MK = ph.sbuf("mask", [P, TILES, n_exp])
        MX = ph.sbuf("max", [P, TILES])
        EX = ph.sbuf("exp", [P, TILES, n_exp])
        loaded, done, ready, turned, chain, shifted, exped = (
            ph.sem(s) for s in ("loaded", "done", "ready", "turned", "chain", "shifted", "exped"))
        full = [P, TILES, n_exp, n_exp]
        with nc.Block() as block:
            @block.sync
            def _(sp):
                sp.dma_start(WG[:], wg).then_inc(loaded, 16)
                if bias is not None:
                    sp.dma_start(BG[:], bias.partition_broadcast(P)).then_inc(loaded, 16)

            @block.tensor
            def _(pe):
                pe.wait_ge(loaded, 16 * (1 + (bias is not None)))
                for n in range(BLOCKS):
                    for k in range(KD):
                        last = pe.matmul(ps[0:n_exp, n, :], WG[:, k, :], RT[:, k, n * BLOCK:(n + 1) * BLOCK],
                                         start=k == 0, stop=k == KD - 1)
                    last.then_inc(done, 1)
                pe.wait_ge(ready, BLOCKS)
                for t in range(TILES):
                    last = pe.transpose(ps[:, 4, t * n_exp:(t + 1) * n_exp], LT[:, t * P:(t + 1) * P],
                                        ident[0:n_exp, 0:n_exp])
                last.then_inc(turned, 1)

            @block.scalar
            def _(act):
                for n in range(BLOCKS):
                    act.wait_ge(done, n + 1)
                    act.activation(LT[:, n * BLOCK:(n + 1) * BLOCK], ps[0:n_exp, n, :], ACT.Copy).then_inc(ready, 1)
                if softmax:
                    act.wait_ge(shifted, 1)
                    act.activation(EX[:], EX[:], ACT.Exp).then_inc(exped, 1)

            @block.vector
            def _(dve):
                link = Chain(dve, chain)
                dve.wait_ge(turned, 1)
                link(dve.tensor_copy(L[:], ps[:, 4, 0:TILES * n_exp].rearrange("p (t e) -> p t e", e=n_exp)))
                if bias is not None:
                    link(dve.tensor_tensor(L[:], L[:], BG[:].unsqueeze(1).to_broadcast([P, TILES, n_exp]), ALU.add))
                own, other = L[:].unsqueeze(3).to_broadcast(full), L[:].unsqueeze(2).to_broadcast(full)
                dve.tensor_tensor(CMP[:], other, own, ALU.is_gt).then_inc(chain, 1)
                dve.tensor_tensor(EQ[:], other, own, ALU.is_equal).then_inc(chain, 1)
                link.n += 2
                dve.wait_ge(chain, link.n)
                before = G["before"][:, 0:n_exp, 0:n_exp].unsqueeze(1).to_broadcast(full)
                link(dve.tensor_tensor(EQ[:], EQ[:], before, ALU.mult))
                link(dve.tensor_tensor(CMP[:], CMP[:], EQ[:], ALU.add))
                link(dve.tensor_reduce(RK[:], CMP[:], AX.X, ALU.add))
                link(dve.tensor_scalar(MK[:], RK[:], float(top) - 0.5, None, ALU.is_lt))
                if first_col:
                    link(dve.memset(GW[:, :, 0:first_col], 1.0))
                dst = GW[:, :, first_col:first_col + n_exp]
                if not softmax:
                    link(dve.tensor_copy(dst, MK[:]))
                    return
                link(dve.tensor_reduce(MX[:], L[:], AX.X, ALU.max))
                dve.tensor_tensor(EX[:], L[:], MX[:].unsqueeze(2).to_broadcast([P, TILES, n_exp]),
                                  ALU.subtract).then_inc(shifted, 1)
                dve.wait_ge(exped, 1)
                link(dve.tensor_tensor(EX[:], EX[:], MK[:], ALU.mult))
                link(dve.tensor_reduce(MX[:], EX[:], AX.X, ALU.add))
                link(dve.reciprocal(MX[:], MX[:]))
                link(dve.tensor_tensor(dst, EX[:], MX[:].unsqueeze(2).to_broadcast([P, TILES, n_exp]), ALU.mult))


def experts(nc, G, name, w, n_exp, n_h):
    X, RT, GW, ps = G["X"], G["RT"], G["GW"], G["psum"]
    W1, W3 = KD * n_h * P, n_h * D
    WN = 2 * W1 + W3
    QUARTER = WN // BLOCKS
    with Phase(nc, name) as ph:
        WR = ph.sbuf("w_raw", [P, WN])
        WS = ph.sbuf("w_split", [P, 2, 2, WN], R32)
        XS = ph.sbuf("x_split", [P, 2, KD, TOKENS], R32)
        SL = ph.sbuf("silu", [P, 2, BLOCK])
        GF = ph.sbuf("hidden", [P, 2, BLOCK])
        GS = ph.sbuf("hidden_split", [P, 2, n_h, BLOCK], R32)
        names = ["loaded", "w_hi", "w_split", "x_hi", "x_lo", "up_done", "silu", "hidden", "g_hi", "g_lo", "down_done", "added", "sp_steps", "pe_steps"]
        S = {n: ph.sem(n) for n in names}
        TT = BLOCK // P

        def up(r, a, k, m, which):
            o = which * W1 + k * n_h * P + m * P
            return WS[:, r, a, o:o + P]

        def down(r, a, m):
            o = 2 * W1 + m * D
            return WS[:, r, a, o:o + D]

        def over_experts(eng, body):
            odd = n_exp % 2
            if odd:
                body(0, 0)
            with eng.Fori(0, n_exp // 2) as i:
                body(2 * i + odd, odd)
                body(2 * i + odd + 1, 1 - odd)

        with nc.Block() as block:
            @block.sync
            def _(sp):
                sp.dma_start(WR[:], w[0]).then_inc(S["loaded"], 16)
                with sp.Fori(1, n_exp) as e:
                    sp.wait_ge(S["w_split"], BLOCKS * e)
                    sp.sem_inc(S["sp_steps"], 1)
                    sp.dma_start(WR[:], w[bass.ds(e, 1)].rearrange("o p n -> (o p) n")).then_inc(S["loaded"], 16)

            @block.tensor
            def _(pe):
                def expert(e, r):
                    pe.wait_ge(S["w_split"], BLOCKS * e + BLOCKS)
                    pe.sem_inc(S["pe_steps"], 1)
                    with pe.Fori(0, BLOCKS) as n:
                        for m in range(n_h):
                            pe.wait_ge(S["hidden"], (e * BLOCKS + n) * n_h + m + 1)
                            for which in range(2):
                                last = split_matmuls(pe, ps[:, 2 * (m % 2) + which, :],
                                                     lambda a, k: up(r, a, k, m, which),
                                                     lambda a, k: XS[:, a, k, bass.ds(n * BLOCK, BLOCK)], KD)
                            last.then_inc(S["up_done"], 1)
                        for t in range(TT):
                            pe.wait_ge(S["added"], (e * BLOCKS + n) * TT + t + 1)
                            for m in range(n_h):
                                if t == 0:
                                    pe.wait_ge(S["g_lo"], (e * BLOCKS + n) * n_h + m + 1 + 2)
                                for i, (a, b) in enumerate(((0, 0), (0, 1), (1, 0))):
                                    last = pe.matmul(ps[:, 4 + t, 0:D], GS[:, a, m, t * P:(t + 1) * P], down(r, b, m),
                                                     start=m == 0 and i == 0, stop=m == n_h - 1 and i == 2)
                            last.then_inc(S["down_done"], 1)
                pe.wait_ge(S["x_lo"], 1)
                over_experts(pe, expert)

            @block.scalar
            def _(act):
                def expert(e, r):
                    with act.Fori(0, BLOCKS) as n:
                        for m in range(n_h):
                            act.wait_ge(S["up_done"], (e * BLOCKS + n) * n_h + m + 1)
                            act.wait_ge(S["hidden"], (e * BLOCKS + n) * n_h + m + 1)
                            act.activation(SL[:, m % 2], ps[:, 2 * (m % 2), :], ACT.Silu).then_inc(S["silu"], 1)
                over_experts(act, expert)

            @block.vector
            def _(dve):
                dve.sem_inc(S["hidden"], 2)
                dve.sem_inc(S["added"], TT)
                dve.sem_inc(S["g_lo"], 2)
                dve.tensor_copy(XS[:, 0], RT[:]).then_inc(S["x_hi"], 1)

                def expert(e, r):
                    with dve.Fori(0, BLOCKS) as n:
                        for m in range(n_h):
                            c = (e * BLOCKS + n) * n_h + m
                            dve.wait_ge(S["silu"], c + 1)
                            dve.wait_ge(S["g_lo"], c + 1)
                            dve.tensor_tensor(GF[:, m % 2], ps[:, 2 * (m % 2) + 1, :], SL[:, m % 2],
                                              ALU.mult).then_inc(S["hidden"], 1)
                            dve.wait_ge(S["hidden"], c + 3)
                            dve.tensor_copy(GS[:, 0, m], GF[:, m % 2]).then_inc(S["g_hi"], 1)
                        for t in range(TT):
                            c = (e * BLOCKS + n) * TT + t
                            dve.wait_ge(S["down_done"], c + 1)
                            x = X[:, bass.ds(n * TT + t, 1), :].rearrange("p o n -> p (o n)")
                            gate = GW[:, bass.ds(n * TT + t, 1), bass.ds(e, 1)].rearrange("p o n -> p (o n)")
                            dve.scalar_tensor_tensor(x, ps[:, 4 + t, 0:D], gate, x, ALU.mult, ALU.add).then_inc(S["added"], 1)
                over_experts(dve, expert)

            @block.gpsimd
            def _(pool):
                def split(e, r, n):
                    q = bass.ds(n * QUARTER, QUARTER)
                    pool.tensor_copy(WS[:, r, 0, q], WR[:, q]).then_inc(S["w_hi"], 1)
                    pool.wait_ge(S["w_hi"], e * BLOCKS + n + 1)
                    pool.tensor_tensor(WS[:, r, 1, q], WR[:, q], WS[:, r, 0, q], ALU.subtract).then_inc(S["w_split"], 1)

                pool.wait_ge(S["loaded"], 16)
                for n in range(BLOCKS):
                    split(0, 0, n)
                pool.wait_ge(S["x_hi"], 1)
                pool.tensor_tensor(XS[:, 1], RT[:], XS[:, 0], ALU.subtract).then_inc(S["x_lo"], 1)

                def expert(e, r, more=True):
                    with pool.Fori(0, BLOCKS) as n:
                        for m in range(n_h):
                            c = (e * BLOCKS + n) * n_h + m
                            pool.wait_ge(S["g_hi"], c + 1)
                            pool.tensor_tensor(GS[:, 1, m], GF[:, m % 2], GS[:, 0, m], ALU.subtract).then_inc(S["g_lo"], 1)
                        if more:
                            pool.wait_ge(S["loaded"], e * 16 + 32)
                            split(e + 1, 1 - r, n)
                odd = n_exp % 2
                if odd:
                    expert(0, 0)
                with pool.Fori(0, n_exp // 2 - 1) as i:
                    expert(2 * i + odd, odd)
                    expert(2 * i + odd + 1, 1 - odd)
                expert(n_exp - 2, odd)
                expert(n_exp - 1, 1 - odd, more=False)


def program(nc, A, out, stop=None):
    scr = {n: nc.dram_tensor(f"scr_{n}", [3, D, TOKENS], BF16, kind="Internal").ap() for n in ("q0", "k0", "q1", "k1")}
    scr["r"] = nc.dram_tensor("scr_r", [6, D, TOKENS], BF16, kind="Internal").ap()
    scr["v"] = nc.dram_tensor("scr_v", [TOKENS, D], F32, kind="Internal").ap()
    with ExitStack() as ctx:
        def sb(name, shape, dt=F32):
            return ctx.enter_context(nc.sbuf_tensor(name, shape, dt))
        G = {"X": sb("x_tokens", [P, TILES, D]), "U": sb("u_tokens", [P, TILES, D]), "ident": sb("ident", [P, P]),
             "group_avg": sb("group_avg", [P, P]), "mask": sb("mask", [P, 2, P]),
             "where": sb("where", [STACK, SEQ], BF16), "before": sb("before", [P, 8, 8])}
        G["psum"] = ctx.enter_context(nc.psum_tensor("psum", [P, 8, 512], F32))
        X = G["X"]

        with Phase(nc, "load") as ph:
            where32 = ph.sbuf("where32", [STACK, SEQ])
            loaded, cast = ph.sem("loaded"), ph.sem("cast")
            with nc.Block() as block:
                @block.sync
                def _(sp):
                    sp.dma_start(X[:], A["x"].rearrange("b (t y) x c -> (y x) (b t) c", t=2)).then_inc(loaded, 16)
                    sp.dma_start(G["ident"][:], A["c_ident"]).then_inc(loaded, 16)
                    sp.dma_start(G["group_avg"][:], A["c_group"]).then_inc(loaded, 16)
                    sp.dma_start(G["mask"][:], A["c_mask"]).then_inc(loaded, 16)
                    sp.dma_start(where32[:], A["c_where"]).then_inc(loaded, 16)
                    sp.dma_start(G["before"][:], A["c_before"]).then_inc(loaded, 16)

                @block.vector
                def _(dve):
                    dve.wait_ge(loaded, 96)
                    dve.tensor_copy(G["where"][:], where32[:]).then_inc(cast, 1)

        vs = ExitStack()
        def values_tensor(name):
            vs.close()
            G["v0"] = vs.enter_context(nc.sbuf_tensor(name, [P, TILES, D], F32)) if name else None

        def attention_inputs():
            part = ExitStack()
            for n in ("RT", "QF", "KF"):
                G[n] = part.enter_context(nc.sbuf_tensor(f"{n}_{nc.next_id()}", [P, KD, TOKENS], F32))
            return part

        values_tensor("v0")
        with attention_inputs():
            normalise(nc, G, "n0", "group")
            project(nc, G, "p0", [A["L0_conv_w_qkv0"]], None, True, G["v0"], scr["q0"], scr["k0"])
            project(nc, G, "p1", [A["L0_conv_w_qkv1"]], None, False, G["U"], scr["q1"], scr["k1"])
        attend(nc, G, "a0", "linear", G["v0"], scr["q0"], scr["k0"], A["L0_conv_w_out0"], by_columns=True)
        attend(nc, G, "a1", "linear", G["U"], scr["q1"], scr["k1"], A["L0_conv_w_out1"])
        if stop == "L0":
            return store(nc, G, out)

        with attention_inputs():
            normalise(nc, G, "n2", "group")
            b = A["L1_conv_qkv_b"]
            project(nc, G, "p2", [A["L1_conv_qkv_w"]], (b[0:D], b[D:2 * D], b[2 * D:3 * D]), False, G["v0"], scr["q0"], scr["k0"])
            relative(nc, G, "r2", A["rel_h"], A["rel_w"], scr["r"])
        attend(nc, G, "a2", "rel", G["v0"], scr["q0"], scr["k0"], A["L1_conv_proj_w"], A["L1_conv_proj_b"], scr_r=scr["r"])
        if stop == "L1":
            return store(nc, G, out)

        with attention_inputs():
            normalise(nc, G, "n3", "layer")
            project(nc, G, "p3", [A["L2_attn_wq"], A["L2_attn_wk"], A["L2_attn_wv"]],
                    (A["L2_attn_bq"], A["L2_attn_bk"], A["L2_attn_bv"]), False, G["v0"], scr["q0"], scr["k0"], scr["v"])
        attend(nc, G, "a3", "rows", G["v0"], scr["q0"], scr["k0"], A["L2_attn_wo"], A["L2_attn_bo"], scr_v=scr["v"])
        affine_norm(nc, G, "f3", A["L2_attn_gamma"], A["L2_attn_beta"])
        if stop == "L2a":
            return store(nc, G, out)

        values_tensor(None)

        def feed_forward(n, wg, bias, n_exp, top, first_col, softmax, w, n_h):
            with ExitStack() as part:
                G["GW"] = part.enter_context(nc.sbuf_tensor(f"gates{n}", [P, TILES, first_col + n_exp], F32))
                G["RT"] = part.enter_context(nc.sbuf_tensor(f"x_norm{n}", [P, KD, TOKENS], F32))
                normalise(nc, G, f"n{n}", "layer")
                route(nc, G, f"g{n}", wg, bias, n_exp, top, first_col, softmax)
                experts(nc, G, f"e{n}", w, first_col + n_exp, n_h)
        feed_forward(4, A["L2_ffn_Wg"], None, 8, 1, 0, False, A["w_ffn2"], A["w_ffn2"].shape[2] // (3 * D))
        if stop == "L2f":
            return store(nc, G, out)

        values_tensor("v5")
        with attention_inputs():
            normalise(nc, G, "n5", "layer")
            b, w = A["L3_attn_b_attn"], A["L3_attn_w_attn"]
            project(nc, G, "p5", [w], (b[0:D], b[D:2 * D], b[2 * D:3 * D]), False, G["v0"], scr["q0"], scr["k0"])
        attend(nc, G, "a5", "heads", G["v0"], scr["q0"], scr["k0"], A["L3_attn_w_proj"], A["L3_attn_b_proj"])
        if stop == "L3a":
            return store(nc, G, out)

        values_tensor(None)
        feed_forward(6, A["L3_ffn_Wg"], A["L3_ffn_routing_bias"], 8, 4, 1, True, A["w_ffn3"], A["w_ffn3"].shape[2] // (3 * D))
        store(nc, G, out)


def store(nc, G, out):
    with Phase(nc, "store") as ph:
        stored = ph.sem("stored")
        with nc.Block() as block:
            @block.sync
            def _(sp):
                sp.dma_start(out.rearrange("b (t y) x c -> (y x) (b t) c", t=2), G["X"][:]).then_inc(stored, 16)
                sp.wait_ge(stored, 16)


def affine_norm(nc, G, name, gamma, beta, eps=1e-5):
    X, U = G["X"], G["U"]
    with Phase(nc, name) as ph:
        GB = ph.sbuf("gamma_beta", [P, 2, D])
        ST = ph.sbuf("stats", [P, TILES, 6])
        MV = ph.sbuf("mean_var", [P, TILES, 2])
        VE, SD, RS, TM = (ph.sbuf(n, [P, TILES]) for n in ("var_eps", "std", "rstd", "tmp"))
        loaded, chain, var_ready, std_ready, normed, scaled = (
            ph.sem(s) for s in ("loaded", "chain", "var_ready", "std_ready", "normed", "scaled"))
        with nc.Block() as block:
            @block.sync
            def _(sp):
                for i, v in enumerate((gamma, beta)):
                    sp.dma_start(GB[:, i, :], v.partition_broadcast(P)).then_inc(loaded, 16)

            @block.scalar
            def _(act):
                act.wait_ge(var_ready, 1)
                act.activation(SD[:], VE[:], ACT.Sqrt).then_inc(std_ready, 1)

            @block.vector
            def _(dve):
                link = Chain(dve, chain)
                for t in range(TILES):
                    link(dve.bn_stats(ST[:, t, :], U[:, t, :]))
                for t in range(TILES):
                    link(dve.bn_aggr(MV[:, t, :], ST[:, t, :]))
                dve.tensor_scalar_add(VE[:], MV[:, :, 1], eps).then_inc(var_ready, 1)
                dve.wait_ge(std_ready, 1)
                inverse_root(dve, link, SD[:], VE[:], RS[:], TM[:])
                dve.wait_ge(loaded, 32)
                for t in range(TILES):
                    link(dve.tensor_scalar(U[:, t, :], U[:, t, :], MV[:, t, 0:1], RS[:, t:t + 1], ALU.subtract, ALU.mult))
                    dve.tensor_tensor(U[:, t, :], U[:, t, :], GB[:, 0, :], ALU.mult).then_inc(normed, 1)
                for t in range(TILES):
                    dve.wait_ge(scaled, t + 1)
                    dve.tensor_tensor(X[:, t, :], X[:, t, :], U[:, t, :], ALU.add).then_inc(chain, 1)

            @block.gpsimd
            def _(pool):
                pool.wait_ge(loaded, 32)
                for t in range(TILES):
                    pool.wait_ge(normed, t + 1)
                    pool.tensor_tensor(U[:, t, :], U[:, t, :], GB[:, 1, :], ALU.add).then_inc(scaled, 1)


def layouts(inputs):
    a = {k: np.asarray(v) for k, v in inputs.items()}
    dist = np.arange(SIDE)[:, None] - np.arange(SIDE)[None, :] + SIDE - 1
    out = {k: v for k, v in a.items() if not k.startswith(("L1_conv_rel", "L2_ffn", "L3_ffn"))}
    out["rel_h"] = a["L1_conv_rel_pos_h"].T[:, dist]
    out["rel_w"] = a["L1_conv_rel_pos_w"].T[:, dist]
    i = np.arange(P)
    out["c_ident"] = np.eye(P, dtype=np.float32)
    out["c_group"] = (i[:, None] // GROUP == i[None, :] // GROUP).astype(np.float32) / GROUP
    same = (i[:, None] // SIDE == i[None, :] // SIDE).astype(np.float32) / SIDE
    out["c_mask"] = np.stack([same, same], axis=1)
    key = np.arange(SEQ)
    where = [(np.arange(SIDE)[:, None] == k[None, :]).astype(np.float32) for k in (key // SIDE, key % SIDE)]
    out["c_where"] = np.concatenate([where[0]] * 3 + [where[1]] * 3)
    e = np.arange(8)
    out["c_before"] = np.broadcast_to((e[None, :] < e[:, None]).astype(np.float32), (P, 8, 8))
    for n in ("L2_ffn_Wg", "L3_ffn_Wg"):
        out[n] = a[n].T.reshape(KD, P, -1).transpose(1, 0, 2)
    out["L3_ffn_routing_bias"] = a["L3_ffn_routing_bias"]
    out["w_ffn2"] = expert_layout(a["L2_ffn_gate_bank"], a["L2_ffn_up_bank"], a["L2_ffn_down_bank"])
    w1, w2, w3 = (np.concatenate([a[f"L3_ffn_Ws{i}"][None], a[f"L3_ffn_W{i}"]]) for i in (1, 2, 3))
    out["w_ffn3"] = expert_layout(w1.transpose(0, 2, 1), w2.transpose(0, 2, 1), w3.transpose(0, 2, 1))
    return {k: np.ascontiguousarray(v) for k, v in out.items()}


def expert_layout(w1, w2, w3):
    n, _, h = w1.shape
    pad = -h % P
    ups = [np.pad(w, ((0, 0), (0, 0), (0, pad))).reshape(n, KD, P, h + pad).transpose(0, 2, 1, 3).reshape(n, P, -1)
           for w in (w1, w2)]
    down = np.pad(w3, ((0, 0), (0, pad), (0, 0))).reshape(n, (h + pad) // P, P, D).transpose(0, 2, 1, 3).reshape(n, P, -1)
    return np.concatenate(ups + [down], axis=2)


def kernel(**inputs):
    import concourse.bacc as bacc
    from concourse.bass_utils import run_bass_kernel_spmd
    nc = bacc.Bacc("TRN2", target_bir_lowering=False, num_devices=1)
    arrays = {f"in_{k}": v for k, v in layouts(inputs).items()}
    aps = {k[3:]: nc.dram_tensor(k, v.shape, mybir.dt.from_np(v.dtype), kind="ExternalInput").ap()
           for k, v in arrays.items()}
    out = nc.dram_tensor("out", [IMAGES, SIDE, SIDE, D], F32, kind="ExternalOutput").ap()
    program(nc, aps, out)
    return run_bass_kernel_spmd(nc, [arrays], core_ids=[0]).results[0]["out"]
```

```python
from contextlib import ExitStack

import concourse.bass as bass
import numpy as np
from concourse import mybir

F32, R32, BF16 = mybir.dt.float32, mybir.dt.float32r, mybir.dt.bfloat16
ALU = mybir.AluOpType
ACT = mybir.ActivationFunctionType
AX = mybir.AxisListType

P = 128
IMAGES, SIDE, D = 8, 16, 256
SEQ = SIDE * SIDE
TOKENS = IMAGES * SEQ
TILES = TOKENS // P
KD = D // P
HEADS, DH = 16, 16
BLOCK = 512
BLOCKS = TOKENS // BLOCK
GROUP = 8
PAIRS = [(0, 0), (1, 0), (2, 0), (0, 1), (1, 1), (0, 2)]
STACK = len(PAIRS) * DH
SHIFT = 2


class Phase:

    def __init__(self, nc, name):
        self.nc, self.name, self.ctx, self.sems = nc, name, ExitStack(), []

    def sem(self, name):
        s = self.ctx.enter_context(self.nc.semaphore(f"{self.name}_{name}"))
        self.sems.append(s)
        return s

    def sbuf(self, name, shape, dt=F32):
        return self.ctx.enter_context(self.nc.sbuf_tensor(f"{self.name}_{name}", shape, dt))

    def __enter__(self):
        return self

    def __exit__(self, *e):
        if e[0] is None:
            with self.nc.Block() as block:
                @block.sync
                def _(sp):
                    for s in self.sems:
                        sp.sem_clear(s)
        self.ctx.close()


class Chain:

    def __init__(self, eng, sem):
        self.eng, self.sem, self.n = eng, sem, 0

    def __call__(self, ins):
        self.n += 1
        ins.then_inc(self.sem, 1)
        self.eng.wait_ge(self.sem, self.n)


def split_matmuls(eng, out, lhs, rhs, n_k):
    terms = [(k, a, b) for k in range(n_k) for a, b in ((0, 0), (0, 1), (1, 0))]
    for i, (k, a, b) in enumerate(terms):
        last = eng.matmul(out, lhs(a, k), rhs(b, k), start=i == 0, stop=i == len(terms) - 1)
    return last


def inverse_root(dve, link, root, ve, r, t):
    link(dve.reciprocal(r, root))
    link(dve.tensor_tensor(t, r, r, ALU.mult))
    link(dve.tensor_tensor(t, t, ve, ALU.mult))
    link(dve.tensor_scalar(t, t, -0.5, 1.5, ALU.mult, ALU.add))
    link(dve.tensor_tensor(r, r, t, ALU.mult))


def normalise(nc, G, name, norm, eps=1e-5):
    X, U, RT, ident, ps = G["X"], G["U"], G["RT"], G["ident"], G["psum"]
    gn = norm == "group"
    with Phase(nc, name) as ph:
        ST = ph.sbuf("stats", [P, TILES, 6])
        MV = ph.sbuf("mean_var", [P, TILES, 2])
        SG = ph.sbuf("group_in", [P, 2, TILES])
        ME = ph.sbuf("group_mean", [P, 2, TILES])
        VE = ph.sbuf("var_eps", [P, TILES])
        SD = ph.sbuf("std", [P, TILES])
        RS = ph.sbuf("rstd", [P, TILES])
        TM = ph.sbuf("tmp", [P, TILES])
        transposed, evacuated, stats = ph.sem("transposed"), ph.sem("evacuated"), ph.sem("stats")
        group_in, group_out, var_ready, std_ready = (ph.sem("group_in"), ph.sem("group_out"),
                                                     ph.sem("var_ready"), ph.sem("std_ready"))
        chain, normed = ph.sem("chain"), ph.sem("normed")
        src = X if gn else U
        mean = (lambda t: ME[:, 0, t:t + 1]) if gn else (lambda t: MV[:, t, 0:1])

        def pair(b):
            return ps[:, b % 4, :].rearrange("p (k t) -> p k t", k=KD)

        with nc.Block() as block:
            @block.tensor
            def _(pe):
                for b in range(IMAGES):
                    if not gn:
                        pe.wait_ge(normed, 2 * b + 2)
                    if b >= 4:
                        pe.wait_ge(evacuated, b - 3)
                    for j in range(2):
                        for k in range(KD):
                            last = pe.transpose(pair(b)[:, k, j * P:(j + 1) * P],
                                                src[:, 2 * b + j, k * P:(k + 1) * P], ident[:])
                    last.then_inc(transposed, 1)
                if gn:
                    pe.wait_ge(group_in, 1)
                    pe.matmul(ps[:, 4, 0:2 * TILES], G["group_avg"][:],
                              SG[:].rearrange("p a t -> p (a t)"), start=True, stop=True).then_inc(group_out, 1)

            @block.scalar
            def _(act):
                def evacuate():
                    for b in range(IMAGES):
                        act.wait_ge(transposed, b + 1)
                        act.activation(RT[:, :, b * SEQ:(b + 1) * SEQ], pair(b), ACT.Copy).then_inc(evacuated, 1)
                if gn:
                    evacuate()
                act.wait_ge(var_ready, 1)
                act.activation(SD[:], VE[:], ACT.Sqrt).then_inc(std_ready, 1)
                if not gn:
                    evacuate()

            @block.vector
            def _(dve):
                link = Chain(dve, chain)
                for t in range(TILES):
                    if gn:
                        b, k = t // KD, t % KD
                        dve.wait_ge(evacuated, b + 1)
                        dve.bn_stats(ST[:, t, :], RT[:, k, b * SEQ:(b + 1) * SEQ]).then_inc(stats, 1)
                    else:
                        dve.bn_stats(ST[:, t, :], X[:, t, :]).then_inc(stats, 1)
                for t in range(TILES):
                    dve.wait_ge(stats, t + 1)
                    dve.bn_aggr(MV[:, t, :], ST[:, t, :]).then_inc(stats, 1)
                dve.wait_ge(stats, 2 * TILES)
                if gn:
                    link(dve.tensor_copy(SG[:, 0, :], MV[:, :, 0]))
                    link(dve.tensor_tensor(TM[:], SG[:, 0, :], SG[:, 0, :], ALU.mult))
                    dve.tensor_tensor(SG[:, 1, :], TM[:], MV[:, :, 1], ALU.add).then_inc(group_in, 1)
                    dve.wait_ge(group_out, 1)
                    link(dve.tensor_copy(ME[:].rearrange("p a t -> p (a t)"), ps[:, 4, 0:2 * TILES]))
                    link(dve.tensor_tensor(TM[:], ME[:, 0, :], ME[:, 0, :], ALU.mult))
                    link(dve.tensor_tensor(VE[:], ME[:, 1, :], TM[:], ALU.subtract))
                    dve.tensor_scalar_add(VE[:], VE[:], eps).then_inc(var_ready, 1)
                else:
                    dve.tensor_scalar_add(VE[:], MV[:, :, 1], eps).then_inc(var_ready, 1)
                dve.wait_ge(std_ready, 1)
                inverse_root(dve, link, SD[:], VE[:], RS[:], TM[:])
                for t in range(TILES):
                    if gn:
                        b, k = t // KD, t % KD
                        dst = RT[:, k, b * SEQ:(b + 1) * SEQ]
                        dve.tensor_scalar(dst, dst, mean(t), RS[:, t:t + 1], ALU.subtract, ALU.mult)\
                           .then_inc(normed, 1)
                    else:
                        dve.tensor_scalar(U[:, t, :], X[:, t, :], mean(t), RS[:, t:t + 1],
                                          ALU.subtract, ALU.mult).then_inc(normed, 1)


def project(nc, G, name, wqkv, bias, by_columns, vt, scr_q, scr_k, scr_v=None):
    RT, QF, KF, ps = G["RT"], G["QF"], G["KF"], G["psum"]
    with Phase(nc, name) as ph:
        WR = ph.sbuf("w_raw", [P, KD, 3 * D])
        WS = ph.sbuf("w_split", [P, 2, KD, 3 * D], R32)
        XS = ph.sbuf("x_split", [P, 2, 2, KD, BLOCK], R32)
        PT = ph.sbuf("parts", [P, 4, 3, BLOCK], BF16)
        R1 = ph.sbuf("rest", [P, 4, BLOCK])
        BQK = ph.sbuf("bias_qk", [P, 4])
        BV = ph.sbuf("bias_v", [P, 2, D])
        loaded, w_hi, w_lo = ph.sem("loaded"), ph.sem("w_hi"), ph.sem("w_lo")
        x_hi, x_lo = ph.sem("x_hi"), ph.sem("x_lo")
        qk_done, f_ready, part1, rest1, part2, part3 = (
            ph.sem(s) for s in ("qk_done", "f_ready", "part1", "rest1", "part2", "part3"))
        v_done, v_ready = ph.sem("v_done"), ph.sem("v_ready")
        spilled = [ph.sem(f"spilled{u}") for u in range(4)]
        v_spilled = ph.sem("v_spilled")
        n_loads = len(wqkv) + (4 if bias else 0)

        def blocks(n):
            if not by_columns:
                return [(RT[:, :, n * BLOCK:(n + 1) * BLOCK], lambda a: XS[:, n % 2, a])]
            return [(RT[:, :, b * SEQ:(b + 1) * SEQ].rearrange("p k (y x) -> p k x y", x=SIDE),
                     lambda a, h=b % 2: XS[:, n % 2, a, :, h * SEQ:(h + 1) * SEQ].rearrange("p k (x y) -> p k x y", y=SIDE))
                    for b in (2 * n, 2 * n + 1)]

        def feat(u, n):
            return (QF, KF)[u // 2][:, u % 2, n * BLOCK:(n + 1) * BLOCK]

        with nc.Block() as block:
            @block.sync
            def _(sp):
                col = 0
                for w in wqkv:
                    n = w.shape[1]
                    sp.dma_start(WR[:, :, col:col + n], w.rearrange("(k p) n -> p k n", p=P)).then_inc(loaded, 16)
                    col += n
                if bias:
                    bq, bk, bv = bias
                    with nc.allow_non_contiguous_dma("512 biases, one to a partition"):
                        sp.dma_start(BQK[:, 0:2], bq.rearrange("(u p) -> p u", p=P)).then_inc(loaded, 16)
                        sp.dma_start(BQK[:, 2:4], bk.rearrange("(u p) -> p u", p=P)).then_inc(loaded, 16)
                    for i in range(2):
                        sp.dma_start(BV[:, i, :], bv.partition_broadcast(P)).then_inc(loaded, 16)
                for n in range(BLOCKS):
                    for u in range(4):
                        sp.wait_ge(part3, 4 * n + u + 1)
                        dst = (scr_q, scr_k)[u // 2][:, (u % 2) * P:(u % 2 + 1) * P, n * BLOCK:(n + 1) * BLOCK]
                        sp.dma_start(dst.rearrange("a p n -> p a n"), PT[:, u, :, :]).then_inc(spilled[u], 16)
                if scr_v is not None:
                    sp.wait_ge(v_ready, 2 * BLOCKS)
                    sp.dma_start(scr_v.rearrange("(t p) n -> p t n", p=P), vt[:]).then_inc(v_spilled, 16)
                    sp.wait_ge(v_spilled, 16)
                for u in range(4):
                    sp.wait_ge(spilled[u], 16 * BLOCKS)

            @block.tensor
            def _(pe):
                pe.wait_ge(w_hi, 1)
                pe.wait_ge(w_lo, 1)
                for n in range(BLOCKS):
                    s = n % 2
                    pe.wait_ge(x_hi, n + 1)
                    pe.wait_ge(x_lo, n + 1)
                    for u in range(4):
                        if n:
                            pe.wait_ge(f_ready, 4 * (n - 1) + u + 1)
                        split_matmuls(pe, ps[:, u, :], lambda a, k: WS[:, a, k, u * P:(u + 1) * P],
                                      lambda a, k: XS[:, s, a, k, :], KD).then_inc(qk_done, 1)
                    for h in range(2):
                        if n:
                            pe.wait_ge(v_ready, 2 * (n - 1) + h + 1)
                        for j in range(2):
                            t0 = (2 * h + j) * P
                            last = split_matmuls(pe, ps[:, 4 + h, j * D:(j + 1) * D],
                                                 lambda a, k: XS[:, s, a, k, t0:t0 + P],
                                                 lambda a, k: WS[:, a, k, 2 * D:3 * D], KD)
                        last.then_inc(v_done, 1)

            def v_bank(h):
                return ps[:, 4 + h, :].rearrange("p (t n) -> p t n", t=2)

            @block.scalar
            def _(act):
                if bias:
                    act.wait_ge(loaded, 16 * n_loads)
                for n in range(BLOCKS):
                    for u in range(4):
                        act.wait_ge(qk_done, 4 * n + u + 1)
                        if bias:
                            act.activation(feat(u, n), ps[:, u, :], ACT.Identity, bias=BQK[:, u:u + 1]).then_inc(f_ready, 1)
                        else:
                            act.activation(feat(u, n), ps[:, u, :], ACT.Copy).then_inc(f_ready, 1)
                    if not bias:
                        for h in range(2):
                            act.wait_ge(v_done, 2 * n + h + 1)
                            act.activation(vt[:, 4 * n + 2 * h:4 * n + 2 * h + 2, :], v_bank(h), ACT.Copy).then_inc(v_ready, 1)

            @block.vector
            def _(dve):
                def split_block(n):
                    if n >= 2:
                        dve.wait_ge(v_done, 2 * (n - 1))
                    for src, split in blocks(n):
                        last = dve.tensor_copy(split(0), src)
                    last.then_inc(x_hi, 1)
                split_block(0)
                split_block(1)
                dve.wait_ge(loaded, 16 * n_loads)
                dve.tensor_copy(WS[:, 0], WR[:]).then_inc(w_hi, 1)
                dve.wait_ge(w_hi, 1)
                dve.tensor_tensor(WS[:, 1], WR[:], WS[:, 0], ALU.subtract).then_inc(w_lo, 1)
                for n in range(BLOCKS):
                    for u in range(4):
                        dve.wait_ge(f_ready, 4 * n + u + 1)
                        if n:
                            dve.wait_ge(spilled[u], 16 * n)
                        dve.tensor_copy(PT[:, u, 0, :], feat(u, n)).then_inc(part1, 1)
                    if n + 2 < BLOCKS:
                        split_block(n + 2)
                    for u in range(4):
                        dve.wait_ge(rest1, 4 * n + u + 1)
                        dve.tensor_copy(PT[:, u, 1, :], R1[:, u, :]).then_inc(part2, 1)
                        dve.wait_ge(part2, 4 * n + u + 1)
                        dve.tensor_tensor(PT[:, u, 2, :], R1[:, u, :], PT[:, u, 1, :], ALU.subtract).then_inc(part3, 1)
                    if bias:
                        for h in range(2):
                            dve.wait_ge(v_done, 2 * n + h + 1)
                            dve.tensor_tensor(vt[:, 4 * n + 2 * h:4 * n + 2 * h + 2, :], v_bank(h), BV[:],
                                              ALU.add).then_inc(v_ready, 1)

            @block.gpsimd
            def _(pool):
                def split_block(n):
                    pool.wait_ge(x_hi, n + 1)
                    for src, split in blocks(n):
                        last = pool.tensor_tensor(split(1), src, split(0), ALU.subtract)
                    last.then_inc(x_lo, 1)
                split_block(0)
                split_block(1)
                for n in range(BLOCKS):
                    for u in range(4):
                        pool.wait_ge(part1, 4 * n + u + 1)
                        if n:
                            pool.wait_ge(part3, 4 * (n - 1) + u + 1)
                        pool.tensor_tensor(R1[:, u, :], feat(u, n), PT[:, u, 0, :], ALU.subtract).then_inc(rest1, 1)
                    if n + 2 < BLOCKS:
                        split_block(n + 2)


def attend(nc, G, name, kind, vt, scr_q, scr_k, wo, bo=None, scr_v=None, scr_r=None, by_columns=False):
    X, U, ident, ps, masks = G["X"], G["U"], G["ident"], G["psum"], G["mask"]
    softmax, rel, rows = kind != "linear", kind == "rel", kind == "rows"
    K = STACK + SHIFT if softmax else STACK
    RING = 3
    PR = 8
    UNITS = 16
    PER_BANK = 1 if softmax else 2
    ST_BANKS = 2 if softmax else 4
    TURNS = UNITS // PER_BANK
    with Phase(nc, name) as ph:
        QS = ph.sbuf("q_stack", [P, RING, HEADS, SEQ], BF16)
        KS = ph.sbuf("k_stack", [P, RING, HEADS, SEQ], BF16)
        RL = ph.sbuf("rel_stack", [P, RING, HEADS, SEQ], BF16) if rel else None
        VS = ph.sbuf("v_image", [P, 2, UNITS, 32])
        QK = ph.sbuf("staged", [STACK, 2, HEADS, SEQ], BF16) if rows else None
        VG = ph.sbuf("v_rows", [P, 2, 2, UNITS, DH]) if rows else None
        PB = ph.sbuf("probs", [P, PR, 2, SEQ])
        CR = ph.sbuf("context_raw", [P, 4, SEQ])
        CN = ph.sbuf("context", [P, 2, D])
        CT = ph.sbuf("context_t", [P, 2, KD, SEQ], R32)
        IV = ph.sbuf("inv_sum", [P, 2, HEADS])
        MX = ph.sbuf("maxima", [P, 2, 2, 8])
        MR = ph.sbuf("max_rows", [8, 2, 2, SEQ], BF16)
        WR = ph.sbuf("wo_raw", [P, KD, D])
        WS = ph.sbuf("wo_split", [P, 2, KD, D], R32)
        BO = ph.sbuf("bo", [P, D])
        names = ["w_loaded", "w_hi", "w_lo", "stacked", "v_loaded", "v_copied", "s_done", "s_used", "max_turned",
                 "neg_hi", "max_ready", "max_placed", "st_done", "probs", "pv_done", "cr_ready", "c_turned",
                 "inv_ready", "cn_ready", "cn_turned", "ct_hi", "ct_lo", "out_done", "x_ready", "setup", "biased", "permuted", "sp_steps"]
        S = {n: ph.sem(n) for n in names}
        n_stack = 2 * len(PAIRS) + (6 if rel else 0)
        per_half = 16 * 2

        def st_bank(u):
            if softmax:
                return ps[:, 2 + u % 2, :].rearrange("p (t q) -> p t q", t=2)
            return ps[:, u // 2 % 4, :].rearrange("p (u t q) -> p u t q", u=2, t=2)

        def s_bank(u):
            return ps[:, u % 2, :].rearrange("p (t k) -> p t k", t=2)

        def cols(stack, r, b, u, tile, width):
            return stack[0:r, b % RING, u, tile * P:tile * P + width]

        def index(b, n, k=0):
            return b * n + k

        with nc.Block() as block:
            @block.sync
            def _(sp):
                sp.dma_start(WR[:], wo.rearrange("(k p) n -> p k n", p=P)).then_inc(S["w_loaded"], 16)
                if bo is not None:
                    sp.dma_start(BO[:], bo.partition_broadcast(P)).then_inc(S["w_loaded"], 16)

                def hold(sem, value):
                    sp.wait_ge(sem, value)
                    sp.sem_inc(S["sp_steps"], 1)

                def load_v(b):
                    if not (isinstance(b, int) and b == 0):
                        hold(S["v_loaded"], b * 256)
                    for h in range(HEADS):
                        src = scr_v[bass.ds(b * SEQ, SEQ), h * DH:(h + 1) * DH].rearrange("(g s) d -> s g d", s=DH)
                        sp.dma_start(VG[(h % 8) * DH:(h % 8 + 1) * DH, b % 2, h // 8, :, :], src).then_inc(S["v_loaded"], 16)

                def stack(b):
                    if not (isinstance(b, int) and b == 0):
                        hold(S["stacked"], index(b, 16 * n_stack))
                        if rows:
                            hold(S["permuted"], b * 2)
                    for i, (a, c) in enumerate(PAIRS):
                        for j, (scr, part) in enumerate(((scr_q, a), (scr_k, c))):
                            src = scr[part, :, bass.ds(b * SEQ, SEQ)].rearrange("(h c) t -> c h t", c=DH)
                            r = slice(i * DH, (i + 1) * DH)
                            dst = QK[r, j, :, :] if rows else (QS, KS)[j][r, b % RING, :, :]
                            sp.dma_start(dst, src).then_inc(S["stacked"], 16)
                    if rel:
                        for i in range(6):
                            src = scr_r[i, :, bass.ds(b * SEQ, SEQ)].rearrange("(h c) t -> c h t", c=DH)
                            sp.dma_start(RL[i * DH:(i + 1) * DH, b % RING, :, :], src).then_inc(S["stacked"], 16)

                def place_max(b, half):
                    hold(S["max_ready"], index(b, 2, half + 1))
                    if not (isinstance(b, int) and b == 0 and half == 0):
                        hold(S["max_placed"], index(b, 2 * per_half, half * per_half))
                    for part in range(2):
                        row = QS[STACK + part:STACK + part + 1, b % RING, half * 8:half * 8 + 8, :]
                        sp.dma_start(row, MR[:, half, part, :]).then_inc(S["max_placed"], 16)

                def step(i, stacks=True, values=True, ahead=True):
                    if softmax:
                        place_max(i, 1)
                    if rows and values:
                        hold(S["v_copied"], index(i, 4, 4))
                        load_v(i + 2)
                    if softmax and ahead:
                        place_max(i + 1, 0)
                    if stacks:
                        if not rows:
                            hold(S["st_done"], index(i, TURNS, TURNS))
                        stack(i + 3)

                stack(0)
                if rows:
                    load_v(0)
                stack(1)
                if softmax:
                    place_max(0, 0)
                if rows:
                    load_v(1)
                stack(2)
                with sp.Fori(0, IMAGES - 3) as i:
                    step(i)
                step(IMAGES - 3, stacks=False)
                step(IMAGES - 2, stacks=False, values=False)
                step(IMAGES - 1, stacks=False, values=False, ahead=False)

            @block.tensor
            def _(pe):
                def stack_there(b):
                    if rows:
                        pe.wait_ge(S["permuted"], index(b, 2, 2))
                    else:
                        pe.wait_ge(S["stacked"], index(b, 16 * n_stack, 16 * n_stack))

                def scores_for_max(b, u):
                    pe.wait_ge(S["s_used"], index(b, UNITS, u + 1))
                    for t in range(2):
                        last = pe.matmul(s_bank(u)[:, t, :], cols(QS, STACK, b, u, t, P),
                                         cols(KS, STACK, b, u, 0, SEQ), start=True, stop=not rel)
                        if rel:
                            last = pe.matmul(s_bank(u)[:, t, :], cols(RL, STACK, b, u, t, P),
                                             G["where"][0:STACK, :], start=False, stop=True)
                    last.then_inc(S["s_done"], 1)

                def turn_max(b, half):
                    pe.wait_ge(S["s_used"], index(b, UNITS, 8 * half + 8 + 2))
                    pe.wait_ge(S["max_ready"], index(b, 2, half))
                    for t in range(2):
                        last = pe.transpose(ps[0:8, 7, half * SEQ + t * P:half * SEQ + (t + 1) * P],
                                            MX[:, half, t, :], ident[:])
                    last.then_inc(S["max_turned"], 1)

                def scores(b, u):
                    if u % PER_BANK == 0:
                        pe.wait_ge(S["probs"], index(b, TURNS, u // PER_BANK + 1))
                    if softmax and u % 8 == 0:
                        pe.wait_ge(S["max_placed"], index(b, 2 * per_half, (u // 8 + 1) * per_half))
                    for t in range(2):
                        if softmax:
                            last = pe.matmul(st_bank(u)[:, t, :], cols(KS, K, b, u, t, P), cols(QS, K, b, u, 0, SEQ),
                                             start=True, stop=not rel)
                            if rel:
                                last = pe.matmul(st_bank(u)[:, t, :], G["where"][0:STACK, t * P:(t + 1) * P],
                                                 cols(RL, STACK, b, u, 0, SEQ), start=False, stop=True)
                        else:
                            last = pe.matmul(st_bank(u)[:, u % 2, t, :], cols(KS, K, b, u, t, P), cols(QS, K, b, u, t, P),
                                             start=True, stop=True)
                    if u % PER_BANK == PER_BANK - 1:
                        last.then_inc(S["st_done"], 1)

                def values(b, quad, k):
                    if not rows and k % 2 == 0:
                        return
                    if k < 2 and (k == 0 or not rows):
                        if quad % 2 == 0:
                            pe.wait_ge(S["cr_ready"], index(b, 2, quad // 2 + 1))
                        pe.wait_ge(S["v_copied"], index(b, 4, quad + 1))
                    n = k + 1 if rows else 4
                    pe.wait_ge(S["probs"], index(b, TURNS, (4 * quad + n) // PER_BANK + ST_BANKS))
                    bank = ps[:, 4, :]
                    for t in range(2) if rows else (k // 2,):
                        for j in range(4):
                            u = 4 * quad + (k if rows else j)
                            col = slice(32 * j, 32 * j + 32)
                            if rows:
                                pv = PB[:, u % PR, t, :].rearrange("p (a j s) -> p j a s", j=4, s=DH)[:, j]
                                out = bank[col, (u % 8) * 64:(u % 8) * 64 + 64]
                                last = pe.matmul(out, VS[:, t, u, :], pv, start=t == 0, stop=t == 1)
                            elif softmax:
                                out = bank[col, (quad % 2) * SEQ:(quad % 2 + 1) * SEQ]
                                last = pe.matmul(out, VS[:, t, u, :], PB[:, u % PR, t, :], start=t == 0, stop=t == 1)
                            else:
                                out = bank[col, (quad % 2) * SEQ + t * P:(quad % 2) * SEQ + (t + 1) * P]
                                last = pe.matmul(out, VS[:, t, u, :], PB[:, u % PR, t, 0:P], start=True, stop=True)
                    if k == 3:
                        last.then_inc(S["pv_done"], 1)

                def turn_context(b, t):
                    if t == 0:
                        pe.wait_ge(S["cr_ready"], index(b, 2, 2 + 1))
                        pe.wait_ge(S["ct_lo"], index(b, 1, 1))
                    else:
                        pe.wait_ge(S["x_ready"], index(b, 1, 1))
                    for a in range(4):
                        last = pe.transpose(ps[:, 5 + t, a * P:(a + 1) * P], CR[:, a, t * P:(t + 1) * P], ident[:])
                    last.then_inc(S["c_turned"], 1)

                def turn_normed(b):
                    pe.wait_ge(S["cn_ready"], index(b, 2, 2))
                    out = ps[:, 5, :].rearrange("p (k t) -> p k t", k=KD)
                    for t in range(2):
                        for k in range(KD):
                            last = pe.transpose(out[:, k, t * P:(t + 1) * P], CN[:, t, k * P:(k + 1) * P], ident[:])
                    last.then_inc(S["cn_turned"], 1)

                def project_out(b):
                    pe.wait_ge(S["ct_hi"], b + 1)
                    pe.wait_ge(S["ct_lo"], b + 1 + 1)
                    for t in range(2):
                        last = split_matmuls(pe, ps[:, 6, t * D:(t + 1) * D],
                                             lambda a, k: CT[:, a, k, t * P:(t + 1) * P],
                                             lambda a, k: WS[:, a, k, :], KD)
                    last.then_inc(S["out_done"], 1)

                def step(i, first=False, ahead=True):
                    for u in range(UNITS):
                        if softmax and ahead:
                            if u == 0:
                                stack_there(i + 1)
                            scores_for_max(i + 1, u)
                        elif u == 0:
                            stack_there(i)
                        scores(i, u)
                        if u >= 4:
                            values(i, u // 4 - 1, u % 4)
                        elif not first:
                            values(i - 1, 3, u)
                        if softmax and u == 1:
                            turn_max(i, 1)
                        if softmax and ahead and u == 9:
                            turn_max(i + 1, 0)
                        if not first and u in (6, 7):
                            turn_context(i - 1, u - 6)
                        if not first and u == 10:
                            turn_normed(i - 1)
                        if not first and u == 14:
                            project_out(i - 1)

                pe.wait_ge(S["setup"], 5)
                pe.wait_ge(S["w_hi"], 1)
                pe.wait_ge(S["w_lo"], 1)
                stack_there(0)
                if softmax:
                    for u in range(UNITS):
                        scores_for_max(0, u)
                        if u == 9:
                            turn_max(0, 0)
                step(0, first=True)
                with pe.Fori(1, IMAGES - 1) as i:
                    step(i)
                last = IMAGES - 1
                step(last, ahead=False)
                for k in range(4):
                    values(last, 3, k)
                turn_context(last, 0)
                turn_context(last, 1)
                turn_normed(last)
                project_out(last)

            @block.scalar
            def _(act):
                act.sem_inc(S["cr_ready"], 1)

                def copy_context(b, half):
                    act.wait_ge(S["pv_done"], index(b, 4, 2 * half + 2))
                    if half == 0:
                        act.wait_ge(S["c_turned"], index(b, 2, 1))
                    bank = ps[:, 4, :]
                    if rows:
                        src = bank.rearrange("p (g a s) -> p a g s", a=4, s=DH)
                        dst = CR[:, :, half * P:(half + 1) * P].rearrange("p a (g s) -> p a g s", s=DH)
                        act.activation(dst, src, ACT.Copy).then_inc(S["cr_ready"], 1)
                    elif by_columns:
                        for a in range(2):
                            src = bank[:, a * SEQ:(a + 1) * SEQ].rearrange("p (x y) -> p x y", y=SIDE)
                            dst = CR[:, 2 * half + a, :].rearrange("p (y x) -> p x y", x=SIDE)
                            last = act.activation(dst, src, ACT.Copy)
                        last.then_inc(S["cr_ready"], 1)
                    else:
                        act.activation(CR[:, 2 * half:2 * half + 2, :], bank.rearrange("p (a q) -> p a q", a=2),
                                       ACT.Copy).then_inc(S["cr_ready"], 1)

                def split_context(b):
                    act.wait_ge(S["cn_turned"], b + 1)
                    act.wait_ge(S["out_done"], b + 1)
                    act.activation(CT[:, 0], ps[:, 5, :].rearrange("p (k t) -> p k t", k=KD), ACT.Copy).then_inc(S["ct_hi"], 1)

                def step(i, first=False):
                    for u in range(UNITS):
                        if not first and u == 4:
                            copy_context(i - 1, 1)
                        if u == 12:
                            copy_context(i, 0)
                        if not first and u == 13:
                            split_context(i - 1)
                        if softmax:
                            act.wait_ge(S["st_done"], index(i, UNITS, u + 1))
                            if not (first and u < PR) and u % 4 == 0:
                                act.wait_ge(S["pv_done"], index(i, 4, u // 4 - 1))
                            act.activation(PB[:, u % PR], st_bank(u), ACT.Exp, scale=0.25).then_inc(S["probs"], 1)

                if softmax:
                    act.sem_inc(S["probs"], ST_BANKS)
                step(0, first=True)
                with act.Fori(1, IMAGES) as i:
                    step(i)
                copy_context(IMAGES - 1, 1)
                split_context(IMAGES - 1)

            @block.vector
            def _(dve):
                dve.sem_inc(S["s_used"], 2)
                dve.sem_inc(S["ct_lo"], 1)
                dve.sem_inc(S["x_ready"], 1)
                dve.sem_inc(S["c_turned"], 1)
                dve.sem_inc(S["out_done"], 1)
                if not softmax:
                    dve.sem_inc(S["probs"], ST_BANKS)
                for r in range(RING):
                    dve.memset(KS[STACK:STACK + SHIFT, r], 1.0).then_inc(S["setup"], 1)
                dve.memset(VS[:, :, :, DH:32], 0.0).then_inc(S["setup"], 1)
                dve.wait_ge(S["setup"], 4)
                dve.memset(VS[:, :, :, DH:DH + 1], 1.0).then_inc(S["setup"], 1)
                dve.wait_ge(S["w_loaded"], 16 * (1 + (bo is not None)))
                dve.tensor_copy(WS[:, 0], WR[:]).then_inc(S["w_hi"], 1)
                dve.wait_ge(S["w_hi"], 1)
                dve.tensor_tensor(WS[:, 1], WR[:], WS[:, 0], ALU.subtract).then_inc(S["w_lo"], 1)

                def permute(b, j):
                    dve.wait_ge(S["stacked"], index(b, 16 * n_stack, 16 * n_stack))
                    words = [t.bitcast(mybir.dt.int32) for t in ((QS, KS)[j][0:STACK, b % RING], QK[:, j])]
                    dve.tensor_copy(words[0].rearrange("p g (h s) -> p g h s", s=DH // 2),
                                    words[1].rearrange("p h (g s) -> p g h s", s=DH // 2)).then_inc(S["permuted"], 1)

                def maxima(b, u):
                    dve.wait_ge(S["s_done"], index(b, UNITS, u + 1))
                    dve.tensor_reduce(MX[:, u // 8, :, u % 8], s_bank(u), AX.X, ALU.max).then_inc(S["s_used"], 1)

                def split_max(b, half, first=False):
                    dve.wait_ge(S["max_turned"], index(b, 2, half + 1))
                    if not first:
                        dve.wait_ge(S["max_placed"], index(b, 2 * per_half, (half - 1) * per_half))
                    bank = ps[0:8, 7, half * SEQ:(half + 1) * SEQ]
                    dve.tensor_scalar(MR[:, half, 0, :], bank, -1.0, None, ALU.mult).then_inc(S["neg_hi"], 1)
                    dve.wait_ge(S["neg_hi"], index(b, 2, half + 1))
                    dve.scalar_tensor_tensor(MR[:, half, 1, :], bank, -1.0, MR[:, half, 0, :], ALU.mult,
                                             ALU.subtract).then_inc(S["max_ready"], 1)

                def mask(b, u):
                    dve.wait_ge(S["st_done"], index(b, TURNS, u // 2 + 1))
                    dve.tensor_tensor(PB[:, u % PR:u % PR + 2, :, 0:P], st_bank(u),
                                      masks[:].unsqueeze(1).to_broadcast([P, 2, 2, P]), ALU.mult).then_inc(S["probs"], 1)

                def normalise_context(b, t):
                    dve.wait_ge(S["c_turned"], index(b, 2, t + 2))
                    src = ps[:, 5 + t, :].rearrange("p (h e) -> p h e", e=32)
                    dst = CN[:, t, :].rearrange("p (h e) -> p h e", e=DH)
                    if softmax:
                        dve.reciprocal(IV[:, t, :], src[:, :, DH]).then_inc(S["inv_ready"], 1)
                        dve.wait_ge(S["inv_ready"], index(b, 2, t + 1))
                        dve.tensor_tensor(dst, src[:, :, 0:DH], IV[:, t, :].unsqueeze(2).to_broadcast([P, HEADS, DH]),
                                          ALU.mult).then_inc(S["cn_ready"], 1)
                    else:
                        dve.tensor_copy(dst, src[:, :, 0:DH]).then_inc(S["cn_ready"], 1)

                def split_context(b):
                    dve.wait_ge(S["ct_hi"], b + 1)
                    dve.tensor_tensor(CT[:, 1], ps[:, 5, :].rearrange("p (k t) -> p k t", k=KD), CT[:, 0],
                                      ALU.subtract).then_inc(S["ct_lo"], 1)

                def add_out(b):
                    dve.wait_ge(S["out_done"], b + 2)
                    dst = (U if rows else X)[:, bass.ds(2 * b, 2), :]
                    dve.tensor_tensor(dst, ps[:, 6, :].rearrange("p (t n) -> p t n", t=2), dst,
                                      ALU.add).then_inc(S["x_ready"], 1)

                def step(i, first=False, ahead=True, more=True):
                    for u in range(UNITS):
                        if softmax and ahead:
                            maxima(i + 1, u)
                            if u == 10:
                                split_max(i + 1, 0)
                        if softmax and u == 2:
                            split_max(i, 1, first=first)
                        if not softmax:
                            if not (first and u < PR) and u % 4 == 0:
                                dve.wait_ge(S["pv_done"], index(i, 4, u // 4 - 1))
                            if u % 2 == 0:
                                mask(i, u)
                        if rows and more and u in (11, 13):
                            permute(i + 2, u // 13)
                        if not first and u == 8:
                            normalise_context(i - 1, 0)
                            normalise_context(i - 1, 1)
                        if not first and u == 12:
                            split_context(i - 1)
                    if not first:
                        add_out(i - 1)

                if bo is not None:
                    dve.wait_ge(S["biased"], 1)
                if rows:
                    permute(0, 0)
                    permute(0, 1)
                if softmax:
                    for u in range(UNITS):
                        maxima(0, u)
                        if u == 10:
                            split_max(0, 0, first=True)
                if rows:
                    permute(1, 0)
                    permute(1, 1)
                step(0, first=True)
                with dve.Fori(1, IMAGES - 2) as i:
                    step(i)
                step(IMAGES - 2, more=False)
                step(IMAGES - 1, ahead=False, more=False)
                last = IMAGES - 1
                normalise_context(last, 0)
                normalise_context(last, 1)
                split_context(last)
                add_out(last)

            @block.gpsimd
            def _(pool):
                def copy_v(b, quad):
                    dst = VS[:, :, 4 * quad:4 * quad + 4, 0:DH]
                    if rows:
                        if quad == 0:
                            pool.wait_ge(S["v_loaded"], index(b, 256, 256))
                        for t in range(2):
                            last = pool.tensor_copy(dst[:, t], VG[:, b % 2, t, 4 * quad:4 * quad + 4])
                    else:
                        src = vt[:, bass.ds(2 * b, 2), 4 * quad * DH:4 * (quad + 1) * DH]
                        last = pool.tensor_copy(dst, src.rearrange("p t (h e) -> p t h e", e=DH))
                    last.then_inc(S["v_copied"], 1)

                if bo is not None:
                    pool.wait_ge(S["w_loaded"], 32)
                    for t in range(TILES):
                        dst = (U if rows else X)[:, t, :]
                        last = pool.tensor_tensor(dst, dst, BO[:], ALU.add)
                    last.then_inc(S["biased"], 1)
                pool.wait_ge(S["setup"], 5)
                for quad in range(4):
                    copy_v(0, quad)
                with pool.Fori(1, IMAGES) as b:
                    for quad in range(4):
                        pool.wait_ge(S["pv_done"], b * 4 - 3 + quad)
                        copy_v(b, quad)


def relative(nc, G, name, rel_h, rel_w, scr_r):
    QF, ps = G["QF"], G["psum"]
    with Phase(nc, name) as ph:
        T = ph.sbuf("tables", [P, 2, SIDE, P])
        F = ph.sbuf("rel", [P, 2, TOKENS])
        R1 = ph.sbuf("rest", [P, TOKENS])
        PT = ph.sbuf("parts", [P, 3, TOKENS], BF16)
        zeroed, placed, done, ready = ph.sem("zeroed"), ph.sem("placed"), ph.sem("done"), ph.sem("ready")
        part1, rest1, part2, part3, spilled = (ph.sem(s) for s in ("part1", "rest1", "part2", "part3", "spilled"))
        UNITS = [(axis, t) for axis in range(2) for t in range(KD)]

        def queries(t, axis, q):
            x = QF[:, t, :].rearrange("p (b y x) -> p b y x", y=SIDE, x=SIDE)
            return x[:, :, q, :] if axis == 0 else x[:, :, :, q]

        def into(u, axis, g):
            x = F[:, u % 2, :].rearrange("p (b y x) -> p b y x", y=SIDE, x=SIDE)
            if axis == 0:
                return x[:, :, 4 * g:4 * g + 4, :].rearrange("p b q o -> p q b o")
            return x[:, :, :, 4 * g:4 * g + 4].rearrange("p b o q -> p q b o")

        with nc.Block() as block:
            @block.sync
            def _(sp):
                sp.wait_ge(zeroed, 1)
                for axis, table in enumerate((rel_h, rel_w)):
                    for j in range(8):
                        rows = slice(j * DH, (j + 1) * DH)
                        sp.dma_start(T[rows, axis, :, rows], table).then_inc(placed, 16)
                for u, (axis, t) in enumerate(UNITS):
                    sp.wait_ge(part3, u + 1)
                    dst = scr_r[3 * axis:3 * axis + 3, t * P:(t + 1) * P, :].rearrange("a p n -> p a n")
                    sp.dma_start(dst, PT[:]).then_inc(spilled, 16)
                    sp.wait_ge(spilled, 16 * (u + 1))

            @block.tensor
            def _(pe):
                pe.wait_ge(placed, 16 * 16)
                for u, (axis, t) in enumerate(UNITS):
                    for g in range(4):
                        bank = 4 * (u % 2) + g
                        if u >= 2:
                            pe.wait_ge(ready, 4 * (u - 2) + g + 1)
                        for q in range(4 * g, 4 * g + 4):
                            out = ps[:, bank, (q % 4) * P:(q % 4 + 1) * P]
                            last = pe.matmul(out, T[:, axis, q, :], queries(t, axis, q), start=True, stop=True)
                        last.then_inc(done, 1)

            @block.scalar
            def _(act):
                for u, (axis, t) in enumerate(UNITS):
                    if u >= 2:
                        act.wait_ge(rest1, u - 1)
                    for g in range(4):
                        act.wait_ge(done, 4 * u + g + 1)
                        src = ps[:, 4 * (u % 2) + g, :].rearrange("p (q b o) -> p q b o", b=IMAGES, o=SIDE)
                        for q in range(4):
                            last = act.activation(into(u, axis, g)[:, q], src[:, q], ACT.Copy, scale=4.0)
                        last.then_inc(ready, 1)

            @block.vector
            def _(dve):
                dve.memset(T[:].rearrange("p a q m -> p (a q m)"), 0.0).then_inc(zeroed, 1)
                for u in range(len(UNITS)):
                    dve.wait_ge(ready, 4 * u + 4)
                    if u:
                        dve.wait_ge(spilled, 16 * u)
                    dve.tensor_copy(PT[:, 0, :], F[:, u % 2, :]).then_inc(part1, 1)
                    dve.wait_ge(rest1, u + 1)
                    dve.tensor_copy(PT[:, 1, :], R1[:]).then_inc(part2, 1)
                    dve.wait_ge(part2, u + 1)
                    dve.tensor_tensor(PT[:, 2, :], R1[:], PT[:, 1, :], ALU.subtract).then_inc(part3, 1)

            @block.gpsimd
            def _(pool):
                for u in range(len(UNITS)):
                    pool.wait_ge(part1, u + 1)
                    if u:
                        pool.wait_ge(part3, u)
                    pool.tensor_tensor(R1[:], F[:, u % 2, :], PT[:, 0, :], ALU.subtract).then_inc(rest1, 1)


def route(nc, G, name, wg, bias, n_exp, top, first_col, softmax):
    RT, GW, ident, ps = G["RT"], G["GW"], G["ident"], G["psum"]
    with Phase(nc, name) as ph:
        WG = ph.sbuf("wg", [P, KD, n_exp])
        BG = ph.sbuf("bias", [P, n_exp])
        LT = ph.sbuf("logits_t", [n_exp, TOKENS])
        L = ph.sbuf("logits", [P, TILES, n_exp])
        CMP = ph.sbuf("compared", [P, TILES, n_exp, n_exp])
        EQ = ph.sbuf("equal", [P, TILES, n_exp, n_exp])
        RK = ph.sbuf("rank", [P, TILES, n_exp])
        MK = ph.sbuf("mask", [P, TILES, n_exp])
        MX = ph.sbuf("max", [P, TILES])
        EX = ph.sbuf("exp", [P, TILES, n_exp])
        loaded, done, ready, turned, chain, shifted, exped = (
            ph.sem(s) for s in ("loaded", "done", "ready", "turned", "chain", "shifted", "exped"))
        full = [P, TILES, n_exp, n_exp]
        with nc.Block() as block:
            @block.sync
            def _(sp):
                sp.dma_start(WG[:], wg).then_inc(loaded, 16)
                if bias is not None:
                    sp.dma_start(BG[:], bias.partition_broadcast(P)).then_inc(loaded, 16)

            @block.tensor
            def _(pe):
                pe.wait_ge(loaded, 16 * (1 + (bias is not None)))
                for n in range(BLOCKS):
                    for k in range(KD):
                        last = pe.matmul(ps[0:n_exp, n, :], WG[:, k, :], RT[:, k, n * BLOCK:(n + 1) * BLOCK],
                                         start=k == 0, stop=k == KD - 1)
                    last.then_inc(done, 1)
                pe.wait_ge(ready, BLOCKS)
                for t in range(TILES):
                    last = pe.transpose(ps[:, 4, t * n_exp:(t + 1) * n_exp], LT[:, t * P:(t + 1) * P],
                                        ident[0:n_exp, 0:n_exp])
                last.then_inc(turned, 1)

            @block.scalar
            def _(act):
                for n in range(BLOCKS):
                    act.wait_ge(done, n + 1)
                    act.activation(LT[:, n * BLOCK:(n + 1) * BLOCK], ps[0:n_exp, n, :], ACT.Copy).then_inc(ready, 1)
                if softmax:
                    act.wait_ge(shifted, 1)
                    act.activation(EX[:], EX[:], ACT.Exp).then_inc(exped, 1)

            @block.vector
            def _(dve):
                link = Chain(dve, chain)
                dve.wait_ge(turned, 1)
                link(dve.tensor_copy(L[:], ps[:, 4, 0:TILES * n_exp].rearrange("p (t e) -> p t e", e=n_exp)))
                if bias is not None:
                    link(dve.tensor_tensor(L[:], L[:], BG[:].unsqueeze(1).to_broadcast([P, TILES, n_exp]), ALU.add))
                own, other = L[:].unsqueeze(3).to_broadcast(full), L[:].unsqueeze(2).to_broadcast(full)
                dve.tensor_tensor(CMP[:], other, own, ALU.is_gt).then_inc(chain, 1)
                dve.tensor_tensor(EQ[:], other, own, ALU.is_equal).then_inc(chain, 1)
                link.n += 2
                dve.wait_ge(chain, link.n)
                before = G["before"][:, 0:n_exp, 0:n_exp].unsqueeze(1).to_broadcast(full)
                link(dve.tensor_tensor(EQ[:], EQ[:], before, ALU.mult))
                link(dve.tensor_tensor(CMP[:], CMP[:], EQ[:], ALU.add))
                link(dve.tensor_reduce(RK[:], CMP[:], AX.X, ALU.add))
                link(dve.tensor_scalar(MK[:], RK[:], float(top) - 0.5, None, ALU.is_lt))
                if first_col:
                    link(dve.memset(GW[:, :, 0:first_col], 1.0))
                dst = GW[:, :, first_col:first_col + n_exp]
                if not softmax:
                    link(dve.tensor_copy(dst, MK[:]))
                    return
                link(dve.tensor_reduce(MX[:], L[:], AX.X, ALU.max))
                dve.tensor_tensor(EX[:], L[:], MX[:].unsqueeze(2).to_broadcast([P, TILES, n_exp]),
                                  ALU.subtract).then_inc(shifted, 1)
                dve.wait_ge(exped, 1)
                link(dve.tensor_tensor(EX[:], EX[:], MK[:], ALU.mult))
                link(dve.tensor_reduce(MX[:], EX[:], AX.X, ALU.add))
                link(dve.reciprocal(MX[:], MX[:]))
                link(dve.tensor_tensor(dst, EX[:], MX[:].unsqueeze(2).to_broadcast([P, TILES, n_exp]), ALU.mult))


def experts(nc, G, name, w, n_exp, n_h):
    X, RT, GW, ps = G["X"], G["RT"], G["GW"], G["psum"]
    W1, W3 = KD * n_h * P, n_h * D
    WN = 2 * W1 + W3
    QUARTER = WN // BLOCKS
    LAG = 2
    RG = 3 if n_h % 3 == 0 else 2
    with Phase(nc, name) as ph:
        WR = ph.sbuf("w_raw", [P, WN])
        WS = ph.sbuf("w_split", [P, 2, 2, WN], R32)
        XS = ph.sbuf("x_split", [P, 2, KD, TOKENS], R32)
        SL = ph.sbuf("silu", [P, 2, BLOCK])
        GF = ph.sbuf("hidden", [P, 2, BLOCK])
        GS = ph.sbuf("hidden_split", [P, 2, RG, BLOCK], R32)
        names = ["loaded", "w_hi", "w_split", "x_hi", "x_lo", "up_done", "silu", "hidden", "g_hi", "g_lo",
                 "used", "added", "sp_steps", "pe_steps"]
        S = {n: ph.sem(n) for n in names}
        TT = BLOCK // P

        def up(r, a, k, m, which):
            o = which * W1 + k * n_h * P + m * P
            return WS[:, r, a, o:o + P]

        def down(r, a, m):
            o = 2 * W1 + m * D
            return WS[:, r, a, o:o + D]

        def over_experts(eng, body):
            body(0, 0)
            pairs = (n_exp - 2) // 2
            with eng.Fori(0, pairs) as i:
                body(2 * i + 1, 1)
                body(2 * i + 2, 0)
            for e in range(2 * pairs + 1, n_exp):
                body(e, e % 2)

        with nc.Block() as block:
            @block.sync
            def _(sp):
                sp.dma_start(WR[:], w[0]).then_inc(S["loaded"], 16)
                with sp.Fori(1, n_exp) as e:
                    sp.wait_ge(S["w_split"], BLOCKS * e)
                    sp.sem_inc(S["sp_steps"], 1)
                    sp.dma_start(WR[:], w[bass.ds(e, 1)].rearrange("o p n -> (o p) n")).then_inc(S["loaded"], 16)

            @block.tensor
            def _(pe):
                def make_hidden(e, r, n, m):
                    pe.wait_ge(S["hidden"], (e * BLOCKS + n) * n_h + m + 1)
                    for which in range(2):
                        last = split_matmuls(pe, ps[:, 2 * (m % 2) + which, :],
                                             lambda a, k: up(r, a, k, m, which),
                                             lambda a, k: XS[:, a, k, bass.ds(n * BLOCK, BLOCK)], KD)
                    last.then_inc(S["up_done"], 1)

                def use_hidden(e, r, n, m):
                    pe.wait_ge(S["g_lo"], (e * BLOCKS + n) * n_h + m + 1)
                    for t in range(TT):
                        if m == 0:
                            pe.wait_ge(S["added"], (e * BLOCKS + n) * TT + t + 1)
                        for i, (a, b) in enumerate(((0, 0), (0, 1), (1, 0))):
                            last = pe.matmul(ps[:, 4 + t, 0:D], GS[:, a, m % RG, t * P:(t + 1) * P], down(r, b, m),
                                             start=m == 0 and i == 0, stop=m == n_h - 1 and i == 2)
                        last.then_inc(S["used"], 1)

                def steps(e, r, n, before):
                    for m in range(n_h):
                        make_hidden(e, r, n, m)
                        if m >= LAG:
                            use_hidden(e, r, n, m - LAG)
                        elif before:
                            use_hidden(*before, n_h - LAG + m)

                def expert(e, r):
                    pe.wait_ge(S["w_split"], BLOCKS * e + BLOCKS)
                    pe.sem_inc(S["pe_steps"], 1)
                    steps(e, r, 0, None if isinstance(e, int) and e == 0 else (e - 1, 1 - r, BLOCKS - 1))
                    with pe.Fori(1, BLOCKS) as n:
                        steps(e, r, n, (e, r, n - 1))
                pe.wait_ge(S["x_lo"], 1)
                over_experts(pe, expert)
                for m in range(n_h - LAG, n_h):
                    use_hidden(n_exp - 1, (n_exp - 1) % 2, BLOCKS - 1, m)

            @block.scalar
            def _(act):
                def expert(e, r):
                    with act.Fori(0, BLOCKS) as n:
                        for m in range(n_h):
                            act.wait_ge(S["up_done"], (e * BLOCKS + n) * n_h + m + 1)
                            act.wait_ge(S["hidden"], (e * BLOCKS + n) * n_h + m + 1)
                            act.activation(SL[:, m % 2], ps[:, 2 * (m % 2), :], ACT.Silu).then_inc(S["silu"], 1)
                over_experts(act, expert)

            @block.vector
            def _(dve):
                dve.sem_inc(S["hidden"], 2)
                dve.sem_inc(S["added"], TT)
                dve.tensor_copy(XS[:, 0], RT[:]).then_inc(S["x_hi"], 1)

                def add_out(e, n):
                    for t in range(TT):
                        dve.wait_ge(S["used"], ((e * BLOCKS + n) * n_h + n_h - 1) * TT + t + 1)
                        x = X[:, bass.ds(n * TT + t, 1), :].rearrange("p o n -> p (o n)")
                        gate = GW[:, bass.ds(n * TT + t, 1), bass.ds(e, 1)].rearrange("p o n -> p (o n)")
                        dve.scalar_tensor_tensor(x, ps[:, 4 + t, 0:D], gate, x, ALU.mult, ALU.add).then_inc(S["added"], 1)

                def steps(e, n, before):
                    first = before is None
                    for m in range(n_h):
                        c = (e * BLOCKS + n) * n_h + m
                        dve.wait_ge(S["silu"], c + 1)
                        if not first or m >= 2:
                            dve.wait_ge(S["g_lo"], c - 1)
                        dve.tensor_tensor(GF[:, m % 2], ps[:, 2 * (m % 2) + 1, :], SL[:, m % 2],
                                          ALU.mult).then_inc(S["hidden"], 1)
                        if not first or m >= RG:
                            dve.wait_ge(S["used"], (c - RG + 1) * TT)
                        dve.wait_ge(S["hidden"], c + 3)
                        dve.tensor_copy(GS[:, 0, m % RG], GF[:, m % 2]).then_inc(S["g_hi"], 1)
                        if m == LAG - 1 and not first:
                            add_out(*before)

                def expert(e, r):
                    steps(e, 0, None if isinstance(e, int) and e == 0 else (e - 1, BLOCKS - 1))
                    with dve.Fori(1, BLOCKS) as n:
                        steps(e, n, (e, n - 1))
                over_experts(dve, expert)
                add_out(n_exp - 1, BLOCKS - 1)

            @block.gpsimd
            def _(pool):
                def split(e, r, n):
                    q = bass.ds(n * QUARTER, QUARTER)
                    pool.tensor_copy(WS[:, r, 0, q], WR[:, q]).then_inc(S["w_hi"], 1)
                    pool.wait_ge(S["w_hi"], e * BLOCKS + n + 1)
                    pool.tensor_tensor(WS[:, r, 1, q], WR[:, q], WS[:, r, 0, q], ALU.subtract).then_inc(S["w_split"], 1)

                pool.wait_ge(S["loaded"], 16)
                for n in range(BLOCKS):
                    split(0, 0, n)
                pool.wait_ge(S["x_hi"], 1)
                pool.tensor_tensor(XS[:, 1], RT[:], XS[:, 0], ALU.subtract).then_inc(S["x_lo"], 1)

                def expert(e, r):
                    last = isinstance(e, int) and e == n_exp - 1
                    with pool.Fori(0, BLOCKS) as n:
                        for m in range(n_h):
                            pool.wait_ge(S["g_hi"], (e * BLOCKS + n) * n_h + m + 1)
                            pool.tensor_tensor(GS[:, 1, m % RG], GF[:, m % 2], GS[:, 0, m % RG],
                                               ALU.subtract).then_inc(S["g_lo"], 1)
                            if m == LAG - 1 and not last:
                                if not (isinstance(e, int) and e == 0):
                                    pool.wait_ge(S["used"], e * (BLOCKS * n_h * TT))
                                pool.wait_ge(S["loaded"], e * 16 + 32)
                                split(e + 1, 1 - r, n)
                over_experts(pool, expert)


def program(nc, A, out, stop=None):
    scr = {n: nc.dram_tensor(f"scr_{n}", [3, D, TOKENS], BF16, kind="Internal").ap() for n in ("q0", "k0", "q1", "k1")}
    scr["r"] = nc.dram_tensor("scr_r", [6, D, TOKENS], BF16, kind="Internal").ap()
    scr["v"] = nc.dram_tensor("scr_v", [TOKENS, D], F32, kind="Internal").ap()
    with ExitStack() as ctx:
        def sb(name, shape, dt=F32):
            return ctx.enter_context(nc.sbuf_tensor(name, shape, dt))
        G = {"X": sb("x_tokens", [P, TILES, D]), "U": sb("u_tokens", [P, TILES, D]), "ident": sb("ident", [P, P]),
             "group_avg": sb("group_avg", [P, P]), "mask": sb("mask", [P, 2, P]),
             "where": sb("where", [STACK, SEQ], BF16), "before": sb("before", [P, 8, 8])}
        G["psum"] = ctx.enter_context(nc.psum_tensor("psum", [P, 8, 512], F32))
        X = G["X"]

        with Phase(nc, "load") as ph:
            where32 = ph.sbuf("where32", [STACK, SEQ])
            loaded, cast = ph.sem("loaded"), ph.sem("cast")
            with nc.Block() as block:
                @block.sync
                def _(sp):
                    sp.dma_start(X[:], A["x"].rearrange("b (t y) x c -> (y x) (b t) c", t=2)).then_inc(loaded, 16)
                    sp.dma_start(G["ident"][:], A["c_ident"]).then_inc(loaded, 16)
                    sp.dma_start(G["group_avg"][:], A["c_group"]).then_inc(loaded, 16)
                    sp.dma_start(G["mask"][:], A["c_mask"]).then_inc(loaded, 16)
                    sp.dma_start(where32[:], A["c_where"]).then_inc(loaded, 16)
                    sp.dma_start(G["before"][:], A["c_before"]).then_inc(loaded, 16)

                @block.vector
                def _(dve):
                    dve.wait_ge(loaded, 96)
                    dve.tensor_copy(G["where"][:], where32[:]).then_inc(cast, 1)

        vs = ExitStack()
        def values_tensor(name):
            vs.close()
            G["v0"] = vs.enter_context(nc.sbuf_tensor(name, [P, TILES, D], F32)) if name else None

        def attention_inputs():
            part = ExitStack()
            for n in ("RT", "QF", "KF"):
                G[n] = part.enter_context(nc.sbuf_tensor(f"{n}_{nc.next_id()}", [P, KD, TOKENS], F32))
            return part

        values_tensor("v0")
        with attention_inputs():
            normalise(nc, G, "n0", "group")
            project(nc, G, "p0", [A["L0_conv_w_qkv0"]], None, True, G["v0"], scr["q0"], scr["k0"])
            project(nc, G, "p1", [A["L0_conv_w_qkv1"]], None, False, G["U"], scr["q1"], scr["k1"])
        attend(nc, G, "a0", "linear", G["v0"], scr["q0"], scr["k0"], A["L0_conv_w_out0"], by_columns=True)
        attend(nc, G, "a1", "linear", G["U"], scr["q1"], scr["k1"], A["L0_conv_w_out1"])
        if stop == "L0":
            return (vs.close(), store(nc, G, out))

        with attention_inputs():
            normalise(nc, G, "n2", "group")
            b = A["L1_conv_qkv_b"]
            project(nc, G, "p2", [A["L1_conv_qkv_w"]], (b[0:D], b[D:2 * D], b[2 * D:3 * D]), False, G["v0"], scr["q0"], scr["k0"])
            relative(nc, G, "r2", A["rel_h"], A["rel_w"], scr["r"])
        attend(nc, G, "a2", "rel", G["v0"], scr["q0"], scr["k0"], A["L1_conv_proj_w"], A["L1_conv_proj_b"], scr_r=scr["r"])
        if stop == "L1":
            return (vs.close(), store(nc, G, out))

        with attention_inputs():
            normalise(nc, G, "n3", "layer")
            project(nc, G, "p3", [A["L2_attn_wq"], A["L2_attn_wk"], A["L2_attn_wv"]],
                    (A["L2_attn_bq"], A["L2_attn_bk"], A["L2_attn_bv"]), False, G["v0"], scr["q0"], scr["k0"], scr["v"])
        attend(nc, G, "a3", "rows", G["v0"], scr["q0"], scr["k0"], A["L2_attn_wo"], A["L2_attn_bo"], scr_v=scr["v"])
        affine_norm(nc, G, "f3", A["L2_attn_gamma"], A["L2_attn_beta"])
        if stop == "L2a":
            return (vs.close(), store(nc, G, out))

        values_tensor(None)

        def feed_forward(n, wg, bias, n_exp, top, first_col, softmax, w, n_h):
            with ExitStack() as part:
                G["GW"] = part.enter_context(nc.sbuf_tensor(f"gates{n}", [P, TILES, first_col + n_exp], F32))
                G["RT"] = part.enter_context(nc.sbuf_tensor(f"x_norm{n}", [P, KD, TOKENS], F32))
                normalise(nc, G, f"n{n}", "layer")
                route(nc, G, f"g{n}", wg, bias, n_exp, top, first_col, softmax)
                experts(nc, G, f"e{n}", w, first_col + n_exp, n_h)
        feed_forward(4, A["L2_ffn_Wg"], None, 8, 1, 0, False, A["w_ffn2"], A["w_ffn2"].shape[2] // (3 * D))
        if stop == "L2f":
            return (vs.close(), store(nc, G, out))

        values_tensor("v5")
        with attention_inputs():
            normalise(nc, G, "n5", "layer")
            b, w = A["L3_attn_b_attn"], A["L3_attn_w_attn"]
            project(nc, G, "p5", [w], (b[0:D], b[D:2 * D], b[2 * D:3 * D]), False, G["v0"], scr["q0"], scr["k0"])
        attend(nc, G, "a5", "heads", G["v0"], scr["q0"], scr["k0"], A["L3_attn_w_proj"], A["L3_attn_b_proj"])
        if stop == "L3a":
            return (vs.close(), store(nc, G, out))

        values_tensor(None)
        feed_forward(6, A["L3_ffn_Wg"], A["L3_ffn_routing_bias"], 8, 4, 1, True, A["w_ffn3"], A["w_ffn3"].shape[2] // (3 * D))
        store(nc, G, out)


def store(nc, G, out):
    with Phase(nc, "store") as ph:
        stored = ph.sem("stored")
        with nc.Block() as block:
            @block.sync
            def _(sp):
                sp.dma_start(out.rearrange("b (t y) x c -> (y x) (b t) c", t=2), G["X"][:]).then_inc(stored, 16)
                sp.wait_ge(stored, 16)


def affine_norm(nc, G, name, gamma, beta, eps=1e-5):
    X, U = G["X"], G["U"]
    with Phase(nc, name) as ph:
        GB = ph.sbuf("gamma_beta", [P, 2, D])
        ST = ph.sbuf("stats", [P, TILES, 6])
        MV = ph.sbuf("mean_var", [P, TILES, 2])
        VE, SD, RS, TM = (ph.sbuf(n, [P, TILES]) for n in ("var_eps", "std", "rstd", "tmp"))
        loaded, chain, var_ready, std_ready, normed, scaled = (
            ph.sem(s) for s in ("loaded", "chain", "var_ready", "std_ready", "normed", "scaled"))
        with nc.Block() as block:
            @block.sync
            def _(sp):
                for i, v in enumerate((gamma, beta)):
                    sp.dma_start(GB[:, i, :], v.partition_broadcast(P)).then_inc(loaded, 16)

            @block.scalar
            def _(act):
                act.wait_ge(var_ready, 1)
                act.activation(SD[:], VE[:], ACT.Sqrt).then_inc(std_ready, 1)

            @block.vector
            def _(dve):
                link = Chain(dve, chain)
                for t in range(TILES):
                    link(dve.bn_stats(ST[:, t, :], U[:, t, :]))
                for t in range(TILES):
                    link(dve.bn_aggr(MV[:, t, :], ST[:, t, :]))
                dve.tensor_scalar_add(VE[:], MV[:, :, 1], eps).then_inc(var_ready, 1)
                dve.wait_ge(std_ready, 1)
                inverse_root(dve, link, SD[:], VE[:], RS[:], TM[:])
                dve.wait_ge(loaded, 32)
                for t in range(TILES):
                    link(dve.tensor_scalar(U[:, t, :], U[:, t, :], MV[:, t, 0:1], RS[:, t:t + 1], ALU.subtract, ALU.mult))
                    dve.tensor_tensor(U[:, t, :], U[:, t, :], GB[:, 0, :], ALU.mult).then_inc(normed, 1)
                for t in range(TILES):
                    dve.wait_ge(scaled, t + 1)
                    dve.tensor_tensor(X[:, t, :], X[:, t, :], U[:, t, :], ALU.add).then_inc(chain, 1)

            @block.gpsimd
            def _(pool):
                pool.wait_ge(loaded, 32)
                for t in range(TILES):
                    pool.wait_ge(normed, t + 1)
                    pool.tensor_tensor(U[:, t, :], U[:, t, :], GB[:, 1, :], ALU.add).then_inc(scaled, 1)


def layouts(inputs):
    a = {k: np.asarray(v) for k, v in inputs.items()}
    dist = np.arange(SIDE)[:, None] - np.arange(SIDE)[None, :] + SIDE - 1
    out = {k: v for k, v in a.items() if not k.startswith(("L1_conv_rel", "L2_ffn", "L3_ffn"))}
    out["rel_h"] = a["L1_conv_rel_pos_h"].T[:, dist]
    out["rel_w"] = a["L1_conv_rel_pos_w"].T[:, dist]
    i = np.arange(P)
    out["c_ident"] = np.eye(P, dtype=np.float32)
    out["c_group"] = (i[:, None] // GROUP == i[None, :] // GROUP).astype(np.float32) / GROUP
    same = (i[:, None] // SIDE == i[None, :] // SIDE).astype(np.float32) / SIDE
    out["c_mask"] = np.stack([same, same], axis=1)
    key = np.arange(SEQ)
    where = [(np.arange(SIDE)[:, None] == k[None, :]).astype(np.float32) for k in (key // SIDE, key % SIDE)]
    out["c_where"] = np.concatenate([where[0]] * 3 + [where[1]] * 3)
    e = np.arange(8)
    out["c_before"] = np.broadcast_to((e[None, :] < e[:, None]).astype(np.float32), (P, 8, 8))
    for n in ("L2_ffn_Wg", "L3_ffn_Wg"):
        out[n] = a[n].T.reshape(KD, P, -1).transpose(1, 0, 2)
    out["L3_ffn_routing_bias"] = a["L3_ffn_routing_bias"]
    out["w_ffn2"] = expert_layout(a["L2_ffn_gate_bank"], a["L2_ffn_up_bank"], a["L2_ffn_down_bank"])
    w1, w2, w3 = (np.concatenate([a[f"L3_ffn_Ws{i}"][None], a[f"L3_ffn_W{i}"]]) for i in (1, 2, 3))
    out["w_ffn3"] = expert_layout(w1.transpose(0, 2, 1), w2.transpose(0, 2, 1), w3.transpose(0, 2, 1))
    return {k: np.ascontiguousarray(v) for k, v in out.items()}


def expert_layout(w1, w2, w3):
    n, _, h = w1.shape
    pad = -h % P
    ups = [np.pad(w, ((0, 0), (0, 0), (0, pad))).reshape(n, KD, P, h + pad).transpose(0, 2, 1, 3).reshape(n, P, -1)
           for w in (w1, w2)]
    down = np.pad(w3, ((0, 0), (0, pad), (0, 0))).reshape(n, (h + pad) // P, P, D).transpose(0, 2, 1, 3).reshape(n, P, -1)
    return np.concatenate(ups + [down], axis=2)


def kernel(**inputs):
    import concourse.bacc as bacc
    from concourse.bass_utils import run_bass_kernel_spmd
    nc = bacc.Bacc("TRN2", target_bir_lowering=False, num_devices=1)
    arrays = {f"in_{k}": v for k, v in layouts(inputs).items()}
    aps = {k[3:]: nc.dram_tensor(k, v.shape, mybir.dt.from_np(v.dtype), kind="ExternalInput").ap()
           for k, v in arrays.items()}
    out = nc.dram_tensor("out", [IMAGES, SIDE, SIDE, D], F32, kind="ExternalOutput").ap()
    program(nc, aps, out)
    return run_bass_kernel_spmd(nc, [arrays], core_ids=[0]).results[0]["out"]
```

```python
from contextlib import ExitStack

import concourse.bass as bass
import numpy as np
from concourse import mybir

F32, R32, BF16 = mybir.dt.float32, mybir.dt.float32r, mybir.dt.bfloat16
ALU = mybir.AluOpType
ACT = mybir.ActivationFunctionType
AX = mybir.AxisListType

P = 128
IMAGES, SIDE, D = 8, 16, 256
SEQ = SIDE * SIDE
TOKENS = IMAGES * SEQ
TILES = TOKENS // P
KD = D // P
HEADS, DH = 16, 16
BLOCK = 512
BLOCKS = TOKENS // BLOCK
FFN2_HIDDEN, FFN3_HIDDEN = 256, 682
GROUP = 8
PAIRS = [(0, 0), (1, 0), (2, 0), (0, 1), (1, 1), (0, 2)]
STACK = len(PAIRS) * DH
SHIFT = 2


class Phase:

    def __init__(self, nc, name):
        self.nc, self.name, self.ctx, self.sems = nc, name, ExitStack(), []

    def sem(self, name):
        s = self.ctx.enter_context(self.nc.semaphore(f"{self.name}_{name}"))
        self.sems.append(s)
        return s

    def sbuf(self, name, shape, dt=F32):
        return self.ctx.enter_context(self.nc.sbuf_tensor(f"{self.name}_{name}", shape, dt))

    def __enter__(self):
        return self

    def __exit__(self, *e):
        if e[0] is None:
            with self.nc.Block() as block:
                @block.sync
                def _(sp):
                    for s in self.sems:
                        sp.sem_clear(s)
        self.ctx.close()


class Chain:

    def __init__(self, eng, sem):
        self.eng, self.sem, self.n = eng, sem, 0

    def __call__(self, ins):
        self.n += 1
        ins.then_inc(self.sem, 1)
        self.eng.wait_ge(self.sem, self.n)


def split_matmuls(eng, out, lhs, rhs, n_k):
    terms = [(k, a, b) for k in range(n_k) for a, b in ((0, 0), (0, 1), (1, 0))]
    for i, (k, a, b) in enumerate(terms):
        last = eng.matmul(out, lhs(a, k), rhs(b, k), start=i == 0, stop=i == len(terms) - 1)
    return last


def inverse_root(dve, link, root, ve, r, t):
    link(dve.reciprocal(r, root))
    link(dve.tensor_tensor(t, r, r, ALU.mult))
    link(dve.tensor_tensor(t, t, ve, ALU.mult))
    link(dve.tensor_scalar(t, t, -0.5, 1.5, ALU.mult, ALU.add))
    link(dve.tensor_tensor(r, r, t, ALU.mult))


def normalise(nc, G, name, norm, loads=(), splits=(), rests=True, stats_there=False, eps=1e-5):
    X, U, RT, ident, ps = G["X"], G["U"], G["RT"], G["ident"], G["psum"]
    gn = norm == "group"
    with Phase(nc, name) as ph:
        ST = G["stats"]
        MV = ph.sbuf("mean_var", [P, TILES, 2])
        SG = ph.sbuf("group_in", [P, 2, TILES])
        ME = ph.sbuf("group_mean", [P, 2, TILES])
        VE = ph.sbuf("var_eps", [P, TILES])
        SD = ph.sbuf("std", [P, TILES])
        RS = ph.sbuf("rstd", [P, TILES])
        TM = ph.sbuf("tmp", [P, TILES])
        transposed, evacuated, stats = ph.sem("transposed"), ph.sem("evacuated"), ph.sem("stats")
        group_in, group_out, var_ready, std_ready = (ph.sem("group_in"), ph.sem("group_out"),
                                                     ph.sem("var_ready"), ph.sem("std_ready"))
        chain, normed = ph.sem("chain"), ph.sem("normed")
        w_loaded, w_hi, w_lo = ph.sem("w_loaded"), ph.sem("w_hi"), ph.sem("w_lo")
        src = X if gn else U
        mean = (lambda t: ME[:, 0, t:t + 1]) if gn else (lambda t: MV[:, t, 0:1])

        def pair(b):
            return ps[:, b % 4, :].rearrange("p (k t) -> p k t", k=KD)

        with nc.Block() as block:
            @block.sync
            def _(sp):
                with nc.allow_non_contiguous_dma("512 biases, one to a partition"):
                    for dst, src in loads:
                        sp.dma_start(dst, src).then_inc(w_loaded, 16)
                if loads:
                    sp.wait_ge(w_loaded, 16 * len(loads))

            @block.gpsimd
            def _(pool):
                for i, (raw, halves) in enumerate(splits if rests else ()):
                    pool.wait_ge(w_hi, i + 1)
                    pool.tensor_tensor(halves[:, 1], raw[:], halves[:, 0], ALU.subtract).then_inc(w_lo, 1)

            @block.tensor
            def _(pe):
                for b in range(IMAGES):
                    if not gn:
                        pe.wait_ge(normed, 2 * b + 2)
                    if b >= 4:
                        pe.wait_ge(evacuated, b - 3)
                    for j in range(2):
                        for k in range(KD):
                            last = pe.transpose(pair(b)[:, k, j * P:(j + 1) * P],
                                                src[:, 2 * b + j, k * P:(k + 1) * P], ident[:])
                    last.then_inc(transposed, 1)
                if gn:
                    pe.wait_ge(group_in, 1)
                    pe.matmul(ps[:, 4, 0:2 * TILES], G["group_avg"][:],
                              SG[:].rearrange("p a t -> p (a t)"), start=True, stop=True).then_inc(group_out, 1)

            @block.scalar
            def _(act):
                def evacuate():
                    for b in range(IMAGES):
                        act.wait_ge(transposed, b + 1)
                        act.activation(RT[:, :, b * SEQ:(b + 1) * SEQ], pair(b), ACT.Copy).then_inc(evacuated, 1)
                def split_weights():
                    if splits:
                        act.wait_ge(w_loaded, 16 * len(loads))
                    for raw, halves in splits:
                        act.activation(halves[:, 0], raw[:], ACT.Copy).then_inc(w_hi, 1)
                if gn:
                    evacuate()
                    split_weights()
                act.wait_ge(var_ready, 1)
                act.activation(SD[:], VE[:], ACT.Sqrt).then_inc(std_ready, 1)
                if not gn:
                    split_weights()
                if not gn:
                    evacuate()

            @block.vector
            def _(dve):
                link = Chain(dve, chain)
                for t in range(0 if stats_there else TILES):
                    if gn:
                        b, k = t // KD, t % KD
                        dve.wait_ge(evacuated, b + 1)
                        dve.bn_stats(ST[:, t, :], RT[:, k, b * SEQ:(b + 1) * SEQ]).then_inc(stats, 1)
                    else:
                        dve.bn_stats(ST[:, t, :], X[:, t, :]).then_inc(stats, 1)
                made = 0 if stats_there else TILES
                for t in range(TILES):
                    if not stats_there:
                        dve.wait_ge(stats, t + 1)
                    dve.bn_aggr(MV[:, t, :], ST[:, t, :]).then_inc(stats, 1)
                dve.wait_ge(stats, made + TILES)
                if gn:
                    link(dve.tensor_copy(SG[:, 0, :], MV[:, :, 0]))
                    link(dve.tensor_tensor(TM[:], SG[:, 0, :], SG[:, 0, :], ALU.mult))
                    dve.tensor_tensor(SG[:, 1, :], TM[:], MV[:, :, 1], ALU.add).then_inc(group_in, 1)
                    dve.wait_ge(group_out, 1)
                    link(dve.tensor_copy(ME[:].rearrange("p a t -> p (a t)"), ps[:, 4, 0:2 * TILES]))
                    link(dve.tensor_tensor(TM[:], ME[:, 0, :], ME[:, 0, :], ALU.mult))
                    link(dve.tensor_tensor(VE[:], ME[:, 1, :], TM[:], ALU.subtract))
                    dve.tensor_scalar_add(VE[:], VE[:], eps).then_inc(var_ready, 1)
                else:
                    dve.tensor_scalar_add(VE[:], MV[:, :, 1], eps).then_inc(var_ready, 1)
                dve.wait_ge(std_ready, 1)
                inverse_root(dve, link, SD[:], VE[:], RS[:], TM[:])
                for t in range(TILES):
                    if gn:
                        b, k = t // KD, t % KD
                        dst = RT[:, k, b * SEQ:(b + 1) * SEQ]
                        dve.tensor_scalar(dst, dst, mean(t), RS[:, t:t + 1], ALU.subtract, ALU.mult)\
                           .then_inc(normed, 1)
                    else:
                        dve.tensor_scalar(U[:, t, :], X[:, t, :], mean(t), RS[:, t:t + 1],
                                          ALU.subtract, ALU.mult).then_inc(normed, 1)


def project(nc, G, name, jobs, scr_v=None):
    RT, QF, KF, ps = G["RT"], G["QF"], G["KF"], G["psum"]
    with Phase(nc, name) as ph:
        bias = "bias_qk" in jobs[0][0]
        STEPS = BLOCKS * len(jobs)
        XS = ph.sbuf("x_split", [P, 2, 2, KD, BLOCK], R32)
        PT = ph.sbuf("parts", [P, 4, 3, BLOCK], BF16)
        R1 = ph.sbuf("rest", [P, 4, BLOCK])
        x_hi, x_lo = ph.sem("x_hi"), ph.sem("x_lo")
        qk_done, f_ready, part1, rest1, part2, part3 = (
            ph.sem(s) for s in ("qk_done", "f_ready", "part1", "rest1", "part2", "part3"))
        v_done, v_ready = ph.sem("v_done"), ph.sem("v_ready")
        spilled = [ph.sem(f"spilled{u}") for u in range(4)]
        v_spilled = ph.sem("v_spilled")

        def part_of(n):
            return jobs[n // BLOCKS] + (n % BLOCKS,)

        def blocks(n):
            _, by_columns, _, _, _, block = part_of(n)
            if not by_columns:
                return [(RT[:, :, block * BLOCK:(block + 1) * BLOCK], lambda a: XS[:, n % 2, a])]
            return [(RT[:, :, b * SEQ:(b + 1) * SEQ].rearrange("p k (y x) -> p k x y", x=SIDE),
                     lambda a, h=b % 2: XS[:, n % 2, a, :, h * SEQ:(h + 1) * SEQ].rearrange("p k (x y) -> p k x y", y=SIDE))
                    for b in (2 * block, 2 * block + 1)]

        def feat(u, n):
            block = n % BLOCKS
            return (QF, KF)[u // 2][:, u % 2, block * BLOCK:(block + 1) * BLOCK]

        def v_tiles(n, h):
            _, _, vt, _, _, block = part_of(n)
            return vt[:, 4 * block + 2 * h:4 * block + 2 * h + 2, :]

        with nc.Block() as block:
            @block.sync
            def _(sp):
                for n in range(STEPS):
                    _, _, vt, scr_q, scr_k, block = part_of(n)
                    tokens = slice(block * BLOCK, (block + 1) * BLOCK)
                    for u in range(4):
                        sp.wait_ge(part3, 4 * n + u + 1)
                        dst = (scr_q, scr_k)[u // 2][:, (u % 2) * P:(u % 2 + 1) * P, tokens]
                        sp.dma_start(dst.rearrange("a p n -> p a n"), PT[:, u, :, :]).then_inc(spilled[u], 16)
                    if scr_v is not None:
                        sp.wait_ge(v_ready, 2 * n + 2)
                        dst = scr_v[tokens, :].rearrange("(t p) n -> p t n", p=P)
                        sp.dma_start(dst, vt[:, 4 * block:4 * block + 4, :]).then_inc(v_spilled, 16)
                if scr_v is not None:
                    sp.wait_ge(v_spilled, 16 * STEPS)
                for u in range(4):
                    sp.wait_ge(spilled[u], 16 * STEPS)

            @block.tensor
            def _(pe):
                for n in range(STEPS):
                    s, WS = n % 2, part_of(n)[0]["split"]
                    pe.wait_ge(x_hi, n + 1)
                    pe.wait_ge(x_lo, n + 1)
                    for u in range(4):
                        if n:
                            pe.wait_ge(f_ready, 4 * (n - 1) + u + 1)
                        split_matmuls(pe, ps[:, u, :], lambda a, k: WS[:, a, k, u * P:(u + 1) * P],
                                      lambda a, k: XS[:, s, a, k, :], KD).then_inc(qk_done, 1)
                    for h in range(2):
                        if n:
                            pe.wait_ge(v_ready, 2 * (n - 1) + h + 1)
                        for j in range(2):
                            t0 = (2 * h + j) * P
                            last = split_matmuls(pe, ps[:, 4 + h, j * D:(j + 1) * D],
                                                 lambda a, k: XS[:, s, a, k, t0:t0 + P],
                                                 lambda a, k: WS[:, a, k, 2 * D:3 * D], KD)
                        last.then_inc(v_done, 1)

            def v_bank(h):
                return ps[:, 4 + h, :].rearrange("p (t n) -> p t n", t=2)

            @block.scalar
            def _(act):
                for n in range(STEPS):
                    W = part_of(n)[0]
                    for u in range(4):
                        act.wait_ge(qk_done, 4 * n + u + 1)
                        if bias:
                            act.activation(feat(u, n), ps[:, u, :], ACT.Identity, bias=W["bias_qk"][:, u:u + 1]).then_inc(f_ready, 1)
                        else:
                            act.activation(feat(u, n), ps[:, u, :], ACT.Copy).then_inc(f_ready, 1)
                    if not bias:
                        for h in range(2):
                            act.wait_ge(v_done, 2 * n + h + 1)
                            act.activation(v_tiles(n, h), v_bank(h), ACT.Copy).then_inc(v_ready, 1)

            @block.vector
            def _(dve):
                def split_block(n):
                    if n >= 2:
                        dve.wait_ge(v_done, 2 * (n - 1))
                    for src, split in blocks(n):
                        last = dve.tensor_copy(split(0), src)
                    last.then_inc(x_hi, 1)
                split_block(0)
                split_block(1)
                for n in range(STEPS):
                    for u in range(4):
                        dve.wait_ge(f_ready, 4 * n + u + 1)
                        if n:
                            dve.wait_ge(spilled[u], 16 * n)
                        dve.tensor_copy(PT[:, u, 0, :], feat(u, n)).then_inc(part1, 1)
                    if n + 2 < STEPS:
                        split_block(n + 2)
                    for u in range(4):
                        dve.wait_ge(rest1, 4 * n + u + 1)
                        dve.tensor_copy(PT[:, u, 1, :], R1[:, u, :]).then_inc(part2, 1)
                        dve.wait_ge(part2, 4 * n + u + 1)
                        dve.tensor_tensor(PT[:, u, 2, :], R1[:, u, :], PT[:, u, 1, :], ALU.subtract).then_inc(part3, 1)
                    if bias:
                        for h in range(2):
                            dve.wait_ge(v_done, 2 * n + h + 1)
                            dve.tensor_tensor(v_tiles(n, h), v_bank(h), part_of(n)[0]["bias_v"][:],
                                              ALU.add).then_inc(v_ready, 1)

            @block.gpsimd
            def _(pool):
                def split_block(n):
                    pool.wait_ge(x_hi, n + 1)
                    for src, split in blocks(n):
                        last = pool.tensor_tensor(split(1), src, split(0), ALU.subtract)
                    last.then_inc(x_lo, 1)
                split_block(0)
                split_block(1)
                for n in range(STEPS):
                    for u in range(4):
                        pool.wait_ge(part1, 4 * n + u + 1)
                        if n:
                            pool.wait_ge(part3, 4 * (n - 1) + u + 1)
                        pool.tensor_tensor(R1[:, u, :], feat(u, n), PT[:, u, 0, :], ALU.subtract).then_inc(rest1, 1)
                    if n + 2 < STEPS:
                        split_block(n + 2)


def attend(nc, G, name, kind, vt, scr_q, scr_k, wo, bo=None, scr_v=None, scr_r=None, by_columns=False, stats=False):
    X, U, ident, ps, masks = G["X"], G["U"], G["ident"], G["psum"], G["mask"]
    softmax, rel, rows = kind != "linear", kind == "rel", kind == "rows"
    K = STACK + SHIFT if softmax else STACK
    RING = 3
    PR = 8
    UNITS = 16
    PER_BANK = 1 if softmax else 2
    ST_BANKS = 2 if softmax else 4
    AT_TURN, AT_DIVIDE, AT_NORMED, AT_SPLIT, AT_OUT = (5, 7, 9, 11, (13, 14)) if softmax else (5, 6, 9, 10, (13, 13))
    TURNS = UNITS // PER_BANK
    with Phase(nc, name) as ph:
        QS = ph.sbuf("q_stack", [P, RING, HEADS, SEQ], BF16)
        KS = ph.sbuf("k_stack", [P, RING, HEADS, SEQ], BF16)
        RL = ph.sbuf("rel_stack", [P, RING, HEADS, SEQ], BF16) if rel else None
        VS = ph.sbuf("v_image", [P, 2, UNITS, 32])
        QK = ph.sbuf("staged", [STACK, 2, HEADS, SEQ], BF16) if rows else None
        VG = ph.sbuf("v_rows", [P, 2, 2, UNITS, DH]) if rows else None
        PB = ph.sbuf("probs", [P, PR, 2, SEQ])
        CR = ph.sbuf("context_raw", [P, 4, SEQ])
        CN = ph.sbuf("context", [P, 2, D])
        CT = ph.sbuf("context_t", [P, 2, KD, SEQ], R32)
        IV = ph.sbuf("inv_sum", [P, 2, HEADS])
        MX = ph.sbuf("maxima", [P, 2, 2, 8])
        MR = ph.sbuf("max_rows", [8, 2, 2, SEQ], BF16)
        WR = ph.sbuf("wo_raw", [P, KD, D])
        WS = ph.sbuf("wo_split", [P, 2, KD, D], R32)
        BO = ph.sbuf("bo", [P, D])
        names = ["w_loaded", "w_hi", "w_lo", "stacked", "v_loaded", "v_copied", "s_done", "s_used", "max_turned",
                 "neg_hi", "max_ready", "max_placed", "st_done", "probs", "pv_done", "cr_ready", "c_turned",
                 "inv_ready", "cn_ready", "cn_turned", "ct_hi", "ct_lo", "out_done", "x_ready", "setup", "biased",
                 "permuted", "stats", "sp_steps"]
        S = {n: ph.sem(n) for n in names}
        n_stack = 2 * len(PAIRS) + (6 if rel else 0)
        per_half = 16 * 2

        def st_bank(u):
            if softmax:
                return ps[:, 2 + u % 2, :].rearrange("p (t q) -> p t q", t=2)
            return ps[:, u // 2 % 4, :].rearrange("p (u t q) -> p u t q", u=2, t=2)

        def s_bank(u):
            return ps[:, u % 2, :].rearrange("p (t k) -> p t k", t=2)

        def cols(stack, r, slot, u, tile, width):
            return stack[0:r, slot, u, tile * P:tile * P + width]

        def index(b, n, k=0):
            return b * n + k

        def load_stack(eng, b, which, with_rel):
            for i, pair in enumerate(PAIRS):
                r = slice(i * DH, (i + 1) * DH)
                for j in which:
                    src = (scr_q, scr_k)[j][pair[j], :, bass.ds(b * SEQ, SEQ)].rearrange("(h c) t -> c h t", c=DH)
                    dst = QK[r, j, :, :] if rows else (QS, KS)[j][r, b % RING, :, :]
                    eng.dma_start(dst, src).then_inc(S["stacked"], 16)
            if with_rel:
                for i in range(6):
                    src = scr_r[i, :, bass.ds(b * SEQ, SEQ)].rearrange("(h c) t -> c h t", c=DH)
                    eng.dma_start(RL[i * DH:(i + 1) * DH, b % RING, :, :], src).then_inc(S["stacked"], 16)

        with nc.Block() as block:
            @block.sync
            def _(sp):
                def hold(sem, value):
                    sp.wait_ge(sem, value)
                    sp.sem_inc(S["sp_steps"], 1)

                def load_v(b):
                    if not (isinstance(b, int) and b == 0):
                        hold(S["v_loaded"], b * 256)
                    for h in range(HEADS):
                        src = scr_v[bass.ds(b * SEQ, SEQ), h * DH:(h + 1) * DH].rearrange("(g s) d -> s g d", s=DH)
                        sp.dma_start(VG[(h % 8) * DH:(h % 8 + 1) * DH, b % 2, h // 8, :, :], src).then_inc(S["v_loaded"], 16)

                def stack(b):
                    hold(S["stacked"], index(b, 16 * n_stack))
                    if rows:
                        hold(S["permuted"], b * 2)
                    load_stack(sp, b, (0, 1), rel)

                def place_max(b, half):
                    hold(S["max_ready"], index(b, 2, half + 1))
                    if not (isinstance(b, int) and b == 0 and half == 0):
                        hold(S["max_placed"], index(b, 2 * per_half, half * per_half))
                    for part in range(2):
                        row = QS[STACK + part:STACK + part + 1, b % RING, half * 8:half * 8 + 8, :]
                        sp.dma_start(row, MR[:, half, part, :]).then_inc(S["max_placed"], 16)

                def step(i, first=False, stacks=True, ahead=True):
                    place_max(i, 1)
                    if stacks:
                        if not (rows or first):
                            hold(S["st_done"], index(i, TURNS))
                        stack(i + 2)
                    if ahead:
                        place_max(i + 1, 0)
                    if rows and stacks:
                        hold(S["v_copied"], index(i, 4, 4))
                        load_v(i + 2)

                load_stack(sp, 0, (0,), rel)
                sp.dma_start(WR[:], wo.rearrange("(k p) n -> p k n", p=P)).then_inc(S["w_loaded"], 16)
                if bo is not None:
                    sp.dma_start(BO[:], bo.partition_broadcast(P)).then_inc(S["w_loaded"], 16)
                if rows:
                    load_v(0)
                stack(1)
                if softmax:
                    place_max(0, 0)
                    if rows:
                        load_v(1)
                    step(0, first=True)
                    with sp.Fori(1, IMAGES - 2) as i:
                        step(i)
                    step(IMAGES - 2, stacks=False)
                    step(IMAGES - 1, stacks=False, ahead=False)
                else:
                    stack(2)
                    with sp.Fori(RING, IMAGES) as b:
                        hold(S["st_done"], index(b - RING, TURNS, TURNS))
                        stack(b)

            @block.tensor
            def _(pe):
                def stack_there(b):
                    if rows:
                        pe.wait_ge(S["permuted"], index(b, 2, 2))
                    else:
                        pe.wait_ge(S["stacked"], index(b, 16 * n_stack, 16 * n_stack))

                def scores_for_max(b, slot, u):
                    pe.wait_ge(S["s_used"], index(b, UNITS, u + 1))
                    for t in range(2):
                        last = pe.matmul(s_bank(u)[:, t, :], cols(QS, STACK, slot, u, t, P),
                                         cols(KS, STACK, slot, u, 0, SEQ), start=True, stop=not rel)
                        if rel:
                            last = pe.matmul(s_bank(u)[:, t, :], cols(RL, STACK, slot, u, t, P),
                                             G["where"][0:STACK, :], start=False, stop=True)
                    last.then_inc(S["s_done"], 1)

                def turn_max(b, half):
                    pe.wait_ge(S["s_used"], index(b, UNITS, 8 * half + 8 + 2))
                    pe.wait_ge(S["max_ready"], index(b, 2, half))
                    for t in range(2):
                        last = pe.transpose(ps[0:8, 7, half * SEQ + t * P:half * SEQ + (t + 1) * P],
                                            MX[:, half, t, :], ident[:])
                    last.then_inc(S["max_turned"], 1)

                def scores(b, slot, u):
                    if u % PER_BANK == 0:
                        pe.wait_ge(S["probs"], index(b, TURNS, u // PER_BANK + 1))
                    if softmax and u % 8 == 0:
                        pe.wait_ge(S["max_placed"], index(b, 2 * per_half, (u // 8 + 1) * per_half))
                    for t in range(2):
                        if softmax:
                            last = pe.matmul(st_bank(u)[:, t, :], cols(KS, K, slot, u, t, P), cols(QS, K, slot, u, 0, SEQ),
                                             start=True, stop=not rel)
                            if rel:
                                last = pe.matmul(st_bank(u)[:, t, :], G["where"][0:STACK, t * P:(t + 1) * P],
                                                 cols(RL, STACK, slot, u, 0, SEQ), start=False, stop=True)
                        else:
                            last = pe.matmul(st_bank(u)[:, u % 2, t, :], cols(KS, K, slot, u, t, P), cols(QS, K, slot, u, t, P),
                                             start=True, stop=True)
                    if u % PER_BANK == PER_BANK - 1:
                        last.then_inc(S["st_done"], 1)

                def values(b, quad, k):
                    if not rows and k % 2 == 0 or not softmax and k != 3:
                        return
                    if k == (0 if rows else 1 if softmax else 3):
                        if quad % 2 == 0:
                            pe.wait_ge(S["cr_ready"], index(b, 2, quad // 2 + 1))
                        pe.wait_ge(S["v_copied"], index(b, 4, quad + 1))
                    n = k + 1 if rows else 4
                    pe.wait_ge(S["probs"], index(b, TURNS, (4 * quad + n) // PER_BANK + ST_BANKS))
                    bank = ps[:, 4, :]
                    for t in (k // 2,) if softmax and not rows else range(2):
                        for j in range(4):
                            u = 4 * quad + (k if rows else j)
                            col = slice(32 * j, 32 * j + 32)
                            if rows:
                                pv = PB[:, u % PR, t, :].rearrange("p (a j s) -> p j a s", j=4, s=DH)[:, j]
                                out = bank[col, (u % 8) * 64:(u % 8) * 64 + 64]
                                last = pe.matmul(out, VS[:, t, u, :], pv, start=t == 0, stop=t == 1)
                            elif softmax:
                                out = bank[col, (quad % 2) * SEQ:(quad % 2 + 1) * SEQ]
                                last = pe.matmul(out, VS[:, t, u, :], PB[:, u % PR, t, :], start=t == 0, stop=t == 1)
                            else:
                                out = bank[col, (quad % 2) * SEQ + t * P:(quad % 2) * SEQ + (t + 1) * P]
                                last = pe.matmul(out, VS[:, t, u, :], PB[:, u % PR, t, 0:P], start=True, stop=True)
                    if k == 3:
                        last.then_inc(S["pv_done"], 1)

                def turn_context(b, t):
                    if t == 0:
                        pe.wait_ge(S["cr_ready"], index(b, 2, 2 + 1))
                        pe.wait_ge(S["ct_lo"], index(b, 1, 1))
                    else:
                        pe.wait_ge(S["x_ready"], index(b, 1, 1))
                    for a in range(4):
                        last = pe.transpose(ps[:, 5 + t, a * P:(a + 1) * P], CR[:, a, t * P:(t + 1) * P], ident[:])
                    last.then_inc(S["c_turned"], 1)

                def turn_normed(b):
                    pe.wait_ge(S["cn_ready"], index(b, 2, 2))
                    out = ps[:, 5, :].rearrange("p (k t) -> p k t", k=KD)
                    for t in range(2):
                        for k in range(KD):
                            last = pe.transpose(out[:, k, t * P:(t + 1) * P], CN[:, t, k * P:(k + 1) * P], ident[:])
                    last.then_inc(S["cn_turned"], 1)

                def project_out(b, t):
                    if t == 0:
                        pe.wait_ge(S["ct_hi"], b + 1)
                        pe.wait_ge(S["ct_lo"], b + 1 + 1)
                    last = split_matmuls(pe, ps[:, 6, t * D:(t + 1) * D],
                                         lambda a, k: CT[:, a, k, t * P:(t + 1) * P],
                                         lambda a, k: WS[:, a, k, :], KD)
                    if t == 1:
                        last.then_inc(S["out_done"], 1)

                def step(i, slot, first=False, ahead=True):
                    for u in range(UNITS):
                        if softmax and ahead:
                            if u == 0:
                                stack_there(i + 1)
                            scores_for_max(i + 1, (slot + 1) % RING, u)
                        elif u == 0:
                            stack_there(i)
                        scores(i, slot, u)
                        if u >= 4:
                            values(i, u // 4 - 1, u % 4)
                        elif not first:
                            values(i - 1, 3, u)
                        if softmax and u == 1:
                            turn_max(i, 1)
                        if softmax and ahead and u == 9:
                            turn_max(i + 1, 0)
                        if not first and u in (AT_TURN, AT_TURN + 1):
                            turn_context(i - 1, u - AT_TURN)
                        if not first and u == AT_NORMED:
                            turn_normed(i - 1)
                        for t in range(2):
                            if not first and u == AT_OUT[t]:
                                project_out(i - 1, t)

                stack_there(0)
                if softmax:
                    for u in range(UNITS):
                        scores_for_max(0, 0, u)
                        if u == 9:
                            turn_max(0, 0)
                pe.wait_ge(S["setup"], RING + 2 if softmax else 2)
                step(0, 0, first=True)
                pe.wait_ge(S["w_lo"], 1)
                with pe.Fori(0, (IMAGES - 2) // RING) as turn:
                    for j in range(1, 1 + RING):
                        step(turn * RING + j, j % RING)
                last = IMAGES - 1
                step(last, last % RING, ahead=False)
                for k in range(4):
                    values(last, 3, k)
                turn_context(last, 0)
                turn_context(last, 1)
                turn_normed(last)
                for t in range(2):
                    project_out(last, t)

            @block.scalar
            def _(act):
                load_stack(act, 0, (1,), False)
                act.sem_inc(S["cr_ready"], 1)

                def copy_context(b, half):
                    act.wait_ge(S["pv_done"], index(b, 4, 2 * half + 2))
                    if half == 0:
                        act.wait_ge(S["c_turned"], index(b, 2, 1))
                    bank = ps[:, 4, :]
                    if rows:
                        src = bank.rearrange("p (g a s) -> p a g s", a=4, s=DH)
                        dst = CR[:, :, half * P:(half + 1) * P].rearrange("p a (g s) -> p a g s", s=DH)
                        act.activation(dst, src, ACT.Copy).then_inc(S["cr_ready"], 1)
                    elif by_columns:
                        for a in range(2):
                            src = bank[:, a * SEQ:(a + 1) * SEQ].rearrange("p (x y) -> p x y", y=SIDE)
                            dst = CR[:, 2 * half + a, :].rearrange("p (y x) -> p x y", x=SIDE)
                            last = act.activation(dst, src, ACT.Copy)
                        last.then_inc(S["cr_ready"], 1)
                    else:
                        act.activation(CR[:, 2 * half:2 * half + 2, :], bank.rearrange("p (a q) -> p a q", a=2),
                                       ACT.Copy).then_inc(S["cr_ready"], 1)

                def split_context(b):
                    act.wait_ge(S["cn_turned"], b + 1)
                    act.wait_ge(S["out_done"], b + 1)
                    act.activation(CT[:, 0], ps[:, 5, :].rearrange("p (k t) -> p k t", k=KD), ACT.Copy).then_inc(S["ct_hi"], 1)

                def step(i, first=False):
                    for u in range(UNITS):
                        if not first and u == 4:
                            copy_context(i - 1, 1)
                        if u == 12:
                            copy_context(i, 0)
                        if not first and u == AT_SPLIT + 1:
                            split_context(i - 1)
                        if softmax:
                            act.wait_ge(S["st_done"], index(i, UNITS, u + 1))
                            if not (first and u < PR) and u % 4 == 0:
                                act.wait_ge(S["pv_done"], index(i, 4, u // 4 - 1))
                            act.activation(PB[:, u % PR], st_bank(u), ACT.Exp, scale=0.25).then_inc(S["probs"], 1)

                if softmax:
                    act.sem_inc(S["probs"], ST_BANKS)
                step(0, first=True)
                with act.Fori(1, IMAGES) as i:
                    step(i)
                copy_context(IMAGES - 1, 1)
                split_context(IMAGES - 1)

            @block.vector
            def _(dve):
                dve.sem_inc(S["s_used"], 2)
                dve.sem_inc(S["ct_lo"], 1)
                dve.sem_inc(S["x_ready"], 1)
                dve.sem_inc(S["c_turned"], 1)
                dve.sem_inc(S["out_done"], 1)
                if not softmax:
                    dve.sem_inc(S["probs"], ST_BANKS)

                def split_weights():
                    dve.wait_ge(S["w_loaded"], 16 * (1 + (bo is not None)))
                    dve.tensor_copy(WS[:, 0], WR[:]).then_inc(S["w_hi"], 1)
                    dve.wait_ge(S["w_hi"], 1)
                    dve.tensor_tensor(WS[:, 1], WR[:], WS[:, 0], ALU.subtract).then_inc(S["w_lo"], 1)

                def permute(b, j):
                    dve.wait_ge(S["stacked"], index(b, 16 * n_stack, 16 * n_stack))
                    words = [t.bitcast(mybir.dt.int32) for t in ((QS, KS)[j][0:STACK, b % RING], QK[:, j])]
                    dve.tensor_copy(words[0].rearrange("p g (h s) -> p g h s", s=DH // 2),
                                    words[1].rearrange("p h (g s) -> p g h s", s=DH // 2)).then_inc(S["permuted"], 1)

                def maxima(b, u):
                    dve.wait_ge(S["s_done"], index(b, UNITS, u + 1))
                    dve.tensor_reduce(MX[:, u // 8, :, u % 8], s_bank(u), AX.X, ALU.max).then_inc(S["s_used"], 1)

                def split_max(b, half, first=False):
                    dve.wait_ge(S["max_turned"], index(b, 2, half + 1))
                    if not first:
                        dve.wait_ge(S["max_placed"], index(b, 2 * per_half, (half - 1) * per_half))
                    bank = ps[0:8, 7, half * SEQ:(half + 1) * SEQ]
                    dve.tensor_scalar(MR[:, half, 0, :], bank, -1.0, None, ALU.mult).then_inc(S["neg_hi"], 1)
                    dve.wait_ge(S["neg_hi"], index(b, 2, half + 1))
                    dve.scalar_tensor_tensor(MR[:, half, 1, :], bank, -1.0, MR[:, half, 0, :], ALU.mult,
                                             ALU.subtract).then_inc(S["max_ready"], 1)

                def mask(b, u):
                    dve.wait_ge(S["st_done"], index(b, TURNS, u // 2 + 1))
                    dve.tensor_tensor(PB[:, u % PR:u % PR + 2, :, 0:P], st_bank(u),
                                      masks[:].unsqueeze(1).to_broadcast([P, 2, 2, P]), ALU.mult).then_inc(S["probs"], 1)

                def normalise_context(b, t):
                    dve.wait_ge(S["c_turned"], index(b, 2, t + 2))
                    src = ps[:, 5 + t, :].rearrange("p (h e) -> p h e", e=32)
                    dst = CN[:, t, :].rearrange("p (h e) -> p h e", e=DH)
                    if softmax:
                        dve.reciprocal(IV[:, t, :], src[:, :, DH]).then_inc(S["inv_ready"], 1)
                        dve.wait_ge(S["inv_ready"], index(b, 2, t + 1))
                        dve.tensor_tensor(dst, src[:, :, 0:DH], IV[:, t, :].unsqueeze(2).to_broadcast([P, HEADS, DH]),
                                          ALU.mult).then_inc(S["cn_ready"], 1)
                    else:
                        dve.tensor_copy(dst, src[:, :, 0:DH]).then_inc(S["cn_ready"], 1)

                def split_context(b):
                    dve.wait_ge(S["ct_hi"], b + 1)
                    dve.tensor_tensor(CT[:, 1], ps[:, 5, :].rearrange("p (k t) -> p k t", k=KD), CT[:, 0],
                                      ALU.subtract).then_inc(S["ct_lo"], 1)

                def add_out(b):
                    dve.wait_ge(S["out_done"], b + 2)
                    dst = (U if rows else X)[:, bass.ds(2 * b, 2), :]
                    dve.tensor_tensor(dst, ps[:, 6, :].rearrange("p (t n) -> p t n", t=2), dst,
                                      ALU.add).then_inc(S["x_ready"], 1)
                    if stats:
                        dve.wait_ge(S["x_ready"], b + 2)
                        for t in range(2):
                            row = G["stats"][:, bass.ds(2 * b + t, 1), :].rearrange("p o n -> p (o n)")
                            src = (U if rows else X)[:, bass.ds(2 * b + t, 1), :].rearrange("p o n -> p (o n)")
                            dve.bn_stats(row, src).then_inc(S["stats"], 1)

                def step(i, first=False, ahead=True, more=True):
                    for u in range(UNITS):
                        if softmax and ahead:
                            maxima(i + 1, u)
                            if u == 10:
                                split_max(i + 1, 0)
                        if softmax and u == 2:
                            split_max(i, 1, first=first)
                        if not softmax:
                            if not (first and u < PR) and u % 4 == 0:
                                dve.wait_ge(S["pv_done"], index(i, 4, u // 4 - 1))
                            if u % 2 == 0:
                                mask(i, u)
                        if rows and more and u in (11, 13):
                            permute(i + 2, u // 13)
                        if not first and u == AT_DIVIDE:
                            normalise_context(i - 1, 0)
                            normalise_context(i - 1, 1)
                        if not first and u == AT_SPLIT:
                            split_context(i - 1)
                    if not first:
                        add_out(i - 1)

                if rows:
                    permute(0, 0)
                    permute(0, 1)
                if softmax:
                    for u in range(UNITS):
                        maxima(0, u)
                        if u == 10:
                            split_max(0, 0, first=True)
                if rows:
                    permute(1, 0)
                    permute(1, 1)
                split_weights()
                step(0, first=True)
                if bo is not None:
                    dve.wait_ge(S["biased"], 1)
                with dve.Fori(1, IMAGES - 2) as i:
                    step(i)
                step(IMAGES - 2, more=False)
                step(IMAGES - 1, ahead=False, more=False)
                last = IMAGES - 1
                normalise_context(last, 0)
                normalise_context(last, 1)
                split_context(last)
                add_out(last)

            @block.gpsimd
            def _(pool):
                def copy_v(b, quad):
                    dst = VS[:, :, 4 * quad:4 * quad + 4, 0:DH]
                    if rows:
                        if quad == 0:
                            pool.wait_ge(S["v_loaded"], index(b, 256, 256))
                        for t in range(2):
                            last = pool.tensor_copy(dst[:, t], VG[:, b % 2, t, 4 * quad:4 * quad + 4])
                    else:
                        src = vt[:, bass.ds(2 * b, 2), 4 * quad * DH:4 * (quad + 1) * DH]
                        last = pool.tensor_copy(dst, src.rearrange("p t (h e) -> p t h e", e=DH))
                    last.then_inc(S["v_copied"], 1)

                pool.memset(VS[:, :, :, DH:32], 0.0).then_inc(S["setup"], 1)
                pool.wait_ge(S["setup"], 1)
                pool.memset(VS[:, :, :, DH:DH + 1], 1.0).then_inc(S["setup"], 1)
                pool.wait_ge(S["setup"], 2)
                if softmax:
                    for r in range(RING):
                        pool.memset(KS[STACK:STACK + SHIFT, r], 1.0).then_inc(S["setup"], 1)
                        pool.wait_ge(S["setup"], 3 + r)
                for quad in range(4):
                    copy_v(0, quad)
                if bo is not None:
                    pool.wait_ge(S["w_loaded"], 32)
                    for t in range(TILES):
                        dst = (U if rows else X)[:, t, :]
                        last = pool.tensor_tensor(dst, dst, BO[:], ALU.add)
                    last.then_inc(S["biased"], 1)
                with pool.Fori(1, IMAGES) as b:
                    for quad in range(4):
                        pool.wait_ge(S["pv_done"], b * 4 - 3 + quad)
                        copy_v(b, quad)


def relative(nc, G, name, rel_h, rel_w, scr_r):
    QF, ps = G["QF"], G["psum"]
    with Phase(nc, name) as ph:
        T = ph.sbuf("tables", [P, 2, SIDE, P])
        F = ph.sbuf("rel", [P, 2, TOKENS])
        HALF = TOKENS // 2
        SLOTS = 4
        R1 = ph.sbuf("rest", [P, 2, HALF])
        PT = ph.sbuf("parts", [P, SLOTS, 3, HALF], BF16)
        zeroed, done, ready = ph.sem("zeroed"), ph.sem("done"), ph.sem("ready")
        placed = [ph.sem(f"placed{axis}") for axis in range(2)]
        part1, rest1, part2, part3 = (ph.sem(s) for s in ("part1", "rest1", "part2", "part3"))
        spilled = [ph.sem(f"spilled{i}") for i in range(SLOTS)]
        UNITS = [(axis, t) for axis in range(2) for t in range(KD)]
        HALVES = 2 * len(UNITS)

        def rel_half(c):
            return F[:, c // 2 % 2, c % 2 * HALF:(c % 2 + 1) * HALF]

        def queries(t, axis, q):
            x = QF[:, t, :].rearrange("p (b y x) -> p b y x", y=SIDE, x=SIDE)
            return x[:, :, q, :] if axis == 0 else x[:, :, :, q]

        def into(u, axis, g):
            x = F[:, u % 2, :].rearrange("p (b y x) -> p b y x", y=SIDE, x=SIDE)
            if axis == 0:
                return x[:, :, 4 * g:4 * g + 4, :].rearrange("p b q o -> p q b o")
            return x[:, :, :, 4 * g:4 * g + 4].rearrange("p b o q -> p q b o")

        with nc.Block() as block:
            @block.sync
            def _(sp):
                sp.wait_ge(zeroed, 2)
                for axis, table in enumerate((rel_h, rel_w)):
                    for j in range(8):
                        rows = slice(j * DH, (j + 1) * DH)
                        sp.dma_start(T[rows, axis, :, rows], table).then_inc(placed[axis], 16)
                for c in range(HALVES):
                    axis, t = UNITS[c // 2]
                    sp.wait_ge(part3, c + 1)
                    dst = scr_r[3 * axis:3 * axis + 3, t * P:(t + 1) * P, c % 2 * HALF:(c % 2 + 1) * HALF]
                    sp.dma_start(dst.rearrange("a p n -> p a n"), PT[:, c % SLOTS]).then_inc(spilled[c % SLOTS], 16)
                for s in spilled:
                    sp.wait_ge(s, 16 * HALVES // SLOTS)

            @block.tensor
            def _(pe):
                for u, (axis, t) in enumerate(UNITS):
                    pe.wait_ge(placed[axis], 16 * 8)
                    for g in range(4):
                        bank = 4 * (u % 2) + g
                        if u >= 2:
                            pe.wait_ge(ready, 4 * (u - 2) + g + 1)
                        for q in range(4 * g, 4 * g + 4):
                            out = ps[:, bank, (q % 4) * P:(q % 4 + 1) * P]
                            last = pe.matmul(out, T[:, axis, q, :], queries(t, axis, q), start=True, stop=True)
                        last.then_inc(done, 1)

            @block.scalar
            def _(act):
                for u, (axis, t) in enumerate(UNITS):
                    if u >= 2:
                        act.wait_ge(rest1, 2 * (u - 1))
                    for g in range(4):
                        act.wait_ge(done, 4 * u + g + 1)
                        src = ps[:, 4 * (u % 2) + g, :].rearrange("p (q b o) -> p q b o", b=IMAGES, o=SIDE)
                        for q in range(4):
                            last = act.activation(into(u, axis, g)[:, q], src[:, q], ACT.Copy, scale=4.0)
                        last.then_inc(ready, 1)

            @block.vector
            def _(dve):
                dve.memset(T[:, 0].rearrange("p q m -> p (q m)"), 0.0).then_inc(zeroed, 1)

                def finish(c):
                    dve.wait_ge(rest1, c + 1)
                    dve.tensor_copy(PT[:, c % SLOTS, 1], R1[:, c % 2]).then_inc(part2, 1)
                    dve.wait_ge(part2, c + 1)
                    dve.tensor_tensor(PT[:, c % SLOTS, 2], R1[:, c % 2], PT[:, c % SLOTS, 1],
                                      ALU.subtract).then_inc(part3, 1)
                for c in range(HALVES):
                    dve.wait_ge(ready, 4 * (c // 2) + 4)
                    if c >= SLOTS:
                        dve.wait_ge(spilled[c % SLOTS], 16 * (c // SLOTS))
                    dve.tensor_copy(PT[:, c % SLOTS, 0], rel_half(c)).then_inc(part1, 1)
                    if c:
                        finish(c - 1)
                finish(HALVES - 1)

            @block.gpsimd
            def _(pool):
                pool.memset(T[:, 1].rearrange("p q m -> p (q m)"), 0.0).then_inc(zeroed, 1)
                for c in range(HALVES):
                    pool.wait_ge(part1, c + 1)
                    if c >= 2:
                        pool.wait_ge(part3, c - 1)
                    pool.tensor_tensor(R1[:, c % 2], rel_half(c), PT[:, c % SLOTS, 0], ALU.subtract).then_inc(rest1, 1)


def route(nc, G, name, wg, bias, n_exp, top, first_col, softmax, scr_g=None):
    RT, GW, ident, ps = G["RT"], G["GW"], G["ident"], G["psum"]
    WR, WS, XS = G["w_raw"], G["w_split"], G["x_split"]
    with Phase(nc, name) as ph:
        WG = ph.sbuf("wg", [P, KD, n_exp])
        BG = ph.sbuf("bias", [P, n_exp])
        LT = ph.sbuf("logits_t", [n_exp, TOKENS])
        L = ph.sbuf("logits", [P, TILES, n_exp])
        CMP = ph.sbuf("compared", [P, TILES, n_exp, n_exp])
        EQ = ph.sbuf("equal", [P, TILES, n_exp, n_exp])
        RK = ph.sbuf("rank", [P, TILES, n_exp])
        MK = ph.sbuf("mask", [P, TILES, n_exp])
        MX = ph.sbuf("max", [P, TILES])
        EX = ph.sbuf("exp", [P, TILES, n_exp])
        loaded, done, ready, turned, chain, shifted, exped = (
            ph.sem(s) for s in ("loaded", "done", "ready", "turned", "chain", "shifted", "exped"))
        w_lo, x_hi, x_lo = (ph.sem(s) for s in ("w_lo", "x_hi", "x_lo"))
        gates_made, gates_turned, gates_ready, spilled = (
            ph.sem(s) for s in ("gates_made", "gates_turned", "gates_ready", "spilled"))
        cols = first_col + n_exp
        GT = ph.sbuf("gates_t", [cols, TOKENS]) if scr_g is not None else None
        full = [P, TILES, n_exp, n_exp]
        with nc.Block() as block:
            @block.sync
            def _(sp):
                sp.dma_start(WG[:], wg).then_inc(loaded, 16)
                if bias is not None:
                    sp.dma_start(BG[:], bias.partition_broadcast(P)).then_inc(loaded, 16)
                if scr_g is not None:
                    sp.wait_ge(gates_ready, BLOCKS)
                    sp.dma_start(scr_g, GT[:]).then_inc(spilled, 16)
                    sp.wait_ge(spilled, 16)

            @block.tensor
            def _(pe):
                pe.wait_ge(loaded, 16 * (1 + (bias is not None)))
                for n in range(BLOCKS):
                    for k in range(KD):
                        last = pe.matmul(ps[0:n_exp, n, :], WG[:, k, :], RT[:, k, n * BLOCK:(n + 1) * BLOCK],
                                         start=k == 0, stop=k == KD - 1)
                    last.then_inc(done, 1)
                pe.wait_ge(ready, BLOCKS)
                for t in range(TILES):
                    last = pe.transpose(ps[:, 4, t * n_exp:(t + 1) * n_exp], LT[:, t * P:(t + 1) * P],
                                        ident[0:n_exp, 0:n_exp])
                last.then_inc(turned, 1)
                if scr_g is not None:
                    pe.wait_ge(gates_made, 1)
                    for t in range(TILES):
                        n, j = divmod(t, BLOCK // P)
                        last = pe.transpose(ps[0:cols, n, j * P:(j + 1) * P], GW[:, t, :], ident[:])
                        if j == BLOCK // P - 1:
                            last.then_inc(gates_turned, 1)

            @block.scalar
            def _(act):
                for n in range(BLOCKS):
                    act.wait_ge(done, n + 1)
                    act.activation(LT[:, n * BLOCK:(n + 1) * BLOCK], ps[0:n_exp, n, :], ACT.Copy).then_inc(ready, 1)
                if softmax:
                    act.wait_ge(shifted, 1)
                    act.activation(EX[:], EX[:], ACT.Exp).then_inc(exped, 1)
                if scr_g is not None:
                    for n in range(BLOCKS):
                        act.wait_ge(gates_turned, n + 1)
                        act.activation(GT[:, n * BLOCK:(n + 1) * BLOCK], ps[0:cols, n, :], ACT.Copy).then_inc(gates_ready, 1)

            @block.vector
            def _(dve):
                link = Chain(dve, chain)
                dve.tensor_copy(XS[:, 0], RT[:]).then_inc(x_hi, 1)
                dve.wait_ge(x_hi, 1)
                dve.tensor_tensor(XS[:, 1], RT[:], XS[:, 0], ALU.subtract).then_inc(x_lo, 1)
                dve.wait_ge(turned, 1)
                link(dve.tensor_copy(L[:], ps[:, 4, 0:TILES * n_exp].rearrange("p (t e) -> p t e", e=n_exp)))
                if bias is not None:
                    link(dve.tensor_tensor(L[:], L[:], BG[:].unsqueeze(1).to_broadcast([P, TILES, n_exp]), ALU.add))
                own, other = L[:].unsqueeze(3).to_broadcast(full), L[:].unsqueeze(2).to_broadcast(full)
                dve.tensor_tensor(CMP[:], other, own, ALU.is_gt).then_inc(chain, 1)
                dve.tensor_tensor(EQ[:], other, own, ALU.is_equal).then_inc(chain, 1)
                link.n += 2
                dve.wait_ge(chain, link.n)
                before = G["before"][:, 0:n_exp, 0:n_exp].unsqueeze(1).to_broadcast(full)
                link(dve.tensor_tensor(EQ[:], EQ[:], before, ALU.mult))
                link(dve.tensor_tensor(CMP[:], CMP[:], EQ[:], ALU.add))
                link(dve.tensor_reduce(RK[:], CMP[:], AX.X, ALU.add))
                link(dve.tensor_scalar(MK[:], RK[:], float(top) - 0.5, None, ALU.is_lt))
                if first_col:
                    link(dve.memset(GW[:, :, 0:first_col], 1.0))
                dst = GW[:, :, first_col:first_col + n_exp]
                if not softmax:
                    link(dve.tensor_copy(dst, MK[:]))
                    return
                link(dve.tensor_reduce(MX[:], L[:], AX.X, ALU.max))
                dve.tensor_tensor(EX[:], L[:], MX[:].unsqueeze(2).to_broadcast([P, TILES, n_exp]),
                                  ALU.subtract).then_inc(shifted, 1)
                dve.wait_ge(exped, 1)
                link(dve.tensor_tensor(EX[:], EX[:], MK[:], ALU.mult))
                link(dve.tensor_reduce(MX[:], EX[:], AX.X, ALU.add))
                link(dve.reciprocal(MX[:], MX[:]))
                link(dve.tensor_tensor(dst, EX[:], MX[:].unsqueeze(2).to_broadcast([P, TILES, n_exp]), ALU.mult))
                dve.sem_inc(gates_made, 1)

            @block.gpsimd
            def _(pool):
                pool.tensor_tensor(WS[:, 0, 1], WR[:], WS[:, 0, 0], ALU.subtract).then_inc(w_lo, 1)


def experts(nc, G, name, w, n_exp, n_h, n_rest=0, rest=0, scr_g=None, stats=False):
    X, U, RT, GW, ps = G["X"], G["U"], G["RT"], G["GW"], G["psum"]
    WR, WS, XS = G["w_raw"], G["w_split"], G["x_split"]
    W1, W3 = KD * n_h * P, n_h * D
    WN = 2 * W1 + W3
    PARTS = BLOCKS - 1
    PART = WN // PARTS
    LAG = 2
    TT = BLOCK // P
    total = n_exp + (n_rest > 0)
    last_expert = total - 1

    def gates_of(m):
        return RT[:, m, :] if m < KD else U[:].rearrange("p t n -> p (t n)")[:, (m - KD) * TOKENS:(m - KD + 1) * TOKENS]

    def is_last(e):
        return isinstance(e, int) and e == last_expert

    def tiles(e):
        return n_rest if n_rest and is_last(e) else n_h

    def tile(e, n, m):
        return e * (BLOCKS * n_h) + n * tiles(e) + m

    def slot(e, n, m):
        return (n * tiles(e) + m) % 2

    def over_experts(eng, body):
        body(0, 0)
        pairs = (total - 2) // 2
        with eng.Fori(0, pairs) as i:
            body(2 * i + 1, 1)
            body(2 * i + 2, 0)
        for e in range(2 * pairs + 1, total):
            body(e, e % 2)

    with Phase(nc, name) as ph:
        SL = ph.sbuf("silu", [P, 2, BLOCK])
        GF = ph.sbuf("hidden", [P, 2, BLOCK])
        GS = ph.sbuf("hidden_split", [P, 2, 2, BLOCK], R32)
        names = ["loaded", "w_hi", "w_split", "up_done", "silu", "hidden", "g_hi", "g_lo", "used", "added",
                 "gates_loaded", "gated", "stats", "sp_steps"]
        S = {n: ph.sem(n) for n in names}

        def up(r, a, k, m, which):
            o = which * W1 + k * n_h * P + m * P
            return WS[:, r, a, o:o + P]

        def down(r, a, m):
            o = 2 * W1 + m * D
            return WS[:, r, a, o:o + D]

        with nc.Block() as block:
            @block.sync
            def _(sp):
                sp.dma_start(WR[:], w[1]).then_inc(S["loaded"], 16)
                if n_rest:
                    per_tile = P // rest
                    for e in range(n_exp):
                        m, j = divmod(e, per_tile)
                        end = P if j == per_tile - 1 or e == n_exp - 1 else (j + 1) * rest
                        row = scr_g[e:e + 1, :].rearrange("o n -> (o n)").partition_broadcast(end - j * rest)
                        sp.dma_start(gates_of(m)[j * rest:end], row).then_inc(S["gates_loaded"], 16)
                with sp.Fori(2, total) as e:
                    sp.wait_ge(S["w_split"], PARTS * e - PARTS)
                    sp.sem_inc(S["sp_steps"], 1)
                    sp.dma_start(WR[:], w[bass.ds(e, 1)].rearrange("o p n -> (o p) n")).then_inc(S["loaded"], 16)

            @block.tensor
            def _(pe):
                def make_hidden(e, r, n, m):
                    s = slot(e, n, m)
                    pe.wait_ge(S["hidden"], tile(e, n, m) + 1)
                    for which in range(2):
                        last = split_matmuls(pe, ps[:, 2 * s + which, :], lambda a, k: up(r, a, k, m, which),
                                             lambda a, k: XS[:, a, k, n * BLOCK:(n + 1) * BLOCK], KD)
                    last.then_inc(S["up_done"], 1)

                def use_hidden(e, r, n, m):
                    s = slot(e, n, m)
                    pe.wait_ge(S["g_lo"], tile(e, n, m) + 1)
                    for t in range(TT):
                        if m == 0:
                            pe.wait_ge(S["added"], (e * BLOCKS + n) * TT + t + 1)
                        for i, (a, b) in enumerate(((0, 0), (0, 1), (1, 0))):
                            last = pe.matmul(ps[:, 4 + t, 0:D], GS[:, a, s, t * P:(t + 1) * P], down(r, b, m),
                                             start=m == 0 and i == 0, stop=m == tiles(e) - 1 and i == 2)
                        last.then_inc(S["used"], 1)

                def steps(e, r, n, before):
                    for m in range(tiles(e)):
                        make_hidden(e, r, n, m)
                        if m >= LAG:
                            use_hidden(e, r, n, m - LAG)
                        elif before:
                            use_hidden(*before, tiles(before[0]) - LAG + m)

                def expert(e, r):
                    first = isinstance(e, int) and e == 0
                    if not first:
                        pe.wait_ge(S["w_split"], PARTS * e)
                    steps(e, r, 0, None if first else (e - 1, 1 - r, BLOCKS - 1))
                    for n in range(1, BLOCKS):
                        steps(e, r, n, (e, r, n - 1))
                over_experts(pe, expert)
                for m in range(tiles(last_expert) - LAG, tiles(last_expert)):
                    use_hidden(last_expert, last_expert % 2, BLOCKS - 1, m)

            @block.scalar
            def _(act):
                def steps(e, r, n, splits):
                    for m in range(tiles(e)):
                        s = slot(e, n, m)
                        act.wait_ge(S["up_done"], tile(e, n, m) + 1)
                        act.wait_ge(S["hidden"], tile(e, n, m) + 1)
                        act.activation(SL[:, s], ps[:, 2 * s, :], ACT.Silu).then_inc(S["silu"], 1)
                        if m == LAG - 1 and splits:
                            if not (isinstance(e, int) and e == 0):
                                act.wait_ge(S["used"], e * (BLOCKS * n_h * TT))
                            act.wait_ge(S["loaded"], e * 16 + 16)
                            q = slice(n * PART, (n + 1) * PART)
                            act.activation(WS[:, 1 - r, 0, q], WR[:, q], ACT.Copy).then_inc(S["w_hi"], 1)

                def expert(e, r):
                    for n in range(BLOCKS):
                        steps(e, r, n, n < PARTS and not is_last(e))
                over_experts(act, expert)

            @block.vector
            def _(dve):
                dve.sem_inc(S["hidden"], 2)
                dve.sem_inc(S["added"], TT)

                def add_out(e, n):
                    column = 0 if n_rest and is_last(e) else e
                    for t in range(TT):
                        dve.wait_ge(S["used"], (tile(e, n, tiles(e) - 1)) * TT + t + 1)
                        x, gate = X[:, n * TT + t, :], GW[:, n * TT + t, bass.ds(column, 1)]
                        dve.scalar_tensor_tensor(x, ps[:, 4 + t, 0:D], gate, x, ALU.mult, ALU.add).then_inc(S["added"], 1)
                    for t in range(TT) if stats and is_last(e) else ():
                        dve.wait_ge(S["added"], (e * BLOCKS + n) * TT + t + 1 + TT)
                        dve.bn_stats(G["stats"][:, n * TT + t, :], X[:, n * TT + t, :]).then_inc(S["stats"], 1)

                def steps(e, n, before):
                    first = before is None
                    for m in range(tiles(e)):
                        c, s = tile(e, n, m), slot(e, n, m)
                        dve.wait_ge(S["silu"], c + 1)
                        if not first or m >= 2:
                            dve.wait_ge(S["g_lo"], c - 1)
                        if n_rest and is_last(e):
                            silu = SL[:, s]
                            if n == 0 and m == 0:
                                dve.wait_ge(S["gates_loaded"], 16 * n_exp)
                            dve.tensor_tensor(silu, silu, gates_of(m)[:, n * BLOCK:(n + 1) * BLOCK],
                                              ALU.mult).then_inc(S["gated"], 1)
                            dve.wait_ge(S["gated"], n * n_rest + m + 1)
                        dve.tensor_tensor(GF[:, s], ps[:, 2 * s + 1, :], SL[:, s], ALU.mult).then_inc(S["hidden"], 1)
                        if not first or m >= 2:
                            dve.wait_ge(S["used"], (c - 1) * TT)
                        dve.wait_ge(S["hidden"], c + 3)
                        dve.tensor_copy(GS[:, 0, s], GF[:, s]).then_inc(S["g_hi"], 1)
                        if m == LAG - 1 and not first:
                            add_out(*before)

                def expert(e, r):
                    steps(e, 0, None if isinstance(e, int) and e == 0 else (e - 1, BLOCKS - 1))
                    for n in range(1, BLOCKS):
                        steps(e, n, (e, n - 1))
                over_experts(dve, expert)
                add_out(last_expert, BLOCKS - 1)

            @block.gpsimd
            def _(pool):
                def steps(e, r, n, splits):
                    for m in range(tiles(e)):
                        s = slot(e, n, m)
                        pool.wait_ge(S["g_hi"], tile(e, n, m) + 1)
                        pool.tensor_tensor(GS[:, 1, s], GF[:, s], GS[:, 0, s], ALU.subtract).then_inc(S["g_lo"], 1)
                        if m == LAG - 1 and splits:
                            pool.wait_ge(S["w_hi"], e * PARTS + n + 1)
                            q = slice(n * PART, (n + 1) * PART)
                            pool.tensor_tensor(WS[:, 1 - r, 1, q], WR[:, q], WS[:, 1 - r, 0, q],
                                               ALU.subtract).then_inc(S["w_split"], 1)

                def expert(e, r):
                    for n in range(BLOCKS):
                        steps(e, r, n, n < PARTS and not is_last(e))
                over_experts(pool, expert)


def program(nc, A, out):
    scr = {n: nc.dram_tensor(f"scr_{n}", [3, D, TOKENS], BF16, kind="Internal").ap() for n in ("q0", "k0", "q1", "k1")}
    scr["r"] = nc.dram_tensor("scr_r", [6, D, TOKENS], BF16, kind="Internal").ap()
    scr["g"] = nc.dram_tensor("scr_g", [9, TOKENS], F32, kind="Internal").ap()
    scr["v"] = nc.dram_tensor("scr_v", [TOKENS, D], F32, kind="Internal").ap()
    with ExitStack() as ctx:
        def sb(name, shape, dt=F32):
            return ctx.enter_context(nc.sbuf_tensor(name, shape, dt))
        G = {"X": sb("x_tokens", [P, TILES, D]), "U": sb("u_tokens", [P, TILES, D]), "ident": sb("ident", [P, P]),
             "group_avg": sb("group_avg", [P, P]), "mask": sb("mask", [P, 2, P]),
             "stats": sb("stats", [P, TILES, 6]), "where": sb("where", [STACK, SEQ], BF16), "before": sb("before", [P, 8, 8])}
        G["psum"] = ctx.enter_context(nc.psum_tensor("psum", [P, 8, 512], F32))
        X = G["X"]

        with Phase(nc, "load") as ph:
            where32 = ph.sbuf("where32", [STACK, SEQ])
            loaded, cast = ph.sem("loaded"), ph.sem("cast")
            with nc.Block() as block:
                @block.sync
                def _(sp):
                    sp.dma_start(X[:], A["x"].rearrange("b (t y) x c -> (y x) (b t) c", t=2)).then_inc(loaded, 16)
                    sp.dma_start(G["ident"][:], A["c_ident"]).then_inc(loaded, 16)
                    sp.dma_start(G["group_avg"][:], A["c_group"]).then_inc(loaded, 16)
                    sp.dma_start(G["mask"][:], A["c_mask"]).then_inc(loaded, 16)
                    sp.dma_start(where32[:], A["c_where"]).then_inc(loaded, 16)
                    sp.dma_start(G["before"][:], A["c_before"]).then_inc(loaded, 16)

                @block.vector
                def _(dve):
                    dve.wait_ge(loaded, 96)
                    dve.tensor_copy(G["where"][:], where32[:]).then_inc(cast, 1)

        vs = ExitStack()
        def values_tensor(name):
            vs.close()
            G["v0"] = vs.enter_context(nc.sbuf_tensor(name, [P, TILES, D], F32)) if name else None

        def attention_inputs():
            part = ExitStack()
            for n in ("RT", "QF", "KF"):
                G[n] = part.enter_context(nc.sbuf_tensor(f"{n}_{nc.next_id()}", [P, KD, TOKENS], F32))
            return part

        def projection(part, name, wqkv, bias=None):
            def sb(n, shape, dt=F32):
                return part.enter_context(nc.sbuf_tensor(f"{name}_{n}", shape, dt))
            raw, W, loads, col = sb("w_raw", [P, KD, 3 * D]), {"split": sb("w_split", [P, 2, KD, 3 * D], R32)}, [], 0
            for w in wqkv:
                loads.append((raw[:, :, col:col + w.shape[1]], w.rearrange("(k p) n -> p k n", p=P)))
                col += w.shape[1]
            if bias:
                W["bias_qk"], W["bias_v"] = sb("bias_qk", [P, 4]), sb("bias_v", [P, 2, D])
                loads += [(W["bias_qk"][:, 2 * i:2 * i + 2], b.rearrange("(u p) -> p u", p=P)) for i, b in enumerate(bias[:2])]
                loads += [(W["bias_v"][:, i, :], bias[2].partition_broadcast(P)) for i in range(2)]
            return W, loads, [(raw, W["split"])]

        values_tensor("v0")
        with attention_inputs() as part:
            W0, loads0, splits0 = projection(part, "p0", [A["L0_conv_w_qkv0"]])
            W1, loads1, splits1 = projection(part, "p1", [A["L0_conv_w_qkv1"]])
            normalise(nc, G, "n0", "group", loads0 + loads1, splits0 + splits1)
            project(nc, G, "p0", [(W0, True, G["v0"], scr["q0"], scr["k0"]), (W1, False, G["U"], scr["q1"], scr["k1"])])
        attend(nc, G, "a0", "linear", G["v0"], scr["q0"], scr["k0"], A["L0_conv_w_out0"], by_columns=True)
        attend(nc, G, "a1", "linear", G["U"], scr["q1"], scr["k1"], A["L0_conv_w_out1"])

        with attention_inputs() as part:
            b = A["L1_conv_qkv_b"]
            W, loads, splits = projection(part, "p2", [A["L1_conv_qkv_w"]], (b[0:D], b[D:2 * D], b[2 * D:3 * D]))
            normalise(nc, G, "n2", "group", loads, splits)
            project(nc, G, "p2", [(W, False, G["v0"], scr["q0"], scr["k0"])])
            relative(nc, G, "r2", A["rel_h"], A["rel_w"], scr["r"])
        attend(nc, G, "a2", "rel", G["v0"], scr["q0"], scr["k0"], A["L1_conv_proj_w"], A["L1_conv_proj_b"], scr_r=scr["r"],
               stats=True)

        with attention_inputs() as part:
            W, loads, splits = projection(part, "p3", [A["L2_attn_wq"], A["L2_attn_wk"], A["L2_attn_wv"]],
                                          (A["L2_attn_bq"], A["L2_attn_bk"], A["L2_attn_bv"]))
            normalise(nc, G, "n3", "layer", loads, splits, stats_there=True)
            project(nc, G, "p3", [(W, False, G["v0"], scr["q0"], scr["k0"])], scr["v"])
        attend(nc, G, "a3", "rows", G["v0"], scr["q0"], scr["k0"], A["L2_attn_wo"], A["L2_attn_bo"], scr_v=scr["v"])
        affine_norm(nc, G, "f3", A["L2_attn_gamma"], A["L2_attn_beta"])

        values_tensor(None)

        def feed_forward(n, wg, bias, n_exp, top, first_col, softmax, w, hidden, stats):
            n_h, rest = divmod(hidden, P)
            cols = first_col + n_exp
            n_rest = -(-cols // (P // rest)) if rest else 0
            scr_g = scr["g"] if rest else None
            with ExitStack() as part:
                G["GW"] = part.enter_context(nc.sbuf_tensor(f"gates{n}", [P, TILES, first_col + n_exp], F32))
                G["RT"] = part.enter_context(nc.sbuf_tensor(f"x_norm{n}", [P, KD, TOKENS], F32))
                G["x_split"] = part.enter_context(nc.sbuf_tensor(f"x_split{n}", [P, 2, KD, TOKENS], R32))
                G["w_raw"] = part.enter_context(nc.sbuf_tensor(f"w_raw{n}", [P, w.shape[2]], F32))
                G["w_split"] = part.enter_context(nc.sbuf_tensor(f"w_split{n}", [P, 2, 2, w.shape[2]], R32))
                normalise(nc, G, f"n{n}", "layer", [(G["w_raw"][:], w[0])], [(G["w_raw"], G["w_split"][:, 0])],
                          rests=False)
                route(nc, G, f"g{n}", wg, bias, n_exp, top, first_col, softmax, scr_g)
                experts(nc, G, f"e{n}", w, cols, n_h, n_rest, rest, scr_g, stats=stats)
        feed_forward(4, A["L2_ffn_Wg"], None, 8, 1, 0, False, A["w_ffn2"], FFN2_HIDDEN, True)

        values_tensor("v5")
        with attention_inputs() as part:
            b = A["L3_attn_b_attn"]
            W, loads, splits = projection(part, "p5", [A["L3_attn_w_attn"]], (b[0:D], b[D:2 * D], b[2 * D:3 * D]))
            normalise(nc, G, "n5", "layer", loads, splits, stats_there=True)
            project(nc, G, "p5", [(W, False, G["v0"], scr["q0"], scr["k0"])])
        attend(nc, G, "a5", "heads", G["v0"], scr["q0"], scr["k0"], A["L3_attn_w_proj"], A["L3_attn_b_proj"])

        values_tensor(None)
        feed_forward(6, A["L3_ffn_Wg"], A["L3_ffn_routing_bias"], 8, 4, 1, True, A["w_ffn3"], FFN3_HIDDEN, False)
        store(nc, G, out)


def store(nc, G, out):
    with Phase(nc, "store") as ph:
        stored = ph.sem("stored")
        with nc.Block() as block:
            @block.sync
            def _(sp):
                sp.dma_start(out.rearrange("b (t y) x c -> (y x) (b t) c", t=2), G["X"][:]).then_inc(stored, 16)
                sp.wait_ge(stored, 16)


def affine_norm(nc, G, name, gamma, beta, eps=1e-5):
    X, U = G["X"], G["U"]
    with Phase(nc, name) as ph:
        GB = ph.sbuf("gamma_beta", [P, 2, D])
        ST = G["stats"]
        MV = ph.sbuf("mean_var", [P, TILES, 2])
        VE, SD, RS, TM = (ph.sbuf(n, [P, TILES]) for n in ("var_eps", "std", "rstd", "tmp"))
        loaded, chain, var_ready, std_ready, scaled, with_beta = (
            ph.sem(s) for s in ("loaded", "chain", "var_ready", "std_ready", "scaled", "with_beta"))
        with nc.Block() as block:
            @block.sync
            def _(sp):
                for i, v in enumerate((gamma, beta)):
                    sp.dma_start(GB[:, i, :], v.partition_broadcast(P)).then_inc(loaded, 16)

            @block.scalar
            def _(act):
                act.wait_ge(var_ready, 1)
                act.activation(SD[:], VE[:], ACT.Sqrt).then_inc(std_ready, 1)

            @block.vector
            def _(dve):
                link = Chain(dve, chain)
                for t in range(TILES):
                    dve.bn_stats(ST[:, t, :], U[:, t, :]).then_inc(chain, 1)
                for t in range(TILES):
                    dve.wait_ge(chain, t + 1)
                    dve.bn_aggr(MV[:, t, :], ST[:, t, :]).then_inc(chain, 1)
                link.n = 2 * TILES
                dve.wait_ge(chain, link.n)
                dve.tensor_scalar_add(VE[:], MV[:, :, 1], eps).then_inc(var_ready, 1)
                dve.wait_ge(loaded, 32)
                for t in range(TILES):
                    dve.scalar_tensor_tensor(U[:, t, :], U[:, t, :], MV[:, t, 0:1], GB[:, 0, :], ALU.subtract,
                                             ALU.mult).then_inc(scaled, 1)
                dve.wait_ge(std_ready, 1)
                inverse_root(dve, link, SD[:], VE[:], RS[:], TM[:])
                for t in range(TILES):
                    dve.wait_ge(scaled, t + 1)
                    dve.wait_ge(with_beta, t + 1)
                    dve.scalar_tensor_tensor(X[:, t, :], U[:, t, :], RS[:, t:t + 1], X[:, t, :], ALU.mult,
                                             ALU.add).then_inc(chain, 1)

            @block.gpsimd
            def _(pool):
                pool.wait_ge(loaded, 32)
                for t in range(TILES):
                    pool.tensor_tensor(X[:, t, :], X[:, t, :], GB[:, 1, :], ALU.add).then_inc(with_beta, 1)


def layouts(inputs):
    a = {k: np.asarray(v) for k, v in inputs.items()}
    dist = np.arange(SIDE)[:, None] - np.arange(SIDE)[None, :] + SIDE - 1
    out = {k: v for k, v in a.items() if not k.startswith(("L1_conv_rel", "L2_ffn", "L3_ffn"))}
    out["rel_h"] = a["L1_conv_rel_pos_h"].T[:, dist]
    out["rel_w"] = a["L1_conv_rel_pos_w"].T[:, dist]
    i = np.arange(P)
    out["c_ident"] = np.eye(P, dtype=np.float32)
    out["c_group"] = (i[:, None] // GROUP == i[None, :] // GROUP).astype(np.float32) / GROUP
    same = (i[:, None] // SIDE == i[None, :] // SIDE).astype(np.float32) / SIDE
    out["c_mask"] = np.stack([same, same], axis=1)
    key = np.arange(SEQ)
    where = [(np.arange(SIDE)[:, None] == k[None, :]).astype(np.float32) for k in (key // SIDE, key % SIDE)]
    out["c_where"] = np.concatenate([where[0]] * 3 + [where[1]] * 3)
    e = np.arange(8)
    out["c_before"] = np.broadcast_to((e[None, :] < e[:, None]).astype(np.float32), (P, 8, 8))
    for n in ("L2_ffn_Wg", "L3_ffn_Wg"):
        out[n] = a[n].T.reshape(KD, P, -1).transpose(1, 0, 2)
    out["L3_ffn_routing_bias"] = a["L3_ffn_routing_bias"]
    out["w_ffn2"] = expert_layout(a["L2_ffn_gate_bank"], a["L2_ffn_up_bank"], a["L2_ffn_down_bank"])
    w1, w2, w3 = (np.concatenate([a[f"L3_ffn_Ws{i}"][None], a[f"L3_ffn_W{i}"]]) for i in (1, 2, 3))
    out["w_ffn3"] = expert_layout(w1.transpose(0, 2, 1), w2.transpose(0, 2, 1), w3.transpose(0, 2, 1))
    return {k: np.ascontiguousarray(v) for k, v in out.items()}


def expert_layout(w1, w2, w3):
    n, _, hidden = w1.shape
    n_h, rest = divmod(hidden, P)
    full = [w1[:, :, :n_h * P], w2[:, :, :n_h * P], w3[:, :n_h * P]]
    if rest:
        more = [np.zeros_like(w[:1]) for w in full]
        for e in range(n):
            m, j = divmod(e, P // rest)
            units = slice(m * P + j * rest, m * P + (j + 1) * rest)
            more[0][0, :, units], more[1][0, :, units] = w1[e, :, n_h * P:], w2[e, :, n_h * P:]
            more[2][0, units] = w3[e, n_h * P:]
        full = [np.concatenate(p) for p in zip(full, more)]
    n = full[0].shape[0]
    ups = [w.reshape(n, KD, P, n_h * P).transpose(0, 2, 1, 3).reshape(n, P, -1) for w in full[:2]]
    down = full[2].reshape(n, n_h, P, D).transpose(0, 2, 1, 3).reshape(n, P, -1)
    return np.concatenate(ups + [down], axis=2)


def kernel(**inputs):
    import concourse.bacc as bacc
    from concourse.bass_utils import run_bass_kernel_spmd
    nc = bacc.Bacc("TRN2", target_bir_lowering=False, num_devices=1)
    arrays = {f"in_{k}": v for k, v in layouts(inputs).items()}
    aps = {k[3:]: nc.dram_tensor(k, v.shape, mybir.dt.from_np(v.dtype), kind="ExternalInput").ap()
           for k, v in arrays.items()}
    out = nc.dram_tensor("out", [IMAGES, SIDE, SIDE, D], F32, kind="ExternalOutput").ap()
    program(nc, aps, out)
    return run_bass_kernel_spmd(nc, [arrays], core_ids=[0]).results[0]["out"]
```
